# Optimizing a Trainium2 kernel written in Bass

```python
import numpy as np
import jax
import jax.numpy as jnp

def _softmax(x, axis=-1):
    return jax.nn.softmax(x, axis=axis)

def _gelu(x):
    return jax.nn.gelu(x, approximate=True)

def _silu(x):
    return jax.nn.silu(x)

def _sigmoid(x):
    return jax.nn.sigmoid(x)

def _layernorm(x, axis=-1, eps=1e-05):
    m = jnp.mean(x, axis=axis, keepdims=True)
    v = jnp.var(x, axis=axis, keepdims=True)
    return (x - m) / jnp.sqrt(v + eps)

def _scatter_add(tgt, idx, src, axis=0):
    return tgt.at[idx].add(src)

def _segment_sum(src, seg, n):
    return jax.ops.segment_sum(src, seg, n)
kernel_name = 'mk_cond_resid_d2_seqx_r2_379773'

def setup_inputs(seed: int=0):
    np.random.seed(seed)
    _w = jnp.asarray

    def _rec_inputs():
        import jax
        import jax.numpy as jnp
        _rk = jax.random.key(seed)
        x = -0.0002928 + 1 * jax.random.normal(jax.random.fold_in(_rk, 1), (4, 1024, 512), jnp.float32)
        _lenS = 1024 - jax.random.randint(jax.random.fold_in(_rk, 7), (4,), 0, max(1, 1024 // 4) + 1, jnp.int32)
        _lenS2 = 1024 - jax.random.randint(jax.random.fold_in(_rk, 8), (4,), 0, max(1, 1024 // 4) + 1, jnp.int32)
        cond_64 = -0.0184271 + 1.00439 * jax.random.normal(jax.random.fold_in(_rk, 12), (4, 64), jnp.float32)
        _validS = jnp.arange(1024)[None, :] < _lenS[:, None]
        _validS2 = jnp.arange(1024)[None, :] < _lenS2[:, None]
        _causal = jnp.tril(jnp.ones((1024, 1024), dtype=bool))
        mask_BxS_bf1 = jnp.ones((4, 1024), dtype=bool)
        return (x, cond_64, mask_BxS_bf1)
    x, cond_64, mask_BxS_bf1 = _rec_inputs()

    def _L0_cond_setup():
        import jax, jax.numpy as jnp
        import numpy as np
        DIM = 512
        HEADS = 16
        DIM_HEAD = 64
        SCALE = 8.0

        def ln(x, g, eps=1e-05):
            mean = x.mean(axis=-1, keepdims=True)
            var = ((x - mean) ** 2).mean(axis=-1, keepdims=True)
            return (x - mean) * jax.lax.rsqrt(var + eps) * g

        def l2norm(t):
            n = jnp.maximum(jnp.linalg.norm(t, axis=-1, keepdims=True), 1e-12)
            return t / n

        def rel_pos_bias(n, w0, b0, g0, w1, b1, g1, w2, b2, dtype):
            pos = jnp.arange(-n + 1, n, dtype=dtype)[:, None]
            h = jax.nn.silu(ln(pos @ w0 + b0, g0))
            h = jax.nn.silu(ln(h @ w1 + b1, g1))
            h = h @ w2 + b2
            i = jnp.arange(n)
            idx = i[:, None] - i[None, :] + n - 1
            bias = h[idx]
            return jnp.transpose(bias, (2, 0, 1))
        key = jax.random.key(seed)
        ks = jax.random.split(key, 16)
        b, n = (2, 1024)
        inner = HEADS * DIM_HEAD
        s = 0.02
        return {'x': jax.random.normal(ks[0], (b, n, DIM), jnp.float32), 'mask': jnp.ones((b, n), dtype=bool), 'g_norm': jnp.ones((DIM,), jnp.float32), 'Wq': jax.random.normal(ks[1], (DIM, inner), jnp.float32) * s, 'Wkv': jax.random.normal(ks[2], (DIM, 2 * DIM_HEAD), jnp.float32) * s, 'q_scale': jnp.ones((DIM_HEAD,), jnp.float32), 'k_scale': jnp.ones((DIM_HEAD,), jnp.float32), 'null_kv': jax.random.normal(ks[3], (2, DIM_HEAD), jnp.float32), 'null_attn_bias': jax.random.normal(ks[4], (HEADS,), jnp.float32), 'w0': jax.random.normal(ks[5], (1, DIM), jnp.float32) * s, 'b0': jnp.zeros((DIM,), jnp.float32), 'g0': jnp.ones((DIM,), jnp.float32), 'w1': jax.random.normal(ks[6], (DIM, DIM), jnp.float32) * s, 'b1': jnp.zeros((DIM,), jnp.float32), 'g1': jnp.ones((DIM,), jnp.float32), 'w2': jax.random.normal(ks[7], (DIM, HEADS), jnp.float32) * s, 'b2': jnp.zeros((HEADS,), jnp.float32), 'Wout': jax.random.normal(ks[8], (inner, DIM), jnp.float32) * s, 'g_out': jnp.ones((DIM,), jnp.float32)}
    _L0_cond_all = _L0_cond_setup()
    _L0_cond_in = {k: v for k, v in _L0_cond_all.items() if k in ('g_norm', 'Wq', 'Wkv', 'q_scale', 'k_scale', 'null_attn_bias', 'w0', 'b0', 'g0', 'w1', 'b1', 'g1', 'w2', 'b2', 'Wout', 'g_out')}
    del _L0_cond_all

    def _L1_cond_setup():
        import jax, jax.numpy as jnp
        import numpy as np
        B, S, H = (4, 1024, 512)
        E = 8
        M = 256
        K = 2
        N_SHARED = 2
        SM = M * N_SHARED
        G = 64
        GE_TEMP = 1.0
        ALPHA = 0.001
        SEQ_AUX = True
        NORM_TOPK = True
        COS_TEMP = 0.78
        CONS_ALPHA = 0.01
        LEAKY_SLOPE = 0.01
        EPS_COS = 1e-08

        def _leaky(x):
            return jnp.where(x >= 0, x, LEAKY_SLOPE * x)

        def _moe_forward(hidden_states, g, wt, wg, w_gate, w_up, w_down, sw_gate, sw_up, sw_down):
            b, s, h = hidden_states.shape
            x = hidden_states.reshape(-1, h)
            T = x.shape[0]
            logits_h = x @ wt.T
            logits_g = g @ wg.T
            logits_g = jnp.repeat(logits_g, s, axis=0)
            logits = (logits_h + logits_g / GE_TEMP) / (1.0 + 1.0 / GE_TEMP)
            scores = jax.nn.softmax(logits, axis=-1)
            topk_w, topk_idx = jax.lax.top_k(scores, K)
            if K > 1 and NORM_TOPK:
                topk_w = topk_w / (topk_w.sum(-1, keepdims=True) + 1e-20)
            onehot = jax.nn.one_hot(topk_idx.reshape(b, s * K), E, dtype=jnp.float32)
            ce = onehot.sum(1) / (s * K / E)
            aux_loss = (ce * scores.reshape(b, s, E).mean(1)).sum(1).mean() * ALPHA
            gp = _leaky(jnp.einsum('th,ehm->etm', x, w_gate))
            up = jnp.einsum('th,ehm->etm', x, w_up)
            y_all = jnp.einsum('etm,emh->eth', gp * up, w_down)
            y_sel = y_all[topk_idx, jnp.arange(T)[:, None], :]
            y = (y_sel * topk_w[..., None]).sum(1).reshape(b, s, h)
            p = _leaky(hidden_states @ sw_gate) * (hidden_states @ sw_up) @ sw_down
            y = y + p
            num = jnp.sum(y * p, -1)
            den = jnp.maximum(jnp.linalg.norm(y, axis=-1), EPS_COS) * jnp.maximum(jnp.linalg.norm(p, axis=-1), EPS_COS)
            closs = CONS_ALPHA * jnp.mean(num / den / (1.0 + COS_TEMP))
            return (y, aux_loss + closs)
        key = jax.random.key(seed)
        ks = jax.random.split(key, 12)
        sh = 1.0 / np.sqrt(H)
        sm = 1.0 / np.sqrt(M)
        ssm = 1.0 / np.sqrt(SM)
        sg = 1.0 / np.sqrt(G)
        return {'hidden_states': jax.random.normal(ks[0], (B, S, H), jnp.float32), 'g': jax.random.normal(ks[1], (B, G), jnp.float32), 'wt': jax.random.uniform(ks[2], (E, H), jnp.float32, -sh, sh), 'wg': jax.random.uniform(ks[3], (E, G), jnp.float32, -sg, sg), 'w_gate': jax.random.uniform(ks[4], (E, H, M), jnp.float32, -sh, sh), 'w_up': jax.random.uniform(ks[5], (E, H, M), jnp.float32, -sh, sh), 'w_down': jax.random.uniform(ks[6], (E, M, H), jnp.float32, -sm, sm), 'sw_gate': jax.random.uniform(ks[7], (H, SM), jnp.float32, -sh, sh), 'sw_up': jax.random.uniform(ks[8], (H, SM), jnp.float32, -sh, sh), 'sw_down': jax.random.uniform(ks[9], (SM, H), jnp.float32, -ssm, ssm)}
    _L1_cond_all = _L1_cond_setup()
    _L1_cond_in = {k: v for k, v in _L1_cond_all.items() if k in ('wt', 'wg', 'w_gate', 'w_up', 'w_down', 'sw_gate', 'sw_up', 'sw_down')}
    del _L1_cond_all
    return {'x': x, 'cond_64': cond_64, 'mask_BxS_bf1': mask_BxS_bf1, 'L0_cond_g_norm': _L0_cond_in['g_norm'], 'L0_cond_Wq': _L0_cond_in['Wq'], 'L0_cond_Wkv': _L0_cond_in['Wkv'], 'L0_cond_q_scale': _L0_cond_in['q_scale'], 'L0_cond_k_scale': _L0_cond_in['k_scale'], 'L0_cond_null_attn_bias': _L0_cond_in['null_attn_bias'], 'L0_cond_w0': _L0_cond_in['w0'], 'L0_cond_b0': _L0_cond_in['b0'], 'L0_cond_g0': _L0_cond_in['g0'], 'L0_cond_w1': _L0_cond_in['w1'], 'L0_cond_b1': _L0_cond_in['b1'], 'L0_cond_g1': _L0_cond_in['g1'], 'L0_cond_w2': _L0_cond_in['w2'], 'L0_cond_b2': _L0_cond_in['b2'], 'L0_cond_Wout': _L0_cond_in['Wout'], 'L0_cond_g_out': _L0_cond_in['g_out'], 'L1_cond_wt': _L1_cond_in['wt'], 'L1_cond_wg': _L1_cond_in['wg'], 'L1_cond_w_gate': _L1_cond_in['w_gate'], 'L1_cond_w_up': _L1_cond_in['w_up'], 'L1_cond_w_down': _L1_cond_in['w_down'], 'L1_cond_sw_gate': _L1_cond_in['sw_gate'], 'L1_cond_sw_up': _L1_cond_in['sw_up'], 'L1_cond_sw_down': _L1_cond_in['sw_down']}

def reference(x, cond_64, mask_BxS_bf1, L0_cond_g_norm, L0_cond_Wq, L0_cond_Wkv, L0_cond_q_scale, L0_cond_k_scale, L0_cond_null_attn_bias, L0_cond_w0, L0_cond_b0, L0_cond_g0, L0_cond_w1, L0_cond_b1, L0_cond_g1, L0_cond_w2, L0_cond_b2, L0_cond_Wout, L0_cond_g_out, L1_cond_wt, L1_cond_wg, L1_cond_w_gate, L1_cond_w_up, L1_cond_w_down, L1_cond_sw_gate, L1_cond_sw_up, L1_cond_sw_down):
    import jax
    import jax.numpy as jnp

    def _L0_cond_ref(x, mask, g_norm, Wq, Wkv, q_scale, k_scale, null_kv, null_attn_bias, w0, b0, g0, w1, b1, g1, w2, b2, Wout, g_out):
        import jax, jax.numpy as jnp
        import numpy as np
        DIM = 512
        HEADS = 16
        DIM_HEAD = 64
        SCALE = 8.0

        def ln(x, g, eps=1e-05):
            mean = x.mean(axis=-1, keepdims=True)
            var = ((x - mean) ** 2).mean(axis=-1, keepdims=True)
            return (x - mean) * jax.lax.rsqrt(var + eps) * g

        def l2norm(t):
            n = jnp.maximum(jnp.linalg.norm(t, axis=-1, keepdims=True), 1e-12)
            return t / n

        def rel_pos_bias(n, w0, b0, g0, w1, b1, g1, w2, b2, dtype):
            pos = jnp.arange(-n + 1, n, dtype=dtype)[:, None]
            h = jax.nn.silu(ln(pos @ w0 + b0, g0))
            h = jax.nn.silu(ln(h @ w1 + b1, g1))
            h = h @ w2 + b2
            i = jnp.arange(n)
            idx = i[:, None] - i[None, :] + n - 1
            bias = h[idx]
            return jnp.transpose(bias, (2, 0, 1))
        b, n, _ = x.shape
        xn = ln(x, g_norm)
        q = (xn @ Wq).reshape(b, n, HEADS, DIM_HEAD).transpose(0, 2, 1, 3)
        kv = xn @ Wkv
        k, v = (kv[..., :DIM_HEAD], kv[..., DIM_HEAD:])
        nk = jnp.broadcast_to(null_kv[0], (b, 1, DIM_HEAD))
        nv = jnp.broadcast_to(null_kv[1], (b, 1, DIM_HEAD))
        k = jnp.concatenate([nk, k], axis=1)
        v = jnp.concatenate([nv, v], axis=1)
        q = l2norm(q) * q_scale
        k = l2norm(k) * k_scale
        sim = jnp.einsum('bhid,bjd->bhij', q, k) * SCALE
        bias = rel_pos_bias(n, w0, b0, g0, w1, b1, g1, w2, b2, q.dtype)
        null_bias = jnp.broadcast_to(null_attn_bias[:, None, None], (HEADS, n, 1))
        attn_bias = jnp.concatenate([null_bias, bias], axis=-1)
        sim = sim + attn_bias
        neg = -jnp.finfo(sim.dtype).max
        causal = jnp.triu(jnp.ones((n, n + 1), dtype=bool), k=2)
        sim = jnp.where(causal, neg, sim)
        m = jnp.pad(mask, ((0, 0), (1, 0)), constant_values=True)[:, None, None, :]
        sim = jnp.where(m, sim, neg)
        attn = jax.nn.softmax(sim, axis=-1)
        out = jnp.einsum('bhij,bjd->bhid', attn, v)
        out = out.transpose(0, 2, 1, 3).reshape(b, n, HEADS * DIM_HEAD)
        return ln(out @ Wout, g_out)

    def _L1_cond_ref(hidden_states, g, wt, wg, w_gate, w_up, w_down, sw_gate, sw_up, sw_down):
        import jax, jax.numpy as jnp
        import numpy as np
        B, S, H = (4, 1024, 512)
        E = 8
        M = 256
        K = 2
        N_SHARED = 2
        SM = M * N_SHARED
        G = 64
        GE_TEMP = 1.0
        ALPHA = 0.001
        SEQ_AUX = True
        NORM_TOPK = True
        COS_TEMP = 0.78
        CONS_ALPHA = 0.01
        LEAKY_SLOPE = 0.01
        EPS_COS = 1e-08

        def _leaky(x):
            return jnp.where(x >= 0, x, LEAKY_SLOPE * x)

        def _moe_forward(hidden_states, g, wt, wg, w_gate, w_up, w_down, sw_gate, sw_up, sw_down):
            b, s, h = hidden_states.shape
            x = hidden_states.reshape(-1, h)
            T = x.shape[0]
            logits_h = x @ wt.T
            logits_g = g @ wg.T
            logits_g = jnp.repeat(logits_g, s, axis=0)
            logits = (logits_h + logits_g / GE_TEMP) / (1.0 + 1.0 / GE_TEMP)
            scores = jax.nn.softmax(logits, axis=-1)
            topk_w, topk_idx = jax.lax.top_k(scores, K)
            if K > 1 and NORM_TOPK:
                topk_w = topk_w / (topk_w.sum(-1, keepdims=True) + 1e-20)
            onehot = jax.nn.one_hot(topk_idx.reshape(b, s * K), E, dtype=jnp.float32)
            ce = onehot.sum(1) / (s * K / E)
            aux_loss = (ce * scores.reshape(b, s, E).mean(1)).sum(1).mean() * ALPHA
            gp = _leaky(jnp.einsum('th,ehm->etm', x, w_gate))
            up = jnp.einsum('th,ehm->etm', x, w_up)
            y_all = jnp.einsum('etm,emh->eth', gp * up, w_down)
            y_sel = y_all[topk_idx, jnp.arange(T)[:, None], :]
            y = (y_sel * topk_w[..., None]).sum(1).reshape(b, s, h)
            p = _leaky(hidden_states @ sw_gate) * (hidden_states @ sw_up) @ sw_down
            y = y + p
            num = jnp.sum(y * p, -1)
            den = jnp.maximum(jnp.linalg.norm(y, axis=-1), EPS_COS) * jnp.maximum(jnp.linalg.norm(p, axis=-1), EPS_COS)
            closs = CONS_ALPHA * jnp.mean(num / den / (1.0 + COS_TEMP))
            return (y, aux_loss + closs)
        y, _ = _moe_forward(hidden_states, g, wt, wg, w_gate, w_up, w_down, sw_gate, sw_up, sw_down)
        return y
    x = x + _L0_cond_ref(x, mask_BxS_bf1, L0_cond_g_norm, L0_cond_Wq, L0_cond_Wkv, L0_cond_q_scale, L0_cond_k_scale, cond_64, L0_cond_null_attn_bias, L0_cond_w0, L0_cond_b0, L0_cond_g0, L0_cond_w1, L0_cond_b1, L0_cond_g1, L0_cond_w2, L0_cond_b2, L0_cond_Wout, L0_cond_g_out)
    x = x + _L1_cond_ref(x, cond_64, L1_cond_wt, L1_cond_wg, L1_cond_w_gate, L1_cond_w_up, L1_cond_w_down, L1_cond_sw_gate, L1_cond_sw_up, L1_cond_sw_down)
    return x

_drawn_inputs = setup_inputs


def setup_inputs(seed=0):
    import zlib

    import numpy as np

    out = dict(_drawn_inputs(seed))
    spreads = {'L0_cond_g_norm': (1.0, 0.2),
     'L0_cond_q_scale': (1.0, 0.2),
     'L0_cond_k_scale': (1.0, 0.2),
     'L0_cond_b0': (0.0, 0.282),
     'L0_cond_g0': (1.0, 0.6),
     'L0_cond_b1': (0.0, 0.388),
     'L0_cond_g1': (1.0, 0.6),
     'L0_cond_b2': (0.0, 0.678),
     'L0_cond_g_out': (1.0, 0.2)}
    factors = {}
    for name, (base, spread) in spreads.items():
        noise = np.random.default_rng([zlib.crc32(name.encode()), seed]).standard_normal(out[name].shape)
        drawn = base * np.exp(spread * noise) if base else spread * noise
        out[name] = jnp.asarray(drawn.astype(out[name].dtype))
    for name, factor in factors.items():
        out[name] = (out[name] * factor).astype(out[name].dtype)
    return out
```

```python
from contextlib import ExitStack

import concourse.bass as bass
from concourse import mybir

P = 128
F32 = mybir.dt.float32
F32R = mybir.dt.float32r
I32 = mybir.dt.int32
U32 = mybir.dt.uint32
ALU = mybir.AluOpType
ACT = mybir.ActivationFunctionType
AX = mybir.AxisListType

B, S, D = 4, 1024, 512
H, DH = 16, 64
KD = D // P
NT = S // P
G = 4
NG = H // G
VW = DH + 1
WQKV = H * DH + 2 * DH + H
KVC = H * DH
NE, MD, SMD = 8, 256, 512
T = B * S
NTT = T // P
SLOTS = 2 * NTT + NE
LN_EPS = 1e-5
NORM_EPS = 1e-12
HEAD = 40.0
LIFT = 24

FILLS = [[(0, 0)], [(1, 0)], [(2, 0), (6, 768)], [(3, 0), (5, 640)], [(4, 0), (7, 512)]]
NF = len(FILLS)


def width(j):
    return S - P * j


def fill_width(k):
    j, c = FILLS[k][-1]
    return c + width(j)


class Chain:

    def __init__(self, eng, sem):
        self.eng, self.sem, self.base, self.n = eng, sem, 0, 0

    def link(self, ins):
        ins.then_inc(self.sem, 1)
        self.n += 1
        self.eng.wait_ge(self.sem, self.base + self.n)


def newton(dve, ch, y, y0, v, t, f):
    ch.link(dve.tensor_tensor(t, y0, y0, ALU.mult))
    ch.link(dve.tensor_tensor(t, t, v, ALU.mult))
    ch.link(dve.tensor_scalar(t, t, -0.5 * f * f * f, 1.5 * f, ALU.mult, ALU.add))
    return dve.tensor_tensor(y, y0, t, ALU.mult)


def setup(nc, a, sb, dr, sem):
    HW = NT * D
    with ExitStack() as ctx:
        def tmp(name, shape, dt=F32):
            return ctx.enter_context(nc.sbuf_tensor(name, shape, dt))

        def psum(name, shape):
            return ctx.enter_context(nc.psum_tensor(name, shape, F32))

        rows = {n: tmp("row_" + n, [P, D]) for n in ("w0", "b0", "g0", "b1", "g1")}
        gn = tmp("gn", [P, KD])
        w1 = tmp("w1", [P, KD, D])
        w2 = tmp("w2", [P, KD, H])
        h = tmp("h", [P, NT, D])
        hT = tmp("hT", [P, KD, S])
        pos = tmp("pos", [P, NT])
        st = tmp("st", [P, NT, 6])
        mv = tmp("mv", [P, NT, 2])
        ve = tmp("ve", [P, NT])
        y0 = tmp("y0", [P, NT])
        nt = tmp("nt", [P, NT])
        rs = tmp("rs", [P, NT])
        cond = tmp("cond", [P, B * DH])
        qs = tmp("qs", [P, DH])
        ks = tmp("ks", [P, DH])
        c2 = tmp("c2", [P, DH])
        ss = tmp("ss", [P, 4])
        kn = tmp("kn", [P, DH])
        wg = tmp("wg", [P, NE, DH])
        wgp = tmp("wgp", [P, NE, DH])
        mask8 = tmp("mask8", [P, NTT], mybir.dt.uint8)
        brow = tmp("brow", [H, P + S])
        braw = tmp("braw", [H, S])
        hcol = tmp("hcol", [H, 8])
        pA = [psum(f"pA{i}", [P, 512]) for i in range(4)]
        pB = psum("pB", [H, 2, 512])
        zero = tmp("zero", [P, D])
        wprod = hT[:, 0, :].rearrange("p (h d) -> p h d", h=H)

        s_rows, s_w, s_cond, s_mask = sem("s_rows"), sem("s_w"), sem("s_cond"), sem("s_mask")
        s_id, s_pos, s_dve, s_var, s_y0 = sem("s_id"), sem("s_pos"), sem("s_dvec"), sem("s_svar"), sem("s_sy0")
        s_z, s_silu, s_tr, s_ev, s_mm, s_mv = (sem("s_" + n) for n in ("z", "silu", "tr", "ev", "mm", "mmev"))
        s_b, s_bex, s_bx, s_eb, s_kn = sem("s_b"), sem("s_bex"), sem("s_bx"), sem("s_eb"), sem("s_kn")
        s_pw, s_dve2, s_hb = sem("s_pw"), sem("s_dve2"), sem("s_hb")
        s_zero, s_fill = sem("s_zero"), sem("s_fill")
        block = ctx.enter_context(nc.Block())

        def bcast(ap, n):
            return bass.AP(ap.tensor, ap.offset, [[0, P], [1, n]])

        @block.sync
        def _(sp):
            sp.dma_start(rows["w0"][:], bcast(a["w0"], D)).then_inc(s_rows, 16)
            for n in ("b0", "g0", "b1", "g1"):
                sp.dma_start(rows[n][:], bcast(a[n], D)).then_inc(s_rows, 16)
            sp.dma_start(cond[:], bcast(a["cond"], B * DH)).then_inc(s_cond, 16)
            sp.dma_start(qs[:], bcast(a["q_scale"], DH)).then_inc(s_cond, 16)
            sp.dma_start(ks[:], bcast(a["k_scale"], DH)).then_inc(s_cond, 16)
            sp.dma_start(wg[:], bass.AP(a["wg"].tensor, 0, [[0, P], [DH, NE], [1, DH]])).then_inc(s_cond, 16)
            sp.dma_start(gn[:], a["g_norm"].rearrange("(k p) -> p k", p=P),
                         allow_slow_non_contiguous=True).then_inc(s_w, 16)
            sp.dma_start(sb["W"][:, :, 0:KVC], a["Wq"].rearrange("(k p) n -> p k n", p=P)).then_inc(s_w, 16)
            sp.dma_start(sb["W"][:, :, KVC:KVC + 2 * DH], a["Wkv"].rearrange("(k p) n -> p k n", p=P)).then_inc(s_w, 16)
            sp.dma_start(mask8[:], a["mask"].rearrange("b (t p) -> p (b t)", p=P),
                         allow_slow_non_contiguous=True).then_inc(s_mask, 16)
            sp.wait_ge(s_bx, 2)
            n = P + S
            for q in range(4):
                hq = H // 4
                src = brow[q * hq:(q + 1) * hq, :].unsqueeze(1).to_broadcast([hq, P, n])
                sp.dma_start(dr["bias"][q * hq:(q + 1) * hq], src).then_inc(s_bex, 16)
            sp.dma_start(dr["enull"].rearrange("(h a) -> h a", a=1), hcol[:, 5:6]).then_inc(s_bex, 16)
            sp.wait_ge(s_bex, 80)
            for q in range(4):
                hq = H // 4
                src = bass.AP(dr["bias"].tensor, q * hq * P * n + P - 1, [[n - 1, P], [P * n, hq], [1, S]])
                sp.dma_start(sb["EB"][:, q * hq:(q + 1) * hq, :], src).then_inc(s_eb, 16)
            sp.dma_start(sb["enull"][:], bcast(dr["enull"], H)).then_inc(s_eb, 16)
            sp.wait_ge(s_eb, 80)

        @block.gpsimd
        def _(pool):
            pool.memset(sb["ident"][:], 0.0).then_inc(s_id, 1)
            pool.wait_ge(s_id, 1)
            pool.affine_select(out=sb["ident"][:], in_=sb["ident"][:], compare_op=ALU.not_equal, fill=1.0, base=0,
                               pattern=[[-1, P]], channel_multiplier=1).then_inc(s_id, 1)
            pool.memset(zero[:], 0.0).then_inc(s_zero, 1)
            pool.iota(pos[:], [[P, NT]], base=0, channel_multiplier=1,
                      allow_small_or_imprecise_dtypes=True).then_inc(s_pos, 1)
            for i, name in enumerate(CREDITS):
                pool.memset(sb["credit"][:, i:i + 1], 0.0).then_inc(sb[name], CREDITS[name])
            pool.wait_ge(s_kn, 2)
            for k in range(KD):
                if k:
                    pool.wait_ge(s_pw, 2 * k)
                pool.tensor_tensor(wprod, sb["W"][:, k, 0:KVC].rearrange("p (h d) -> p h d", h=H),
                                   kn[:].unsqueeze(1).to_broadcast([P, H, DH]), ALU.mult).then_inc(s_pw, 1)

        @block.scalar
        def _(act):
            act.dma_start(w1[:], a["w1"].rearrange("(k p) n -> p k n", p=P)).then_inc(s_mv, 16)
            act.dma_start(w2[:], a["w2"].rearrange("(k p) n -> p k n", p=P)).then_inc(s_mv, 16)
            act.dma_start(hcol[:, 0:1], a["b2"].rearrange("(h a) -> h a", a=1)).then_inc(s_mv, 16)
            act.dma_start(hcol[:, 1:2], a["null_bias"].rearrange("(h a) -> h a", a=1)).then_inc(s_mv, 16)
            act.dma_start(sb["Wo"][:], a["Wout"].rearrange("(k p) n -> p k n", p=P)).then_inc(s_w, 16)
            act.dma_start(sb["gout"][:], bcast(a["g_out"], D)).then_inc(s_w, 16)
            for k in range(KD):
                act.dma_start(sb["wtT"][:, k, :], bass.AP(a["wt"].tensor, k * P, [[1, P], [D, NE]]),
                              allow_slow_non_contiguous=True).then_inc(s_w, 16)
            act.wait_ge(s_zero, 1)
            act.dma_start(dr["xs"].rearrange("(n p) d -> p n d", p=P),
                          zero[:].unsqueeze(1).to_broadcast([P, SLOTS, D])).then_inc(s_fill, 16)
            act.wait_ge(s_kn, 1)
            act.activation(ss[:, 1:2], ss[:, 0:1], ACT.Ln, scale=float(2 ** LIFT)).then_inc(s_y0, 1)
            act.wait_ge(s_y0, 1)
            act.activation(ss[:, 2:3], ss[:, 1:2], ACT.Exp, scale=-0.5).then_inc(s_y0, 1)
            for layer in range(2):
                act.wait_ge(s_var, layer + 1)
                act.activation(nt[:], ve[:], ACT.Ln).then_inc(s_y0, 1)
                act.wait_ge(s_y0, 3 + 2 * layer)
                act.activation(y0[:], nt[:], ACT.Exp, scale=-0.5).then_inc(s_y0, 1)
                act.wait_ge(s_z, layer + 1)
                act.activation(h[:], h[:], ACT.Silu).then_inc(s_silu, 1)
                for i in range(8):
                    if i % 2:
                        act.wait_ge(s_tr, 8 * layer + i + 1)
                        if layer:
                            act.wait_ge(s_mm, NT)
                        act.activation(hT[:, i // 2, (i % 2) * 512:(i % 2 + 1) * 512], pA[i % 4][:], ACT.Copy)\
                           .then_inc(s_ev, 1)
            act.wait_ge(s_b, 1)
            act.activation(brow[:, P - 1:P - 1 + S], braw[:], ACT.Exp, bias=hcol[:, 4:5]).then_inc(s_bx, 1)
            act.activation(hcol[:, 5:6], hcol[:, 1:2], ACT.Exp, bias=hcol[:, 4:5]).then_inc(s_bx, 1)
            act.wait_ge(s_fill, 16)

        @block.tensor
        def _(pe):
            pe.wait_ge(s_id, 2)
            for layer in range(2):
                pe.wait_ge(s_silu, layer + 1)
                for i in range(8):
                    k, half = i // 2, i % 2
                    if i >= 4:
                        pe.wait_ge(s_ev if i % 2 else s_dve2, 4 * layer + (i - 4) // 2 + 1)
                    for c in range(4):
                        ins = pe.transpose(pA[i % 4][:, c * P:(c + 1) * P],
                                           h[:, half * 4 + c, k * P:(k + 1) * P], sb["ident"][:])
                    ins.then_inc(s_tr, 1)
                pe.wait_ge(s_ev, 4 * layer + 4)
                pe.wait_ge(s_dve2, 4 * layer + 4)
                if layer == 0:
                    pe.wait_ge(s_mv, 64)
                    for c in range(NT):
                        if c >= 4:
                            pe.wait_ge(s_hb, c - 3)
                        for k in range(KD):
                            ins = pe.matmul(pA[c % 4][:], hT[:, k, c * P:(c + 1) * P], w1[:, k, :],
                                            start=(k == 0), stop=(k == KD - 1))
                        ins.then_inc(s_mm, 1)
                    pe.wait_ge(s_hb, NT)
                else:
                    for half in range(2):
                        for k in range(KD):
                            ins = pe.matmul(pB[:, half, :], w2[:, k, :], hT[:, k, half * 512:(half + 1) * 512],
                                            start=(k == 0), stop=(k == KD - 1))
                        ins.then_inc(s_mm, 1)

        @block.vector
        def _(dve):
            ch = Chain(dve, s_dve)
            dve.wait_ge(s_cond, 64)
            ch.link(dve.tensor_tensor(c2[:], cond[:, 0:DH], cond[:, 0:DH], ALU.mult))
            ch.link(dve.tensor_reduce(ss[:, 0:1], c2[:], AX.X, ALU.add))
            dve.tensor_scalar(ss[:, 0:1], ss[:, 0:1], NORM_EPS ** 2, None, ALU.max).then_inc(s_kn, 1)
            ch.link(dve.scalar_tensor_tensor(out=sb["kfac"][:], in0=qs[:], scalar=float(DH) ** 0.5, in1=ks[:],
                                             op0=ALU.mult, op1=ALU.mult))
            ch.link(dve.tensor_reduce(c2[:, 0:1], sb["kfac"][:], AX.X, ALU.max, apply_absolute_value=True))
            ch.link(dve.tensor_scalar(sb["negc"][:], c2[:, 0:1], -1.0, HEAD, ALU.mult, ALU.add))
            dve.wait_ge(s_y0, 2)
            dve.wait_ge(s_kn, 1)
            ch.link(newton(dve, ch, ss[:, 3:4], ss[:, 2:3], ss[:, 0:1], ss[:, 1:2], float(2 ** (LIFT // 2))))
            ch.link(dve.scalar_tensor_tensor(out=kn[:], in0=cond[:, 0:DH], scalar=ss[:, 3:4], in1=sb["kfac"][:],
                                             op0=ALU.mult, op1=ALU.mult))
            ch.link(dve.memset(sb["vnull"][:], 1.0))
            ch.link(dve.tensor_copy(sb["vnull"][:, 0:DH], cond[:, DH:2 * DH]))
            dve.wait_ge(s_w, 16 * (5 + KD))
            for k in range(KD):
                ins = dve.tensor_scalar(sb["W"][:, k, 0:KVC + 2 * DH], sb["W"][:, k, 0:KVC + 2 * DH], gn[:, k:k + 1],
                                        None, ALU.mult)
                if k == KD - 1:
                    ins.then_inc(s_kn, 1)
                else:
                    ch.link(ins)
            for b in range(B):
                ch.link(dve.tensor_tensor(wgp[:], wg[:], cond[:, b * DH:(b + 1) * DH].unsqueeze(1)
                                          .to_broadcast([P, NE, DH]), ALU.mult))
                ch.link(dve.tensor_reduce(sb["glog"][:, b, :], wgp[:], AX.X, ALU.add))
            dve.wait_ge(s_mask, 16)
            ch.link(dve.tensor_copy(sb["maskf"][:], mask8[:]))
            dve.wait_ge(s_rows, 80)
            dve.wait_ge(s_pos, 1)
            for k in range(KD):
                dve.wait_ge(s_pw, 1 + 2 * k)
                dve.tensor_reduce(sb["W"][:, k, KVC + 2 * DH:], wprod, AX.X, ALU.add).then_inc(s_pw, 1)
            for c in range(NT):
                ins = dve.scalar_tensor_tensor(out=h[:, c, :], in0=rows["w0"][:], scalar=pos[:, c:c + 1],
                                               in1=rows["b0"][:], op0=ALU.mult, op1=ALU.add)
            ch.link(ins)
            for layer in range(2):
                if layer:
                    for c in range(NT):
                        dve.wait_ge(s_mm, c + 1)
                        ins = dve.tensor_tensor(h[:, c, :], pA[c % 4][:], rows["b1"][:], ALU.add)
                        ins.then_inc(s_hb, 1)
                    dve.wait_ge(s_hb, NT)
                for c in range(NT):
                    ins = dve.bn_stats(st[:, c, :], h[:, c, :])
                ch.link(ins)
                for c in range(NT):
                    ins = dve.bn_aggr(mv[:, c, :], st[:, c, :])
                ch.link(ins)
                dve.tensor_scalar(ve[:], mv[:, :, 1], LN_EPS, None, ALU.add).then_inc(s_var, 1)
                dve.wait_ge(s_var, layer + 1)
                dve.wait_ge(s_y0, 4 + 2 * layer)
                ch.link(newton(dve, ch, rs[:], y0[:], ve[:], nt[:], 1.0))
                for c in range(NT):
                    ins = dve.tensor_scalar(h[:, c, :], h[:, c, :], mv[:, c, 0:1], rs[:, c:c + 1],
                                            ALU.subtract, ALU.mult)
                ch.link(ins)
                gain = rows["g1" if layer else "g0"]
                dve.tensor_tensor(h[:], h[:], gain[:].unsqueeze(1).to_broadcast([P, NT, D]), ALU.mult)\
                   .then_inc(s_z, 1)
                for i in range(0, 8, 2):
                    dve.wait_ge(s_tr, 8 * layer + i + 1)
                    if layer:
                        dve.wait_ge(s_mm, NT)
                    dve.tensor_copy(hT[:, i // 2, 0:512], pA[i % 4][:]).then_inc(s_dve2, 1)
            ch.link(dve.memset(brow[:], 0.0))
            dve.wait_ge(s_mm, NT + 2)
            dve.wait_ge(s_mv, 64)
            ch.link(dve.tensor_scalar(braw[:], pB[:].rearrange("h a n -> h (a n)"), hcol[:, 0:1], None, ALU.add))
            ch.link(dve.tensor_reduce(hcol[:, 2:3], braw[:], AX.X, ALU.max))
            ch.link(dve.tensor_tensor(hcol[:, 3:4], hcol[:, 2:3], hcol[:, 1:2], ALU.max))
            dve.tensor_scalar(hcol[:, 4:5], hcol[:, 3:4], -1.0, None, ALU.mult).then_inc(s_b, 1)


CREDITS = {n: 2 for n in (
    "x_used", "xT_made", "xT_copied", "kv_used", "kT_made", "kT_copied",
    "qn_made", "qst_made", "qT_made", "qTa_copied", "qTv_copied",
    "exp_made", "p_made", "pv_made", "num_made", "ao_made",
    "aT_made", "aTa_copied", "aTv_copied", "y_made", "x1T_made", "x1T_copied", "lg_made", "lg_used")}
CREDITS.update(x1_stored0=16, x1_stored1=16)
EVENTS = ("var_ready", "y0_ready", "kv_made", "ssk_made", "ssk_clamped", "yk_ready", "kst_made",
          "q_made", "sq_made", "ssq_made", "yq_made", "qhi_made", "nz_made", "nexp_made", "pn_made",
          "s_made", "rec_made", "nul_made", "var2_ready", "y02_ready", "x_in0", "x_in1")

A_LAG = dict(stats=0, y0=0, xn=1, T=1, xTc=1, kv=2, sq=2, ck=3, yk=3, k=4, kT=4, kTc=5)
B_LAG = dict(Q=0, sq=0, red=0, y=0, qn=1, hi=1, lo=1, T=2, cp=2)
D_LAG = dict(TA=0, cp=1, Y=1, st=2, y0=2, nrm=3, T1=3, x1Tc=4, lg=4, lgc=5)
CH_A_V, CH_G_V, CH_D_V = 96, 20, 64
CH_A_A, CH_G_A, CH_D_A = 16, 4, 8


def skewed(steps, lags, count):
    order = sorted(steps, key=lambda n: -lags[n])
    for i in range(count + max(lags.values())):
        for n in order:
            if 0 <= i - lags[n] < count:
                steps[n](i - lags[n])


def attention(nc, a, sb, dr, sem, psum):
    e = {n: sem(n) for n in EVENTS}
    e.update({n: sb[n] for n in CREDITS})
    psS, psO = psum["S"], psum["O"]
    R1, R2, xt = sb["R1"], sb["R2"], sb["xt"]
    xnT, QT, KT, V, AO, LG = (sb[n] for n in ("xnT", "QT", "KT", "V", "AO", "LG"))
    ident = sb["ident"]

    def r1(n, size, base=0):
        return R1[:, base + n * size:base + (n + 1) * size]

    xn = [r1(u, D) for u in range(2)]
    kst = [r1(u, 4 * DH, 2 * D).rearrange("p (s r d) -> p s r d", s=2, r=2) for u in range(2)]
    knr = [r1(u, DH, 2 * D + 8 * DH) for u in range(2)]
    ksq = [r1(u, DH, 2 * D + 10 * DH) for u in range(2)]
    qn = [r1(u, 512).rearrange("p (h d) -> p h d", d=DH) for u in range(2)]
    sq = [r1(u, 512, 1024).rearrange("p (h d) -> p h d", d=DH) for u in range(2)]
    qst = [r1(u, 1024, 2048).rearrange("p (h s d) -> p h s d", s=2, d=DH) for u in range(2)]
    E = [r1(u, 1024) for u in range(2)]
    Pw = [r1(u, 1024, 2048) for u in range(2)]
    nul = [R2[:, u * 520:(u + 1) * 520].rearrange("p (t d) -> p t d", d=VW) for u in range(2)]
    num = [R2[:, (2 + u) * 520:(3 + u) * 520].rearrange("p (t d) -> p t d", d=VW) for u in range(2)]
    AOT = [r1(u, 1024).rearrange("p (k t) -> p k t", t=P) for u in range(2)]
    y = [r1(u, 512, 2048) for u in range(2)]
    x1T = [r1(u, 512, 3072).rearrange("p (k t) -> p k t", t=P) for u in range(2)]

    sm = sb["small"]
    c = [0]

    def small(n):
        c[0] += n
        return sm[:, c[0] - n:c[0]]

    st = [small(6) for _ in range(2)]
    mv = [small(2) for _ in range(2)]
    ve, lv, y0, rs, nt = (small(NT) for _ in range(5))
    ssk, ssc, lk, yk, rk = (small(NT) for _ in range(5))
    ssq, lq, yq, rq = (small(32) for _ in range(4))
    nq, idle = small(8), small(1)
    rec = [small(8) for _ in range(2)]
    pz, pe_, pn = (small(32).rearrange("p (t h) -> p t h", h=G) for _ in range(3))
    snull = small(NT * H).rearrange("p (t h) -> p t h", h=H)

    sv, sa = [sem("dve_" + n) for n in "agd"], [sem("act_" + n) for n in "agd"]
    block_ctx = nc.Block()
    with block_ctx as block:
        @block.sync
        def _(sp):
            with sp.Fori(0, B) as b:
                def load(t, m):
                    n = sp.snap(b * 16 + (m + 1))
                    src = a["x"][bass.ds(b, 1), t * P:(t + 1) * P, :].rearrange("a p n -> (a p) n")
                    sp.wait_ge(e["x_used"], n)
                    sp.dma_start(xt[:, t % 2, :], src).then_inc(e[f"x_in{t % 2}"], 16)

                def store(t):
                    n = sp.snap(b * 16 + (8 + t + 3))
                    dst = dr["x1"][bass.ds(b * S + t * P, P), :]
                    sp.wait_ge(e["x_used"], n)
                    sp.dma_start(dst, y[t % 2]).then_inc(e[f"x1_stored{t % 2}"], 16)

                for t in range(NT):
                    load(t, t)
                load(0, 8)
                load(1, 9)
                for t in range(NT):
                    store(t)
                    if t + 2 < NT:
                        load(t + 2, 8 + t + 2)
            for u in range(2):
                sp.wait_ge(e[f"x1_stored{u}"], 16 + 16 * B * NT // 2)

        @block.gpsimd
        def _(pool):
            with pool.Fori(0, B) as b:
                with pool.Fori(0, NG) as g:
                    m0 = pool.snap((b * NG + g) * 4)

                    def lo(pr):
                        u = pr % 2
                        pool.wait_ge(e["qhi_made"], m0 + (pr + 1))
                        pool.tensor_tensor(qst[u][:, :, 1, :], qn[u], qst[u][:, :, 0, :], ALU.subtract)\
                            .then_inc(e["qst_made"], 1)
                    for pr in range(4):
                        lo(pr)

                    def null_part(hh):
                        if hh == 0:
                            pool.wait_ge(e["pn_made"], b * NG + g + 1)
                        pool.wait_ge(e["num_made"], m0 + (hh + 1))
                        pool.tensor_tensor(nul[hh % 2], pn[:, :, hh:hh + 1].to_broadcast([P, NT, VW]),
                                           sb["vnull"][:].unsqueeze(1).to_broadcast([P, NT, VW]), ALU.mult)\
                            .then_inc(e["nul_made"], 1)

                    def scale(hh):
                        dst = AO[:, :, bass.ds((g * G + hh) * DH, DH)]
                        pool.wait_ge(e["rec_made"], m0 + (hh + 1))
                        pool.tensor_tensor(dst, num[hh % 2][:, :, 0:DH],
                                           rec[hh % 2].unsqueeze(2).to_broadcast([P, NT, DH]), ALU.mult)\
                            .then_inc(e["ao_made"], 1)
                    null_part(0)
                    null_part(1)
                    for hh in range(G):
                        scale(hh)
                        if hh + 2 < G:
                            null_part(hh + 2)

        @block.scalar
        def _(act):
            act.preload_act_table_set("natural_log_exp_and_others")
            with act.Fori(0, B) as b:
                n0 = act.snap(b * NT)
                chA = Chain(act, sa[0])
                chA.base = b * CH_A_A

                def y0s(t):
                    act.wait_ge(e["var_ready"], n0 + (t + 1))
                    chA.link(act.activation(lv[:, t:t + 1], ve[:, t:t + 1], ACT.Ln))
                    act.activation(y0[:, t:t + 1], lv[:, t:t + 1], ACT.Exp, scale=-0.5).then_inc(e["y0_ready"], 1)

                def xTc(t):
                    act.wait_ge(e["xT_made"], n0 + (t + 3))
                    act.activation(xnT[:, :, t * P:(t + 1) * P],
                                   psS[t % 2][:, 0, :].rearrange("p (k t) -> p k t", t=P), ACT.Copy)\
                        .then_inc(e["xT_copied"], 1)

                def sqk(t):
                    act.wait_ge(e["kv_made"], n0 + (t + 1))
                    act.activation(ksq[t % 2], psS[t % 2][:, 1, 0:DH], ACT.Square, accum_out=ssk[:, t:t + 1])\
                        .then_inc(e["ssk_made"], 1)

                def yks(t):
                    act.wait_ge(e["ssk_clamped"], n0 + (t + 1))
                    chA.link(act.activation(lk[:, t:t + 1], ssc[:, t:t + 1], ACT.Ln, scale=float(2 ** LIFT)))
                    act.activation(yk[:, t:t + 1], lk[:, t:t + 1], ACT.Exp, scale=-0.5).then_inc(e["yk_ready"], 1)

                def kTc(t):
                    act.wait_ge(e["kT_made"], n0 + (t + 3))
                    act.activation(KT[:, :, t * P:(t + 1) * P],
                                   psO[t % 2][:, 0, 0:256].rearrange("p (s t) -> p s t", t=P), ACT.Copy)\
                        .then_inc(e["kT_copied"], 1)

                skewed(dict(y0=y0s, xTc=xTc, sq=sqk, yk=yks, kTc=kTc), A_LAG, NT)
                assert chA.n == CH_A_A, chA.n
                with act.Fori(0, NG) as g:
                    gi = act.snap(b * NG + g)
                    m0 = act.snap(gi * 4)
                    f0 = act.snap(gi * (G * NF))
                    chG = Chain(act, sa[1])
                    chG.base = gi * (CH_G_A)

                    def sqq(pr):
                        act.wait_ge(e["q_made"], m0 + (pr + 1))
                        act.activation(sq[pr % 2].rearrange("p h d -> p (h d)"), psS[pr % 2][:, 0, :], ACT.Square)\
                            .then_inc(e["sq_made"], 1)

                    def yqs(pr):
                        w = slice(pr * 8, pr * 8 + 8)
                        act.wait_ge(e["ssq_made"], m0 + (pr + 1))
                        chG.link(act.activation(lq[:, w], ssq[:, w], ACT.Ln, scale=float(2 ** LIFT)))
                        act.activation(yq[:, w], lq[:, w], ACT.Exp, scale=-0.5).then_inc(e["yq_made"], 1)

                    def hi(pr):
                        u = pr % 2
                        act.wait_ge(e["qn_made"], m0 + (pr + 3))
                        act.wait_ge(e["qT_made"], m0 + (pr + 1))
                        act.activation(qst[u][:, :, 0, :].bitcast(F32R), qn[u], ACT.Copy).then_inc(e["qhi_made"], 1)

                    def cpq(pr):
                        t = 2 * pr
                        act.wait_ge(e["qT_made"], m0 + (pr + 3))
                        act.activation(QT[:, :, t * P:(t + 1) * P],
                                       psO[pr % 2][:, 0, :].rearrange("p (h t) -> p h t", t=P), ACT.Copy)\
                            .then_inc(e["qTa_copied"], 1)

                    skewed(dict(sq=sqq, y=yqs, hi=hi, cp=cpq), B_LAG, 4)
                    act.wait_ge(e["nz_made"], gi + 1)
                    act.activation(pe_, pz, ACT.Exp, bias=sb["negc"][:]).then_inc(e["nexp_made"], 1)
                    for f in range(G * NF):
                        n = fill_width(f % NF)
                        act.wait_ge(e["s_made"], f0 + (f + 1))
                        act.wait_ge(e["p_made"], f0 + (f + 1))
                        act.activation(E[f % 2][:, 0:n], psS[f % 2][:].rearrange("p a n -> p (a n)")[:, 0:n], ACT.Exp,
                                       bias=sb["negc"][:]).then_inc(e["exp_made"], 1)
                    assert chG.n == CH_G_A, chG.n
                chD = Chain(act, sa[2])
                chD.base = b * CH_D_A

                def cpa(t):
                    act.wait_ge(e["aT_made"], n0 + (t + 3))
                    act.wait_ge(e["y_made"], n0 + (t + 1))
                    act.activation(AOT[t % 2][:, 0:4, :].rearrange("p k t -> p (k t)"), psS[t % 2][:, 0, :], ACT.Copy)\
                        .then_inc(e["aTa_copied"], 1)

                def y0d(t):
                    act.wait_ge(e["var2_ready"], n0 + (t + 1))
                    chD.link(act.activation(lv[:, t:t + 1], ve[:, t:t + 1], ACT.Ln))
                    act.activation(y0[:, t:t + 1], lv[:, t:t + 1], ACT.Exp, scale=-0.5).then_inc(e["y02_ready"], 1)

                def x1Tc(t):
                    act.wait_ge(e["x1T_made"], n0 + (t + 3))
                    act.wait_ge(e["lg_made"], n0 + (t + 1))
                    act.activation(x1T[t % 2].rearrange("p k t -> p (k t)"), psO[t % 2][:, 1, :], ACT.Copy)\
                        .then_inc(e["x1T_copied"], 1)

                skewed(dict(cp=cpa, y0=y0d, x1Tc=x1Tc), D_LAG, NT)
                assert chD.n == CH_D_A, chD.n

        @block.tensor
        def _(pe):
            W, Wo = sb["W"], sb["Wo"]
            with pe.Fori(0, B) as b:
                n0 = pe.snap(b * NT)
                xb = pe.snap(b * 16)

                def T(t):
                    pe.wait_ge(e["x_used"], xb + (t + 3))
                    pe.wait_ge(e["xT_copied"], n0 + (t + 1))
                    for k in range(KD):
                        ins = pe.transpose(psS[t % 2][:, 0, k * P:(k + 1) * P], xn[t % 2][:, k * P:(k + 1) * P], ident[:])
                    ins.then_inc(e["xT_made"], 1)

                def kv(t):
                    pe.wait_ge(e["xT_copied"], n0 + (t + 3))
                    pe.wait_ge(e["kv_used"], n0 + (t + 1))
                    for k in range(KD):
                        ins = pe.matmul(psS[t % 2][:, 1, 0:2 * DH + H], xnT[:, k, t * P:(t + 1) * P], W[:, k, KVC:],
                                        start=(k == 0), stop=(k == KD - 1))
                    ins.then_inc(e["kv_made"], 1)

                def kT(t):
                    pe.wait_ge(e["kst_made"], n0 + (t + 1))
                    pe.wait_ge(e["kT_copied"], n0 + (t + 1))
                    for s in range(2):
                        ins = pe.transpose(psO[t % 2][:, 0, s * P:(s + 1) * P],
                                           kst[t % 2][:, s].rearrange("p r d -> p (r d)"), ident[:])
                    ins.then_inc(e["kT_made"], 1)

                skewed(dict(T=T, kv=kv, kT=kT), A_LAG, NT)
                with pe.Fori(0, NG) as g:
                    gi = pe.snap(b * NG + g)
                    m0 = pe.snap(gi * 4)
                    f0 = pe.snap(gi * (G * NF))
                    pe.wait_ge(e["num_made"], m0 + 2)
                    pe.wait_ge(e["kv_used"], n0 + (NT + 2))
                    pe.wait_ge(e["kT_copied"], n0 + (NT + 2))

                    def Q(pr):
                        pe.wait_ge(e["qn_made"], m0 + (pr + 1))
                        for i in range(2):
                            t = 2 * pr + i
                            for k in range(KD):
                                ins = pe.matmul(psS[pr % 2][:, 0, i * 256:(i + 1) * 256], xnT[:, k, t * P:(t + 1) * P],
                                                W[:, k, bass.ds(g * (G * DH), G * DH)],
                                                start=(k == 0), stop=(k == KD - 1))
                        ins.then_inc(e["q_made"], 1)

                    def TQ(pr):
                        pe.wait_ge(e["qst_made"], m0 + (pr + 3))
                        pe.wait_ge(e["qTa_copied"], m0 + (pr + 1))
                        pe.wait_ge(e["qTv_copied"], m0 + (pr + 1))
                        for i in range(2):
                            for h in range(G):
                                ins = pe.transpose(psO[pr % 2][:, i, h * P:(h + 1) * P],
                                                   qst[pr % 2][:, i * G + h].rearrange("p s d -> p (s d)"), ident[:])
                        ins.then_inc(e["qT_made"], 1)

                    skewed(dict(Q=Q, T=TQ), B_LAG, 4)
                    pe.wait_ge(e["qTa_copied"], m0 + 6)
                    pe.wait_ge(e["qTv_copied"], m0 + 6)

                    def scores(f):
                        hh, k = f // NF, f % NF
                        pe.wait_ge(e["exp_made"], f0 + (f + 1))
                        for j, c0 in FILLS[k]:
                            w, at = width(j), 0
                            while at < w:
                                m = min(w - at, 512 - (c0 + at) % 512)
                                bank, off = (c0 + at) // 512, (c0 + at) % 512
                                for s in range(2):
                                    ins = pe.matmul(psS[f % 2][:, bank, off:off + m], KT[:, s, j * P:(j + 1) * P],
                                                    QT[:, hh, j * P + at:j * P + at + m],
                                                    start=(s == 0), stop=(s == 1))
                                at += m
                        ins.then_inc(e["s_made"], 1)

                    def values(f):
                        hh, k = f // NF, f % NF
                        u = hh % 2
                        pe.wait_ge(e["p_made"], f0 + (f + 3))
                        if k == 0:
                            pe.wait_ge(e["num_made"], m0 + (hh + 1))
                        for j, c0 in FILLS[k]:
                            for i in range(j, NT):
                                ins = pe.matmul(psO[u][:, i // 4, (i % 4) * VW:(i % 4 + 1) * VW],
                                                Pw[f % 2][:, c0 + (i - j) * P:c0 + (i - j + 1) * P], V[:, j, :],
                                                start=(j == 0 and i % 4 == 0), stop=(k == NF - 1),
                                                skip_group_check=True)
                        ins.then_inc(e["pv_made"], 1)

                    for f in range(G * NF + 1):
                        if f < G * NF:
                            scores(f)
                        if f >= 1:
                            values(f - 1)
                pe.wait_ge(e["ao_made"], b * H + (H + 2))

                def TA(t):
                    pe.wait_ge(e["aTa_copied"], n0 + (t + 1))
                    pe.wait_ge(e["aTv_copied"], n0 + (t + 1))
                    for k in range(8):
                        ins = pe.transpose(psS[t % 2][:, k // 4, (k % 4) * P:(k % 4 + 1) * P],
                                           AO[:, t, k * P:(k + 1) * P], ident[:])
                    ins.then_inc(e["aT_made"], 1)

                def Y(t):
                    pe.wait_ge(e["aTa_copied"], n0 + (t + 3))
                    pe.wait_ge(e["aTv_copied"], n0 + (t + 3))
                    if t >= 2:
                        pe.wait_ge(e["x_used"], xb + (8 + t + 1))
                    for k in range(8):
                        ins = pe.matmul(psO[t % 2][:, 0, :], AOT[t % 2][:, k, :], Wo[:, k, :],
                                        start=(k == 0), stop=(k == 7))
                    ins.then_inc(e["y_made"], 1)

                def T1(t):
                    pe.wait_ge(e["x_used"], xb + (8 + t + 3))
                    pe.wait_ge(e["lg_used"], n0 + (t + 1))
                    for k in range(KD):
                        ins = pe.transpose(psO[t % 2][:, 1, k * P:(k + 1) * P], y[t % 2][:, k * P:(k + 1) * P], ident[:])
                    ins.then_inc(e["x1T_made"], 1)

                def lg(t):
                    pe.wait_ge(e["x1T_copied"], n0 + (t + 3))
                    for k in range(KD):
                        ins = pe.matmul(psO[t % 2][:, 1, 0:NE], x1T[t % 2][:, k, :], sb["wtT"][:, k, :],
                                        start=(k == 0), stop=(k == KD - 1))
                    ins.then_inc(e["lg_made"], 1)

                skewed(dict(TA=TA, Y=Y, T1=T1, lg=lg), D_LAG, NT)

        @block.vector
        def _(dve):
            with dve.Fori(0, B) as b:
                n0 = dve.snap(b * NT)
                ch = Chain(dve, sv[0])
                ch.base = b * CH_A_V

                def stats(t):
                    u = t % 2
                    dve.wait_ge(e[f"x_in{u}"], b * 128 + 16 * (t // 2 + 1))
                    ch.link(dve.bn_stats(st[u], xt[:, u, :]))
                    dve.memset(idle, 0.0)
                    ch.link(dve.bn_aggr(mv[u], st[u]))
                    dve.tensor_scalar(ve[:, t:t + 1], mv[u][:, 1:2], LN_EPS, None, ALU.add).then_inc(e["var_ready"], 1)

                def xns(t):
                    u = t % 2
                    dve.wait_ge(e["var_ready"], n0 + (t + 1))
                    dve.wait_ge(e["y0_ready"], n0 + (t + 1))
                    ch.link(newton(dve, ch, rs[:, t:t + 1], y0[:, t:t + 1], ve[:, t:t + 1], nt[:, t:t + 1], 1.0))
                    dve.wait_ge(e["xT_made"], n0 + (t + 1))
                    dve.tensor_scalar(xn[u], xt[:, u, :], mv[u][:, 0:1], rs[:, t:t + 1], ALU.subtract, ALU.mult)\
                        .then_inc(e["x_used"], 1)

                def ck(t):
                    dve.wait_ge(e["ssk_made"], n0 + (t + 1))
                    dve.tensor_scalar(ssc[:, t:t + 1], ssk[:, t:t + 1], NORM_EPS ** 2, None, ALU.max)\
                        .then_inc(e["ssk_clamped"], 1)

                def kst_(t):
                    u = t % 2
                    pkv = psS[u][:, 1, :]
                    mask = sb["maskf"][:, bass.ds(n0 + t, 1)]
                    dve.wait_ge(e["ssk_clamped"], n0 + (t + 1))
                    dve.wait_ge(e["yk_ready"], n0 + (t + 1))
                    ch.link(newton(dve, ch, rk[:, t:t + 1], yk[:, t:t + 1], ssc[:, t:t + 1], nt[:, t:t + 1],
                                   float(2 ** (LIFT // 2))))
                    ch.link(dve.scalar_tensor_tensor(out=knr[u], in0=pkv[:, 0:DH], scalar=rk[:, t:t + 1],
                                                     in1=sb["kfac"][:], op0=ALU.mult, op1=ALU.mult))
                    kb = knr[u].unsqueeze(1).to_broadcast([P, 2, DH])
                    dve.wait_ge(e["kT_made"], n0 + (t + 1))
                    ch.link(dve.tensor_copy(kst[u][:, 0].bitcast(F32R), kb))
                    dve.tensor_tensor(kst[u][:, 1], kb, kst[u][:, 0], ALU.subtract).then_inc(e["kst_made"], 1)
                    dve.tensor_scalar(V[:, t, 0:DH], pkv[:, DH:2 * DH], mask, None, ALU.mult)
                    dve.tensor_copy(V[:, t, DH:VW], mask)
                    dve.tensor_copy(snull[:, t, :], pkv[:, 2 * DH:2 * DH + H]).then_inc(e["kv_used"], 1)

                skewed(dict(stats=stats, xn=xns, ck=ck, k=kst_), A_LAG, NT)
                assert ch.n == CH_A_V, ch.n
                with dve.Fori(0, NG) as g:
                    gi = dve.snap(b * NG + g)
                    m0 = dve.snap(gi * 4)
                    f0 = dve.snap(gi * (G * NF))
                    cg = Chain(dve, sv[1])
                    cg.base = gi * CH_G_V

                    def red(pr):
                        w = slice(pr * 8, pr * 8 + 8)
                        dve.wait_ge(e["sq_made"], m0 + (pr + 1))
                        cg.link(dve.tensor_reduce(ssq[:, w], sq[pr % 2], AX.X, ALU.add))
                        dve.tensor_scalar(ssq[:, w], ssq[:, w], NORM_EPS ** 2, None, ALU.max).then_inc(e["ssq_made"], 1)

                    def qns(pr):
                        w, u = slice(pr * 8, pr * 8 + 8), pr % 2
                        dve.wait_ge(e["ssq_made"], m0 + (pr + 1))
                        dve.wait_ge(e["yq_made"], m0 + (pr + 1))
                        cg.link(newton(dve, cg, rq[:, w], yq[:, w], ssq[:, w], nq, float(2 ** (LIFT // 2))))
                        dve.wait_ge(e["qst_made"], m0 + (pr + 1))
                        dve.tensor_tensor(qn[u], psS[u][:, 0, :].rearrange("p (h d) -> p h d", d=DH),
                                          rq[:, w].unsqueeze(2).to_broadcast([P, 8, DH]), ALU.mult)\
                            .then_inc(e["qn_made"], 1)

                    def cpq(pr):
                        t = 2 * pr + 1
                        dve.wait_ge(e["qT_made"], m0 + (pr + 3))
                        dve.tensor_copy(QT[:, :, t * P:(t + 1) * P],
                                        psO[pr % 2][:, 1, :].rearrange("p (h t) -> p h t", t=P))\
                            .then_inc(e["qTv_copied"], 1)

                    skewed(dict(red=red, qn=qns, cp=cpq), B_LAG, 4)
                    dve.tensor_tensor(pz, snull[:, :, bass.ds(g * G, G)], rq.rearrange("p (t h) -> p t h", h=G),
                                      ALU.mult).then_inc(e["nz_made"], 1)
                    dve.wait_ge(e["nexp_made"], gi + 1)
                    dve.tensor_tensor(pn, pe_, sb["enull"][:, bass.ds(g * G, G)].unsqueeze(1)
                                      .to_broadcast([P, NT, G]), ALU.mult).then_inc(e["pn_made"], 1)

                    def weigh(f):
                        hh, k = f // NF, f % NF
                        dve.wait_ge(e["exp_made"], f0 + (f + 3))
                        dve.wait_ge(e["pv_made"], f0 + (f + 1))
                        for j, c0 in FILLS[k]:
                            w = width(j)
                            ins = dve.tensor_tensor(Pw[f % 2][:, c0:c0 + w], E[f % 2][:, c0:c0 + w],
                                                    sb["EB"][:, bass.ds(g * G + hh, 1), 0:w].rearrange("p a w -> p (a w)"),
                                                    ALU.mult)
                        ins.then_inc(e["p_made"], 1)

                    def total(hh):
                        u = hh % 2
                        dve.wait_ge(e["pv_made"], f0 + (hh * NF + NF + 2))
                        dve.wait_ge(e["nul_made"], m0 + (hh + 1))
                        dve.wait_ge(e["ao_made"], m0 + (hh + 1))
                        for i in range(2):
                            ins = dve.tensor_tensor(num[u][:, 4 * i:4 * i + 4, :],
                                                    psO[u][:, i, 0:4 * VW].rearrange("p (t d) -> p t d", d=VW),
                                                    nul[u][:, 4 * i:4 * i + 4, :], ALU.add)
                        ins.then_inc(e["num_made"], 1)
                        dve.wait_ge(e["num_made"], m0 + (hh + 3))
                        dve.reciprocal(rec[u].unsqueeze(2), num[u][:, :, DH:VW]).then_inc(e["rec_made"], 1)

                    for f in range(G * NF):
                        weigh(f)
                        if f % NF == 0 and f:
                            total(f // NF - 1)
                    total(G - 1)
                    assert cg.n == CH_G_V, cg.n
                cd = Chain(dve, sv[2])
                cd.base = b * CH_D_V

                def cpa(t):
                    dve.wait_ge(e["aT_made"], n0 + (t + 3))
                    dve.wait_ge(e["y_made"], n0 + (t + 1))
                    dve.tensor_copy(AOT[t % 2][:, 4:8, :].rearrange("p k t -> p (k t)"), psS[t % 2][:, 1, :])\
                        .then_inc(e["aTv_copied"], 1)

                def std(t):
                    u = t % 2
                    dve.wait_ge(e["y_made"], n0 + (t + 3))
                    cd.link(dve.bn_stats(st[u], psO[u][:, 0, :]))
                    dve.memset(idle, 0.0)
                    cd.link(dve.bn_aggr(mv[u], st[u]))
                    dve.tensor_scalar(ve[:, t:t + 1], mv[u][:, 1:2], LN_EPS, None, ALU.add).then_inc(e["var2_ready"], 1)

                def nrm(t):
                    u = t % 2
                    dve.wait_ge(e["var2_ready"], n0 + (t + 1))
                    dve.wait_ge(e["y02_ready"], n0 + (t + 1))
                    cd.link(newton(dve, cd, rs[:, t:t + 1], y0[:, t:t + 1], ve[:, t:t + 1], nt[:, t:t + 1], 1.0))
                    dve.wait_ge(e[f"x1_stored{u}"], b * 64 + 16 * (t // 2 + 1))
                    dve.wait_ge(e["x1T_made"], n0 + (t + 1))
                    cd.link(dve.tensor_scalar(y[u], psO[u][:, 0, :], mv[u][:, 0:1], rs[:, t:t + 1], ALU.subtract, ALU.mult))
                    cd.link(dve.tensor_tensor(y[u], y[u], sb["gout"][:], ALU.mult))
                    dve.wait_ge(e[f"x_in{u}"], b * 128 + 16 * (4 + t // 2 + 1))
                    dve.tensor_tensor(y[u], y[u], xt[:, u, :], ALU.add).then_inc(e["x_used"], 1)

                def lgc(t):
                    dve.wait_ge(e["lg_made"], n0 + (t + 3))
                    dve.tensor_tensor(LG[:, bass.ds(n0 + t, 1), :].rearrange("p a n -> p (a n)"), psO[t % 2][:, 1, 0:NE],
                                      sb["glog"][:, bass.ds(b, 1), :].rearrange("p a n -> p (a n)"), ALU.add)\
                        .then_inc(e["lg_used"], 1)

                skewed(dict(cp=cpa, st=std, nrm=nrm, lgc=lgc), D_LAG, NT)
                assert cd.n == CH_D_V, cd.n


def pipelined(eng, steps, lags, count, unroll):
    order = sorted(steps, key=lambda n: -lags[n])
    deep = max(lags.values())
    head = -(-deep // unroll) * unroll

    def round_(i, r):
        for n in order:
            if isinstance(i, int) and not 0 <= i - lags[n] < count:
                continue
            steps[n](i - lags[n], (r - lags[n]) % unroll)

    for i in range(head):
        round_(i, i)
    with eng.Fori(head // unroll, count // unroll) as q:
        for r in range(unroll):
            round_(q * unroll + r, r)
    for i in range(count, count + deep):
        round_(i, i)


def value(eng, x):
    return x if isinstance(x, int) else eng.snap(x)


MOE_CREDITS = dict(xT_made=2, xT_copied=2, g_used=2, hT_made=2, h_copied=1, dn_made=2, yo_made=4, noted=1)


def experts(nc, a, sb, dr, sem, out):
    LG = sb["LG"]
    with ExitStack() as ctx:
        def tile(name, shape, dt=F32):
            return ctx.enter_context(nc.sbuf_tensor("m_" + name, shape, dt))

        def psum(name):
            return ctx.enter_context(nc.psum_tensor("m_" + name, [P, 512], F32))

        wgu = tile("wgu", [P, NE, KD, 2 * MD])
        wd = tile("wd", [P, NE, MD // P, D])
        sgu = tile("sgu", [P, KD, 2 * SMD])
        sd = tile("sd", [P, SMD // P, D])
        ident = tile("ident", [P, P])
        upper = tile("upper", [P, P])
        ones = tile("ones", [P, P])
        xr = tile("xr", [P, 4, D])
        xT = tile("xT", [P, 2, KD, P])
        tl = tile("tl", [P, 2, SMD])
        lh = tile("lh", [P, 2, SMD])
        hT = tile("hT", [P, 2, SMD // P, P])
        yo = tile("yo", [P, 2, D])
        y1 = tile("y1", [P, 4, D])
        y2 = tile("y2", [P, 4, D])
        psA = [psum(f"A{i}") for i in range(2)]
        psG = [psum(f"G{i}") for i in range(2)]
        psU = [psum(f"U{i}") for i in range(2)]
        psH, psY = psum("H"), psum("Y")

        z = tile("z", [P, NTT, NE])
        t8 = tile("t8", [P, NTT, NE])
        ix = tile("ix", [P, NTT, NE], U32)
        ixf = tile("ixf", [P, NTT, 2])
        o1 = tile("o1", [P, NTT, NE])
        o2 = tile("o2", [P, NTT, NE])
        cnt = tile("cnt", [P, NTT, NE])
        tot = tile("tot", [P, NTT, NE])
        inc = tile("inc", [P, NTT, NE])
        col = tile("col", [P, NTT, 2])
        wts = tile("wts", [P, NTT, 2])
        i8 = tile("i8", [P, NE])
        pad = tile("pad", [P, NE])
        padi = tile("padi", [P, NE], I32)
        end = tile("end", [P, NE])
        first = tile("first", [P, NE])
        slot = tile("slot", [P, SLOTS])
        ge = tile("ge", [P, SLOTS, NE])
        sle = tile("sle", [P, SLOTS])
        slei = tile("slei", [P, SLOTS], I32)
        posu = tile("posu", [P, NTT, 2], U32)
        ib = tile("ib", [P, 4, 2], U32)
        gb = tile("gb", [P, 4, 2], U32)
        note = tile("note", [P, 1])

        c = {n: sem("m_" + n) for n in MOE_CREDITS}
        names = ("rv", "ez", "consts", "cnt_made", "pre_made", "pos_made", "w_shared",
                 "w_exp", "gu_made", "t_made", "l_made", "ib_made", "gb_made", "sum_made", "half_made")
        e = {n: sem("m_" + n) for n in names}
        x_in = [sem(f"m_x_in{i}") for i in range(4)]
        scat = [sem(f"m_scat{i}") for i in range(4)]
        y_st = [sem(f"m_y_st{i}") for i in range(2)]
        s_in = [sem(f"m_s_in{i}") for i in range(2)]
        y_out = [sem(f"m_y_out{i}") for i in range(2)]
        b_in = [sem(f"m_b_in{i}") for i in range(4)]
        g_in = [sem(f"m_g_in{i}") for i in range(4)]
        o_out = [sem(f"m_o_out{i}") for i in range(4)]
        block = ctx.enter_context(nc.Block())

        def rows(ap, i):
            return ap[bass.ds(i * P, P), :]

        x1, base, xs, ys, o = dr["x1"], dr["base"], dr["xs"], dr["ys"], out

        LAG = dict(load=0, scat=0, T=0, xTc=0, gu=1, tl=1, lh=1, T2=2, hTc=2, dn=3, yc=3, store=4)

        @block.sync
        def _(sp):
            sp.dma_start(sgu[:, :, 0:SMD], a["sw_gate"].rearrange("(k p) n -> p k n", p=P)).then_inc(e["w_shared"], 16)
            sp.dma_start(sgu[:, :, SMD:], a["sw_up"].rearrange("(k p) n -> p k n", p=P)).then_inc(e["w_shared"], 16)
            sp.dma_start(sd[:], a["sw_down"].rearrange("(k p) n -> p k n", p=P)).then_inc(e["w_shared"], 16)

            def load(i, r):
                src = rows(x1, i)
                n, m = value(sp, (i - r) * 8), value(sp, i + 1)
                if not isinstance(n, int) or n > 0:
                    sp.wait_ge(scat[r], n)
                sp.wait_ge(c["yo_made"], m)
                sp.dma_start(xr[:, r, :], src).then_inc(x_in[r], 16)

            def store(i, r):
                dst = rows(base, i)
                n = value(sp, i + 5)
                sp.wait_ge(c["yo_made"], n)
                sp.dma_start(dst, yo[:, r % 2, :]).then_inc(y_st[r % 2], 16)

            pipelined(sp, dict(load=load, store=store), LAG, NTT, 4)

            for r in range(4):
                sp.wait_ge(scat[r], 32 * (NTT // 4))
            sp.wait_ge(c["yo_made"], NTT + 4)

            def loads(i, r):
                src = rows(xs, i)
                n = value(sp, i + (NTT + 1))
                sp.wait_ge(c["xT_made"], n)
                sp.dma_start(xr[:, r % 2, :], src).then_inc(s_in[r % 2], 16)

            def stores(i, r):
                dst = rows(ys, i)
                n = value(sp, i + (NTT + 5))
                sp.wait_ge(c["yo_made"], n)
                sp.dma_start(dst, yo[:, r % 2, :]).then_inc(y_out[r % 2], 16)

            pipelined(sp, dict(load=loads, store=stores), LAG, SLOTS, 2)
            for r in range(2):
                sp.wait_ge(y_st[r], 16 * (NTT // 2 + 1))

            def bases(i, r):
                src = rows(base, i)
                n = value(sp, (i - r) * 4 + 16)
                sp.wait_ge(o_out[r], n)
                sp.dma_start(xr[:, r, :], src).then_inc(b_in[r], 16)

            def outs(i, r):
                dst = rows(o, i)
                n = value(sp, i + 1)
                sp.wait_ge(e["sum_made"], n)
                sp.dma_start(dst, xr[:, r, :]).then_inc(o_out[r], 16)

            pipelined(sp, dict(load=bases, out=outs), dict(load=0, out=2), NTT, 4)
            for r in range(4):
                sp.wait_ge(o_out[r], 16 * (NTT // 4 + 1))

        @block.gpsimd
        def _(pool):
            col_ = 0
            for name, n in MOE_CREDITS.items():
                pool.memset(sb["credit"][:, col_:col_ + 1], 0.0).then_inc(c[name], n)
                col_ += 1
            for q in y_st + y_out + o_out:
                pool.memset(sb["credit"][:, col_:col_ + 1], 0.0).then_inc(q, 16)
                col_ += 1
            pool.memset(ident[:], 0.0).then_inc(e["consts"], 1)
            pool.memset(upper[:], 1.0).then_inc(e["consts"], 1)
            pool.memset(ones[:], 1.0).then_inc(e["consts"], 1)
            pool.wait_ge(e["consts"], 3)
            pool.affine_select(out=ident[:], in_=ident[:], compare_op=ALU.not_equal, fill=1.0, base=0,
                               pattern=[[-1, P]], channel_multiplier=1).then_inc(e["consts"], 1)
            pool.affine_select(out=upper[:], in_=upper[:], compare_op=ALU.is_gt, fill=0.0, base=0,
                               pattern=[[1, P]], channel_multiplier=-1).then_inc(e["consts"], 1)
            pool.iota(i8[:], [[1, NE]], base=0, channel_multiplier=0,
                      allow_small_or_imprecise_dtypes=True).then_inc(e["consts"], 1)
            pool.iota(slot[:], [[P, SLOTS]], base=0, channel_multiplier=0,
                      allow_small_or_imprecise_dtypes=True).then_inc(e["consts"], 1)
            for k in range(NE):
                pool.dma_start(wgu[:, k, :, 0:MD], a["w_gate"][k].rearrange("(k p) n -> p k n", p=P)).then_inc(e["w_exp"], 16)
                pool.dma_start(wgu[:, k, :, MD:], a["w_up"][k].rearrange("(k p) n -> p k n", p=P)).then_inc(e["w_exp"], 16)
                pool.dma_start(wd[:, k], a["w_down"][k].rearrange("(k p) n -> p k n", p=P)).then_inc(e["w_exp"], 16)

            def held(n):
                pool.wait_ge(c["noted"], n + 1)
                pool.tensor_tensor(note[:], ones[:, 0:1], ones[:, 0:1], ALU.add).then_inc(c["noted"], 1)

            def scatter(i, r):
                pool.wait_ge(x_in[r], (i - r) * 4 + 16)
                pool.wait_ge(e["ib_made"], i + 1)
                held(i)
                for w in range(2):
                    pool.indirect_dma_start(out=xs, out_offset=bass.IndirectOffsetOnAxis(ap=ib[:, r, w:w + 1], axis=0),
                                            in_=xr[:, r, :], in_offset=None).then_inc(scat[r], 16)

            pipelined(pool, dict(scat=scatter), dict(scat=0), NTT, 4)
            for r in range(2):
                pool.wait_ge(y_out[r], 16 * (SLOTS // 2 + 1))

            def gather(i, r):
                pool.wait_ge(e["gb_made"], i + 1)
                held(i + NTT)
                for w, y in enumerate((y1, y2)):
                    pool.indirect_dma_start(out=y[:, r, :], out_offset=None, in_=ys,
                                            in_offset=bass.IndirectOffsetOnAxis(ap=gb[:, r, w:w + 1], axis=0))\
                        .then_inc(g_in[r], 16)

            pipelined(pool, dict(g=gather), dict(g=0), NTT, 4)

        @block.scalar
        def _(act):
            act.wait_ge(e["rv"], 2)
            act.activation(z[:], z[:], ACT.Exp, scale=0.5).then_inc(e["ez"], 1)

            def stages(off, count, unroll, shared):
                n = SMD if shared else MD

                def xTc(i, r):
                    act.wait_ge(c["xT_made"], i + (off + 3))
                    act.wait_ge(c["g_used"], i + (off + 1))
                    act.activation(xT[:, r % 2].rearrange("p k t -> p (k t)"), psA[r % 2][:], ACT.Copy)\
                        .then_inc(c["xT_copied"], 1)

                def tls(i, r):
                    act.wait_ge(e["gu_made"], i + (off + 1))
                    act.wait_ge(c["g_used"], i + (off + 1))
                    act.activation(tl[:, r % 2, 0:n], psG[r % 2][:, 0:n], ACT.Copy, scale=0.01).then_inc(e["t_made"], 1)

                def yc(i, r):
                    act.wait_ge(c["dn_made"], i + (off + 3))
                    act.wait_ge(y_out[r % 2], (i - r) * 8 + 16 * (1 + r // 2))
                    act.activation(yo[:, r % 2, :], psY[:], ACT.Copy).then_inc(c["yo_made"], 1)

                steps = dict(xTc=xTc, tl=tls)
                if not shared:
                    steps["yc"] = yc
                pipelined(act, steps, LAG, count, unroll)

            stages(0, NTT, 4, True)
            for r in range(2):
                act.wait_ge(y_st[r], 16 * (NTT // 2 + 1))
            stages(NTT, SLOTS, 2, False)

        @block.tensor
        def _(pe):
            pe.wait_ge(e["consts"], 7)
            pe.wait_ge(e["cnt_made"], 1)
            pe.matmul(psH[:, 0:NTT * NE], upper[:], cnt[:].rearrange("p t e -> p (t e)"), start=True, stop=True)\
              .then_inc(e["pre_made"], 1)
            pe.matmul(psY[:, 0:NTT * NE], ones[:], cnt[:].rearrange("p t e -> p (t e)"), start=True, stop=True)\
              .then_inc(e["pre_made"], 1)
            pe.wait_ge(e["pos_made"], 1)
            pe.wait_ge(e["w_shared"], 48)

            def stages(off, count, unroll, shared):
                kh = (SMD if shared else MD) // P

                def T(i, r):
                    s = r if shared else r % 2
                    if shared:
                        pe.wait_ge(x_in[r], (i - r) * 4 + 16)
                    else:
                        pe.wait_ge(s_in[r % 2], (i - r) * 8 + 16)
                    pe.wait_ge(c["xT_copied"], i + (off + 1))
                    for k in range(KD):
                        ins = pe.transpose(psA[r % 2][:, k * P:(k + 1) * P], xr[:, s, k * P:(k + 1) * P], ident[:])
                    ins.then_inc(c["xT_made"], 1)

                def gu(i, r):
                    u = r % 2
                    pe.wait_ge(c["xT_copied"], i + (off + 3))
                    pe.wait_ge(c["g_used"], i + (off + 1))
                    if shared:
                        for half, ps in enumerate((psG[u], psU[u])):
                            for k in range(KD):
                                ins = pe.matmul(ps[:], xT[:, u, k, :], sgu[:, k, half * SMD:(half + 1) * SMD],
                                                start=(k == 0), stop=(k == KD - 1))
                    else:
                        x = pe.value_load(slei[0:1, bass.ds(i, 1)], min_val=0, max_val=NE - 1)
                        for k in range(KD):
                            ins = pe.matmul(psG[u][:], xT[:, u, k, :],
                                            wgu[:, bass.ds(x, 1), k, :].rearrange("p a n -> p (a n)"),
                                            start=(k == 0), stop=(k == KD - 1))
                    ins.then_inc(e["gu_made"], 1)

                def T2(i, r):
                    u = r % 2
                    pe.wait_ge(c["g_used"], i + (off + 3))
                    pe.wait_ge(c["h_copied"], i + (off + 1))
                    for k in range(kh):
                        ins = pe.transpose(psH[:, k * P:(k + 1) * P], lh[:, u, k * P:(k + 1) * P], ident[:])
                    ins.then_inc(c["hT_made"], 1)

                def dn(i, r):
                    u = r % 2
                    pe.wait_ge(c["h_copied"], i + (off + 2))
                    pe.wait_ge(c["yo_made"], i + (off + 4))
                    if not shared:
                        x = pe.value_load(slei[0:1, bass.ds(i, 1)], min_val=0, max_val=NE - 1)
                    for k in range(kh):
                        w = sd[:, k, :] if shared else wd[:, bass.ds(x, 1), k, :].rearrange("p a n -> p (a n)")
                        ins = pe.matmul(psY[:], hT[:, u, k, :], w, start=(k == 0), stop=(k == kh - 1))
                    ins.then_inc(c["dn_made"], 1)

                pipelined(pe, dict(T=T, gu=gu, T2=T2, dn=dn), LAG, count, unroll)

            stages(0, NTT, 4, True)
            pe.wait_ge(e["w_exp"], 48 * NE)
            stages(NTT, SLOTS, 2, False)

        @block.vector
        def _(dve):
            ch = Chain(dve, e["rv"])
            m, s = col[:, :, 0], col[:, :, 1]

            def per_tile(ap):
                return ap.unsqueeze(2).to_broadcast([P, NTT, NE])

            ch.link(dve.tensor_reduce(m, LG[:], AX.X, ALU.max))
            ch.link(dve.tensor_tensor(z[:], LG[:], per_tile(m), ALU.subtract))
            dve.wait_ge(e["ez"], 1)
            ch.link(dve.tensor_reduce(s, z[:], AX.X, ALU.add))
            ch.link(dve.reciprocal(m, s))
            ch.link(dve.tensor_tensor(z[:], z[:], per_tile(m), ALU.mult))
            for t in range(NTT):
                ins = dve.max(t8[:, t, :], z[:, t, :])
            ch.link(ins)
            for t in range(NTT):
                ins = dve.max_index(ix[:, t, :], t8[:, t, :], z[:, t, :])
            ch.link(ins)
            ch.link(dve.tensor_copy(ixf[:], ix[:, :, 0:2]))
            dve.wait_ge(e["consts"], 7)
            e8 = i8[:].unsqueeze(1).to_broadcast([P, NTT, NE])
            for w, oh in enumerate((o1, o2)):
                ins = dve.tensor_tensor(oh[:], per_tile(ixf[:, :, w]), e8, ALU.is_equal)
            ch.link(ins)
            dve.tensor_tensor(cnt[:], o1[:], o2[:], ALU.add).then_inc(e["cnt_made"], 1)
            ch.link(dve.tensor_tensor(s, t8[:, :, 0], t8[:, :, 1], ALU.add))
            ch.link(dve.tensor_scalar(s, s, 1e-20, None, ALU.add))
            ch.link(dve.reciprocal(m, s))
            ch.link(dve.tensor_tensor(wts[:], t8[:, :, 0:2], m.unsqueeze(2).to_broadcast([P, NTT, 2]), ALU.mult))
            dve.wait_ge(e["pre_made"], 2)
            ch.link(dve.tensor_copy(tot[:].rearrange("p t e -> p (t e)"), psY[:, 0:NTT * NE]))
            for x in range(NE):
                ins = dve.tensor_tensor_scan(inc[:, :, x], ones[:, 0:NTT], tot[:, :, x], 0.0, ALU.mult, ALU.add)
            ch.link(ins)
            ch.link(dve.tensor_scalar(pad[:], inc[:, NTT - 1, :], float(P - 1), None, ALU.add))
            ch.link(dve.tensor_copy(padi[:], pad[:]))
            sh = P.bit_length() - 1
            ch.link(dve.tensor_scalar(padi[:], padi[:], sh, sh, ALU.logical_shift_right, ALU.logical_shift_left))
            ch.link(dve.tensor_copy(pad[:], padi[:]))
            ch.link(dve.tensor_tensor_scan(end[:], ones[:, 0:NE], pad[:], 0.0, ALU.mult, ALU.add))
            ch.link(dve.tensor_tensor(first[:], end[:], pad[:], ALU.subtract))
            ch.link(dve.tensor_tensor(inc[:], inc[:], tot[:], ALU.subtract))
            ch.link(dve.tensor_tensor(inc[:], inc[:], first[:].unsqueeze(1).to_broadcast([P, NTT, NE]), ALU.add))
            ch.link(dve.tensor_tensor(inc[:].rearrange("p t e -> p (t e)"), psH[:, 0:NTT * NE],
                                      inc[:].rearrange("p t e -> p (t e)"), ALU.add))
            for w, oh in enumerate((o1, o2)):
                ch.link(dve.tensor_tensor(oh[:], oh[:], inc[:], ALU.mult))
                ch.link(dve.tensor_reduce(ixf[:, :, w], oh[:], AX.X, ALU.add))
            ch.link(dve.tensor_copy(posu[:], ixf[:]))
            ch.link(dve.tensor_tensor(ge[:], slot[:].unsqueeze(2).to_broadcast([P, SLOTS, NE]),
                                      end[:].unsqueeze(1).to_broadcast([P, SLOTS, NE]), ALU.is_ge))
            ch.link(dve.tensor_reduce(sle[:], ge[:], AX.X, ALU.add))
            ch.link(dve.tensor_scalar(sle[:], sle[:], float(NE - 1), None, ALU.min))
            dve.tensor_copy(slei[:], sle[:]).then_inc(e["pos_made"], 1)

            def stages(off, count, unroll, shared):
                n = SMD if shared else MD

                def index(i, r):
                    if not isinstance(i, int) or i >= 4:
                        dve.wait_ge(scat[r], (i - r) * 8)
                    dve.tensor_copy(ib[:, r, :], posu[:, bass.ds(i, 1), :].rearrange("p a w -> p (a w)"))\
                       .then_inc(e["ib_made"], 1)

                def lhs(i, r):
                    u = r % 2
                    up = psU[u][:, 0:n] if shared else psG[u][:, MD:2 * MD]
                    dve.wait_ge(e["t_made"], i + (off + 1))
                    dve.wait_ge(c["hT_made"], i + (off + 1))
                    dve.tensor_tensor(lh[:, u, 0:n], psG[u][:, 0:n], tl[:, u, 0:n], ALU.max).then_inc(e["l_made"], 1)
                    dve.wait_ge(e["l_made"], i + (off + 1))
                    dve.tensor_tensor(lh[:, u, 0:n], up, lh[:, u, 0:n], ALU.mult).then_inc(c["g_used"], 1)

                def hTc(i, r):
                    dve.wait_ge(c["hT_made"], i + (off + 3))
                    dve.wait_ge(c["dn_made"], i + (off + 1))
                    dve.tensor_copy(hT[:, r % 2].rearrange("p k t -> p (k t)")[:, 0:n], psH[:, 0:n])\
                       .then_inc(c["h_copied"], 1)

                def add(i, r):
                    dve.wait_ge(c["dn_made"], i + (off + 3))
                    dve.wait_ge(y_st[r % 2], (i - r) * 8 + 16 * (1 + r // 2))
                    dve.tensor_tensor(yo[:, r % 2, :], psY[:], xr[:, r, :], ALU.add).then_inc(c["yo_made"], 1)

                steps = dict(lh=lhs, hTc=hTc)
                if shared:
                    steps.update(scat=index, yc=add)
                pipelined(dve, steps, LAG, count, unroll)

            stages(0, NTT, 4, True)
            stages(NTT, SLOTS, 2, False)

            def gindex(i, r):
                dve.tensor_copy(gb[:, r, :], posu[:, bass.ds(i, 1), :].rearrange("p a w -> p (a w)"))\
                   .then_inc(e["gb_made"], 1)

            def total(i, r):
                dve.wait_ge(b_in[r], (i - r) * 4 + 16)
                dve.wait_ge(g_in[r], (i - r) * 8 + 32)
                w = wts[:, bass.ds(i, 1), :].rearrange("p a w -> p (a w)")
                dve.scalar_tensor_tensor(out=xr[:, r, :], in0=y1[:, r, :], scalar=w[:, 0:1], in1=xr[:, r, :],
                                         op0=ALU.mult, op1=ALU.add).then_inc(e["half_made"], 1)
                dve.wait_ge(e["half_made"], i + 1)
                dve.scalar_tensor_tensor(out=xr[:, r, :], in0=y2[:, r, :], scalar=w[:, 1:2], in1=xr[:, r, :],
                                         op0=ALU.mult, op1=ALU.add).then_inc(e["sum_made"], 1)

            pipelined(dve, dict(g=gindex, s=total), dict(g=0, s=2), NTT, 4)


INS = dict(x="x", cond_64="cond", mask_BxS_bf1="mask", L0_cond_g_norm="g_norm", L0_cond_Wq="Wq", L0_cond_Wkv="Wkv",
           L0_cond_q_scale="q_scale", L0_cond_k_scale="k_scale", L0_cond_null_attn_bias="null_bias",
           L0_cond_w0="w0", L0_cond_b0="b0", L0_cond_g0="g0", L0_cond_w1="w1", L0_cond_b1="b1", L0_cond_g1="g1",
           L0_cond_w2="w2", L0_cond_b2="b2", L0_cond_Wout="Wout", L0_cond_g_out="g_out",
           L1_cond_wt="wt", L1_cond_wg="wg", L1_cond_w_gate="w_gate", L1_cond_w_up="w_up", L1_cond_w_down="w_down",
           L1_cond_sw_gate="sw_gate", L1_cond_sw_up="sw_up", L1_cond_sw_down="sw_down")


def build(nc, a, out):
    with ExitStack() as ctx:
        def sem(name):
            return ctx.enter_context(nc.semaphore(name))

        sb = {n: sem(n) for n in CREDITS}
        dr = dict(bias=nc.dram_tensor("bias_rows", (H, P, P + S), F32, kind="Internal").ap(),
                  enull=nc.dram_tensor("enull_row", (H,), F32, kind="Internal").ap(),
                  x1=nc.dram_tensor("x1_rows", (T, D), F32, kind="Internal").ap(),
                  base=nc.dram_tensor("base_rows", (T, D), F32, kind="Internal").ap(),
                  xs=nc.dram_tensor("sorted_rows", (SLOTS * P, D), F32, kind="Internal").ap(),
                  ys=nc.dram_tensor("expert_rows", (SLOTS * P, D), F32, kind="Internal").ap())
        sb["LG"] = ctx.enter_context(nc.sbuf_tensor("LG", [P, NTT, NE], F32))
        sb["credit"] = ctx.enter_context(nc.sbuf_tensor("credit", [P, 48], F32))
        with ExitStack() as att:
            def tile(name, shape, dt=F32):
                sb[name] = att.enter_context(nc.sbuf_tensor(name, shape, dt))

            tile("ident", [P, P])
            tile("EB", [P, H, S])
            tile("W", [P, KD, WQKV])
            tile("Wo", [P, 8, D])
            tile("wtT", [P, KD, NE])
            tile("gout", [P, D])
            tile("vnull", [P, VW])
            tile("negc", [P, 1])
            tile("enull", [P, H])
            tile("kfac", [P, DH])
            tile("maskf", [P, NTT])
            tile("glog", [P, B, NE])
            setup(nc, a, sb, dr, sem)
            tile("xnT", [P, KD, S])
            tile("QT", [P, G, S], F32R)
            tile("KT", [P, 2, S], F32R)
            tile("V", [P, NT, VW])
            tile("AO", [P, NT, H * DH])
            tile("R1", [P, 4096])
            tile("R2", [P, 4 * NT * VW])
            tile("xt", [P, 2, D])
            tile("small", [P, 560])
            psum = {n: [att.enter_context(nc.psum_tensor(f"ps{n}{i}", [P, 2, 512], F32)) for i in range(2)] for n in "SO"}
            attention(nc, a, sb, dr, sem, psum)
        experts(nc, a, sb, dr, sem, out.rearrange("b s d -> (b s) d"))


def kernel(**inputs):
    import numpy as np
    import concourse.bacc as bacc
    from concourse.bass_utils import run_bass_kernel_spmd

    nc = bacc.Bacc("TRN2", target_bir_lowering=False, num_devices=1)
    arrays, a = {}, {}
    for name, short in INS.items():
        v = np.ascontiguousarray(inputs[name])
        if v.dtype == np.bool_:
            v = v.view(np.uint8)
        arrays[f"in_{name}"] = v
        a[short] = nc.dram_tensor(f"in_{name}", v.shape, mybir.dt.from_np(v.dtype), kind="ExternalInput").ap()
    out = nc.dram_tensor("out_0", (B, S, D), F32, kind="ExternalOutput").ap()
    build(nc, a, out)
    r = run_bass_kernel_spmd(nc, [arrays], core_ids=[0])
    return r.results[0]["out_0"]
```

```python
from contextlib import ExitStack

import concourse.bass as bass
from concourse import mybir

P = 128
F32 = mybir.dt.float32
F32R = mybir.dt.float32r
I32 = mybir.dt.int32
U32 = mybir.dt.uint32
ALU = mybir.AluOpType
ACT = mybir.ActivationFunctionType
AX = mybir.AxisListType

B, S, D = 4, 1024, 512
H, DH = 16, 64
KD = D // P
NT = S // P
G = 2
NG = H // G
VW = DH + 1
WQKV = H * DH + 2 * DH + H
KVC = H * DH
NE, MD, SMD = 8, 256, 512
T = B * S
NTT = T // P
NS = NTT // 2
SLOTS = 2 * NTT + NE
LN_EPS = 1e-5
NORM_EPS = 1e-12
HEAD = 40.0
LIFT = 24

FILLS = [[(0, 0)], [(1, 0)], [(2, 0), (6, 768)], [(3, 0), (5, 640)], [(4, 0), (7, 512)]]
NF = len(FILLS)


def width(j):
    return S - P * j


def fill_width(k):
    j, c = FILLS[k][-1]
    return c + width(j)


class Chain:

    def __init__(self, eng, sem):
        self.eng, self.sem, self.base, self.n = eng, sem, 0, 0

    def link(self, ins):
        ins.then_inc(self.sem, 1)
        self.n += 1
        self.eng.wait_ge(self.sem, self.base + self.n)


def newton(dve, ch, y, y0, v, t, f):
    ch.link(dve.tensor_tensor(t, y0, y0, ALU.mult))
    ch.link(dve.tensor_tensor(t, t, v, ALU.mult))
    ch.link(dve.tensor_scalar(t, t, -0.5 * f * f * f, 1.5 * f, ALU.mult, ALU.add))
    return dve.tensor_tensor(y, y0, t, ALU.mult)


def setup(nc, a, sb, dr, sem):
    HW = NT * D
    with ExitStack() as ctx:
        def tmp(name, shape, dt=F32):
            return ctx.enter_context(nc.sbuf_tensor(name, shape, dt))

        def psum(name, shape):
            return ctx.enter_context(nc.psum_tensor(name, shape, F32))

        rows = {n: tmp("row_" + n, [P, D]) for n in ("w0", "b0", "g0", "b1", "g1")}
        gn = tmp("gn", [P, KD])
        w1 = tmp("w1", [P, KD, D])
        w2 = tmp("w2", [P, KD, H])
        h = tmp("h", [P, NT, D])
        hT = tmp("hT", [P, KD, S])
        pos = tmp("pos", [P, NT])
        st = tmp("st", [P, NT, 6])
        mv = tmp("mv", [P, NT, 2])
        ve = tmp("ve", [P, NT])
        y0 = tmp("y0", [P, NT])
        nt = tmp("nt", [P, NT])
        rs = tmp("rs", [P, NT])
        cond = tmp("cond", [P, B * DH])
        qs = tmp("qs", [P, DH])
        ks = tmp("ks", [P, DH])
        c2 = tmp("c2", [P, DH])
        ss = tmp("ss", [P, 4])
        kn = tmp("kn", [P, DH])
        wg = tmp("wg", [P, NE, DH])
        wgp = tmp("wgp", [P, NE, DH])
        mask8 = tmp("mask8", [P, NTT], mybir.dt.uint8)
        brow = tmp("brow", [H, P + S])
        braw = tmp("braw", [H, S])
        hcol = tmp("hcol", [H, 8])
        pA = [psum(f"pA{i}", [P, 512]) for i in range(4)]
        pB = psum("pB", [H, 2, 512])
        flip = tmp("flip", [P, P])
        turned = [x.rearrange("p a b -> p (a b)").rearrange("p (h s) -> p h s", s=S) for x in (h[:], hT[:])]
        wprod = hT[:, 0, :].rearrange("p (h d) -> p h d", h=H)

        s_rows, s_w, s_cond, s_mask = sem("s_rows"), sem("s_w"), sem("s_cond"), sem("s_mask")
        s_id, s_pos, s_dve, s_var, s_y0 = sem("s_id"), sem("s_pos"), sem("s_dvec"), sem("s_svar"), sem("s_sy0")
        s_z, s_silu, s_tr, s_ev, s_mm, s_mv = (sem("s_" + n) for n in ("z", "silu", "tr", "ev", "mm", "mmev"))
        s_b, s_bex, s_bx, s_eb, s_kn = sem("s_b"), sem("s_bex"), sem("s_bx"), [sem("s_eb0"), sem("s_eb1")], sem("s_kn")
        s_half = [sem("s_half0"), sem("s_half1")]
        s_pw, s_dve2, s_hb = sem("s_pw"), sem("s_dve2"), sem("s_hb")
        s_flip, s_en = sem("s_flip"), sem("s_en")
        block = ctx.enter_context(nc.Block())

        def bcast(ap, n):
            return bass.AP(ap.tensor, ap.offset, [[0, P], [1, n]])

        @block.sync
        def _(sp):
            sp.dma_start(rows["w0"][:], bcast(a["w0"], D)).then_inc(s_rows, 16)
            for n in ("b0", "g0", "b1", "g1"):
                sp.dma_start(rows[n][:], bcast(a[n], D)).then_inc(s_rows, 16)
            sp.dma_start(cond[:], bcast(a["cond"], B * DH)).then_inc(s_cond, 16)
            sp.dma_start(qs[:], bcast(a["q_scale"], DH)).then_inc(s_cond, 16)
            sp.dma_start(ks[:], bcast(a["k_scale"], DH)).then_inc(s_cond, 16)
            sp.dma_start(wg[:], bass.AP(a["wg"].tensor, 0, [[0, P], [DH, NE], [1, DH]])).then_inc(s_cond, 16)
            sp.dma_start(gn[:], a["g_norm"].rearrange("(k p) -> p k", p=P),
                         allow_slow_non_contiguous=True).then_inc(s_w, 16)
            sp.dma_start(sb["W"][:, :, 0:KVC], a["Wq"].rearrange("(k p) n -> p k n", p=P)).then_inc(s_w, 16)
            sp.dma_start(sb["W"][:, :, KVC:KVC + 2 * DH], a["Wkv"].rearrange("(k p) n -> p k n", p=P)).then_inc(s_w, 16)
            sp.dma_start(mask8[:], a["mask"].rearrange("b (t p) -> p (b t)", p=P),
                         allow_slow_non_contiguous=True).then_inc(s_mask, 16)
            sp.wait_ge(s_bx, 2)
            sp.dma_start(dr["bias"], brow[:]).then_inc(s_bex, 16)
            sp.dma_start(dr["enull"].rearrange("(h a) -> h a", a=1), hcol[:, 5:6]).then_inc(s_bex, 16)
            sp.wait_ge(s_bex, 32)
            sp.dma_start(sb["enull"][:], bcast(dr["enull"], H)).then_inc(s_en, 16)
            for q in range(4):
                if q >= 2:
                    sp.wait_ge(s_flip, 8 * (q - 1))
                src = bass.AP(dr["bias"].tensor, 4 * q * (P + S), [[1, P], [P + S, 4], [1, S]])
                sp.dma_start(turned[q % 2], src).then_inc(s_eb[q % 2], 16)
            sp.wait_ge(s_en, 16)

        @block.gpsimd
        def _(pool):
            pool.memset(sb["ident"][:], 0.0).then_inc(s_id, 1)
            pool.wait_ge(s_id, 1)
            pool.affine_select(out=sb["ident"][:], in_=sb["ident"][:], compare_op=ALU.not_equal, fill=1.0, base=0,
                               pattern=[[-1, P]], channel_multiplier=1).then_inc(s_id, 1)
            pool.memset(flip[:], 0.0).then_inc(s_id, 1)
            pool.memset(sb["zero"][:], 0.0).then_inc(s_id, 1)
            pool.wait_ge(s_id, 4)
            pool.affine_select(out=flip[:], in_=flip[:], compare_op=ALU.not_equal, fill=1.0, base=1 - P,
                               pattern=[[1, P]], channel_multiplier=1).then_inc(s_id, 1)
            pool.iota(pos[:], [[P, NT]], base=0, channel_multiplier=1,
                      allow_small_or_imprecise_dtypes=True).then_inc(s_pos, 1)
            for i, name in enumerate(CREDITS):
                pool.memset(sb["credit"][:, i:i + 1], 0.0).then_inc(sb[name], CREDITS[name])
            pool.wait_ge(s_kn, 2)
            for k in range(KD):
                if k:
                    pool.wait_ge(s_pw, 2 * k)
                pool.tensor_tensor(wprod, sb["W"][:, k, 0:KVC].rearrange("p (h d) -> p h d", h=H),
                                   kn[:].unsqueeze(1).to_broadcast([P, H, DH]), ALU.mult).then_inc(s_pw, 1)

        @block.scalar
        def _(act):
            act.dma_start(w1[:], a["w1"].rearrange("(k p) n -> p k n", p=P)).then_inc(s_mv, 16)
            act.dma_start(w2[:], a["w2"].rearrange("(k p) n -> p k n", p=P)).then_inc(s_mv, 16)
            act.dma_start(hcol[:, 0:1], a["b2"].rearrange("(h a) -> h a", a=1)).then_inc(s_mv, 16)
            act.dma_start(hcol[:, 1:2], a["null_bias"].rearrange("(h a) -> h a", a=1)).then_inc(s_mv, 16)
            act.dma_start(sb["Wo"][:], a["Wout"].rearrange("(k p) n -> p k n", p=P)).then_inc(s_w, 16)
            act.dma_start(sb["gout"][:], bcast(a["g_out"], D)).then_inc(s_w, 16)
            for k in range(KD):
                act.dma_start(sb["wtT"][:, k, :], bass.AP(a["wt"].tensor, k * P, [[1, P], [D, NE]]),
                              allow_slow_non_contiguous=True).then_inc(s_w, 16)
            act.wait_ge(s_kn, 1)
            act.activation(ss[:, 1:2], ss[:, 0:1], ACT.Ln, scale=float(2 ** LIFT)).then_inc(s_y0, 1)
            act.wait_ge(s_y0, 1)
            act.activation(ss[:, 2:3], ss[:, 1:2], ACT.Exp, scale=-0.5).then_inc(s_y0, 1)
            for layer in range(2):
                act.wait_ge(s_var, layer + 1)
                act.activation(nt[:], ve[:], ACT.Ln).then_inc(s_y0, 1)
                act.wait_ge(s_y0, 3 + 2 * layer)
                act.activation(y0[:], nt[:], ACT.Exp, scale=-0.5).then_inc(s_y0, 1)
                act.wait_ge(s_z, layer + 1)
                act.activation(h[:], h[:], ACT.Silu).then_inc(s_silu, 1)
                for i in range(8):
                    if i % 2:
                        act.wait_ge(s_tr, 8 * layer + i + 1)
                        if layer:
                            act.wait_ge(s_mm, NT)
                        act.activation(hT[:, i // 2, (i % 2) * 512:(i % 2 + 1) * 512], pA[i % 4][:], ACT.Copy)\
                           .then_inc(s_ev, 1)
            act.wait_ge(s_b, 1)
            act.activation(brow[:, P - 1:P - 1 + S], braw[:], ACT.Exp, bias=hcol[:, 4:5]).then_inc(s_bx, 1)
            act.activation(hcol[:, 5:6], hcol[:, 1:2], ACT.Exp, bias=hcol[:, 4:5]).then_inc(s_bx, 1)
            for i in range(1, 2 * H, 2):
                act.wait_ge(s_flip, i + 1)
                act.activation(sb["EB"][:, i // 2, 512:1024], pA[i % 4][:], ACT.Copy).then_inc(s_half[1], 1)

        @block.tensor
        def _(pe):
            pe.wait_ge(s_id, 2)
            for layer in range(2):
                pe.wait_ge(s_silu, layer + 1)
                for i in range(8):
                    k, half = i // 2, i % 2
                    if i >= 4:
                        pe.wait_ge(s_ev if i % 2 else s_dve2, 4 * layer + (i - 4) // 2 + 1)
                    for c in range(4):
                        ins = pe.transpose(pA[i % 4][:, c * P:(c + 1) * P],
                                           h[:, half * 4 + c, k * P:(k + 1) * P], sb["ident"][:])
                    ins.then_inc(s_tr, 1)
                pe.wait_ge(s_ev, 4 * layer + 4)
                pe.wait_ge(s_dve2, 4 * layer + 4)
                if layer == 0:
                    pe.wait_ge(s_mv, 64)
                    for c in range(NT):
                        if c >= 4:
                            pe.wait_ge(s_hb, c - 3)
                        for k in range(KD):
                            ins = pe.matmul(pA[c % 4][:], hT[:, k, c * P:(c + 1) * P], w1[:, k, :],
                                            start=(k == 0), stop=(k == KD - 1))
                        ins.then_inc(s_mm, 1)
                    pe.wait_ge(s_hb, NT)
                else:
                    for half in range(2):
                        for k in range(KD):
                            ins = pe.matmul(pB[:, half, :], w2[:, k, :], hT[:, k, half * 512:(half + 1) * 512],
                                            start=(k == 0), stop=(k == KD - 1))
                        ins.then_inc(s_mm, 1)
            pe.wait_ge(s_id, 5)
            for i in range(2 * H):
                if i % 8 == 0:
                    pe.wait_ge(s_eb[i // 8 % 2], 16 * (i // 16 + 1))
                if i >= 4:
                    pe.wait_ge(s_half[i % 2], (i - 4) // 2 + 1)
                pe.matmul(pA[i % 4][:], flip[:], turned[i // 8 % 2][:, i // 2 % 4, (i % 2) * 512:(i % 2 + 1) * 512],
                          start=True, stop=True).then_inc(s_flip, 1)

        @block.vector
        def _(dve):
            ch = Chain(dve, s_dve)
            dve.wait_ge(s_id, 2)
            ch.link(dve.tensor_copy(sb["identr"][:], sb["ident"][:]))
            dve.wait_ge(s_cond, 64)
            ch.link(dve.tensor_tensor(c2[:], cond[:, 0:DH], cond[:, 0:DH], ALU.mult))
            ch.link(dve.tensor_reduce(ss[:, 0:1], c2[:], AX.X, ALU.add))
            dve.tensor_scalar(ss[:, 0:1], ss[:, 0:1], NORM_EPS ** 2, None, ALU.max).then_inc(s_kn, 1)
            ch.link(dve.scalar_tensor_tensor(out=sb["kfac"][:], in0=qs[:], scalar=float(DH) ** 0.5, in1=ks[:],
                                             op0=ALU.mult, op1=ALU.mult))
            ch.link(dve.tensor_reduce(c2[:, 0:1], sb["kfac"][:], AX.X, ALU.max, apply_absolute_value=True))
            ch.link(dve.tensor_scalar(sb["negc"][:], c2[:, 0:1], -1.0, HEAD, ALU.mult, ALU.add))
            dve.wait_ge(s_y0, 2)
            dve.wait_ge(s_kn, 1)
            ch.link(newton(dve, ch, ss[:, 3:4], ss[:, 2:3], ss[:, 0:1], ss[:, 1:2], float(2 ** (LIFT // 2))))
            ch.link(dve.scalar_tensor_tensor(out=kn[:], in0=cond[:, 0:DH], scalar=ss[:, 3:4], in1=sb["kfac"][:],
                                             op0=ALU.mult, op1=ALU.mult))
            ch.link(dve.memset(sb["vnull"][:], 1.0))
            ch.link(dve.tensor_copy(sb["vnull"][:, 0:DH], cond[:, DH:2 * DH]))
            dve.wait_ge(s_w, 16 * (5 + KD))
            for k in range(KD):
                ins = dve.tensor_scalar(sb["W"][:, k, 0:KVC + 2 * DH], sb["W"][:, k, 0:KVC + 2 * DH], gn[:, k:k + 1],
                                        None, ALU.mult)
                if k == KD - 1:
                    ins.then_inc(s_kn, 1)
                else:
                    ch.link(ins)
            for b in range(B):
                ch.link(dve.tensor_tensor(wgp[:], wg[:], cond[:, b * DH:(b + 1) * DH].unsqueeze(1)
                                          .to_broadcast([P, NE, DH]), ALU.mult))
                ch.link(dve.tensor_reduce(sb["glog"][:, b, :], wgp[:], AX.X, ALU.add))
            dve.wait_ge(s_mask, 16)
            ch.link(dve.tensor_copy(sb["maskf"][:], mask8[:]))
            dve.wait_ge(s_rows, 80)
            dve.wait_ge(s_pos, 1)
            for k in range(KD):
                dve.wait_ge(s_pw, 1 + 2 * k)
                dve.tensor_reduce(sb["W"][:, k, KVC + 2 * DH:], wprod, AX.X, ALU.add).then_inc(s_pw, 1)
            for c in range(NT):
                ins = dve.scalar_tensor_tensor(out=h[:, c, :], in0=rows["w0"][:], scalar=pos[:, c:c + 1],
                                               in1=rows["b0"][:], op0=ALU.mult, op1=ALU.add)
            ch.link(ins)
            for layer in range(2):
                if layer:
                    for c in range(NT):
                        dve.wait_ge(s_mm, c + 1)
                        ins = dve.tensor_tensor(h[:, c, :], pA[c % 4][:], rows["b1"][:], ALU.add)
                        ins.then_inc(s_hb, 1)
                    dve.wait_ge(s_hb, NT)
                for c in range(NT):
                    ins = dve.bn_stats(st[:, c, :], h[:, c, :])
                ch.link(ins)
                for c in range(NT):
                    ins = dve.bn_aggr(mv[:, c, :], st[:, c, :])
                ch.link(ins)
                dve.tensor_scalar(ve[:], mv[:, :, 1], LN_EPS, None, ALU.add).then_inc(s_var, 1)
                dve.wait_ge(s_var, layer + 1)
                dve.wait_ge(s_y0, 4 + 2 * layer)
                ch.link(newton(dve, ch, rs[:], y0[:], ve[:], nt[:], 1.0))
                for c in range(NT):
                    ins = dve.tensor_scalar(h[:, c, :], h[:, c, :], mv[:, c, 0:1], rs[:, c:c + 1],
                                            ALU.subtract, ALU.mult)
                ch.link(ins)
                gain = rows["g1" if layer else "g0"]
                dve.tensor_tensor(h[:], h[:], gain[:].unsqueeze(1).to_broadcast([P, NT, D]), ALU.mult)\
                   .then_inc(s_z, 1)
                for i in range(0, 8, 2):
                    dve.wait_ge(s_tr, 8 * layer + i + 1)
                    if layer:
                        dve.wait_ge(s_mm, NT)
                    dve.tensor_copy(hT[:, i // 2, 0:512], pA[i % 4][:]).then_inc(s_dve2, 1)
            ch.link(dve.memset(brow[:], 0.0))
            dve.wait_ge(s_mm, NT + 2)
            dve.wait_ge(s_mv, 64)
            ch.link(dve.tensor_scalar(braw[:], pB[:].rearrange("h a n -> h (a n)"), hcol[:, 0:1], None, ALU.add))
            ch.link(dve.tensor_reduce(hcol[:, 2:3], braw[:], AX.X, ALU.max))
            ch.link(dve.tensor_tensor(hcol[:, 3:4], hcol[:, 2:3], hcol[:, 1:2], ALU.max))
            dve.tensor_scalar(hcol[:, 4:5], hcol[:, 3:4], -1.0, None, ALU.mult).then_inc(s_b, 1)
            for i in range(0, 2 * H, 2):
                dve.wait_ge(s_flip, i + 1)
                dve.tensor_copy(sb["EB"][:, i // 2, 0:512], pA[i % 4][:]).then_inc(s_half[0], 1)


CREDITS = {n: 2 for n in (
    "x_used", "xT_made", "xT_copied", "kv_used", "kT_made", "kT_copied",
    "qst_made", "qT_made", "qTa_copied", "qTv_copied",
    "exp_made", "pv_made", "num_made", "ao_made",
    "aT_made", "aTa_copied", "aTv_copied", "y_made", "x1T_made", "x1T_copied", "lg_made", "lg_used")}
CREDITS.update(x1_stored0=16, x1_stored1=16)
EVENTS = ("var_ready", "y0_ready", "kv_made", "ssk_made", "ssk_clamped", "yk_ready", "kst_made",
          "q_made", "sq_made", "qn_made", "p_made", "ssq_made", "yq_made", "qhi_made", "nz_made", "nexp_made", "pn_made",
          "s_made", "rec_made", "nul_made", "var2_ready", "y02_ready", "x_in0", "x_in1", "filled")

A_LAG = dict(stats=0, y0=0, xn=1, T=1, xTc=1, kv=2, sq=2, ck=3, yk=3, k=4, kT=4, kTc=5)
PE_Q = {0: [("Q", 0), ("Q", 1)], 1: [("Q", 2), ("Q", 3)], 2: [("Q", 4)], 3: [("Q", 5)], 4: [("Q", 6), ("Q", 7)],
        5: [("T", 0)], 7: [("T", 1)], 9: [("T", 2)], 11: [("T", 3)]}
ACT_Q = {1: [("sq", 0)], 2: [("y", 0)], 3: [("hi", 0)], 5: [("cp", 0), ("sq", 1)], 6: [("y", 1)], 7: [("hi", 1)],
         9: [("cp", 1)]}
DVE_Q = {1: [("red", 0)], 2: [("qn", 0)], 5: [("red", 1)], 6: [("qn", 1)], 7: [("cp", 0)], 9: [("cp", 1)]}
D_LAG = dict(TA=0, cp=1, Y=1, st=2, y0=2, nrm=3, T1=3, x1Tc=4, lg=4, lgc=5)
CH_A_V, CH_G_V, CH_D_V = 96, 10, 64
CH_A_A, CH_G_A, CH_D_A = 16, 2, 8


def skewed(steps, lags, count):
    order = sorted(steps, key=lambda n: -lags[n])
    for i in range(count + max(lags.values())):
        for n in order:
            if 0 <= i - lags[n] < count:
                steps[n](i - lags[n])


def beside(table, fill, steps):
    for name, n in table.get(fill, ()):
        steps[name](n)


def attention(nc, a, sb, dr, sem, psum):
    e = {n: sem(n) for n in EVENTS}
    e.update({n: sb[n] for n in CREDITS})
    psS, psO = psum["S"], psum["O"]
    R1, R2, xt = sb["R1"], sb["R2"], sb["xt"]
    xnT, QT, KT, V, AO, LG = (sb[n] for n in ("xnT", "QT", "KT", "V", "AO", "LG"))
    ident = sb["ident"]

    def r1(n, size, base=0):
        return R1[:, base + n * size:base + (n + 1) * size]

    xn = [r1(u, D) for u in range(2)]
    knr = [r1(u, DH, 2 * D) for u in range(2)]
    ksq = [r1(u, DH, 2 * D + 2 * DH) for u in range(2)]
    kst = [sb["parts"][:, u * 4 * DH:(u + 1) * 4 * DH].rearrange("p (s r d) -> p s r d", s=2, r=2) for u in range(2)]
    qst = sb["parts"][:].rearrange("p (n s d) -> p n s d", s=2, d=DH)
    identr = sb["identr"]
    qn = R1[:, 3072:3584].rearrange("p (n d) -> p n d", d=DH)
    E = [r1(u, 1024) for u in range(3)]
    nul, *num = [R2[:, u * NT * VW:(u + 1) * NT * VW].rearrange("p (t d) -> p t d", d=VW) for u in range(3)]
    AOT = [r1(u, 1024).rearrange("p (k t) -> p k t", t=P) for u in range(2)]
    y = [r1(u, 512, 2048) for u in range(2)]
    x1T = [R2[:, u * 512:(u + 1) * 512].rearrange("p (k t) -> p k t", t=P) for u in range(2)]

    sm = sb["small"]
    c = [0]

    def small(n):
        c[0] += n
        return sm[:, c[0] - n:c[0]]

    st = [small(6) for _ in range(2)]
    mv = [small(2) for _ in range(2)]
    ve, lv, y0, rs, nt = (small(NT) for _ in range(5))
    ssk, ssc, lk, yk, rk = (small(NT) for _ in range(5))
    ssq, lq, yq, rq = (small(NT * G) for _ in range(4))
    nq, idle = small(8), small(1)
    rec = [small(8) for _ in range(2)]
    pz, pe_, pn = (small(NT * G).rearrange("p (t h) -> p t h", h=G) for _ in range(3))
    snull = small(NT * H).rearrange("p (t h) -> p t h", h=H)

    sv, sa = [sem("dve_" + n) for n in "agd"], [sem("act_" + n) for n in "agd"]
    block_ctx = nc.Block()
    with block_ctx as block:
        @block.sync
        def _(sp):
            with sp.Fori(0, B) as b:
                def load(t, m):
                    n = sp.snap(b * 16 + (m + 1))
                    src = a["x"][bass.ds(b, 1), t * P:(t + 1) * P, :].rearrange("a p n -> (a p) n")
                    sp.wait_ge(e["x_used"], n)
                    sp.dma_start(xt[:, t % 2, :], src).then_inc(e[f"x_in{t % 2}"], 16)

                def store(t):
                    n = sp.snap(b * 16 + (8 + t + 3))
                    dst = dr["x1"][bass.ds(b * S + t * P, P), :]
                    sp.wait_ge(e["x_used"], n)
                    sp.dma_start(dst, y[t % 2]).then_inc(e[f"x1_stored{t % 2}"], 16)

                for t in range(NT):
                    load(t, t)
                load(0, 8)
                load(1, 9)
                n = SLOTS // B * P
                sp.dma_start(dr["xs"][bass.ds(b * n, n), :].rearrange("r d -> (r d)").rearrange("(n p f) -> p n f", p=P, f=P),
                             sb["zero"][:].unsqueeze(1).to_broadcast([P, n * D // (P * P), P])).then_inc(e["filled"], 16)
                for t in range(NT):
                    store(t)
                    if t + 2 < NT:
                        load(t + 2, 8 + t + 2)
            for u in range(2):
                sp.wait_ge(e[f"x1_stored{u}"], 16 + 16 * B * NT // 2)
            sp.wait_ge(e["filled"], 16 * B)

        @block.gpsimd
        def _(pool):
            with pool.Fori(0, B) as b:
                def queries(gi):
                    for q in range(2):
                        pool.wait_ge(e["qhi_made"], gi * 2 + (q + 1))
                        pool.tensor_tensor(qst[:, :, 1, :], qn, qst[:, :, 0, :].bitcast(F32), ALU.subtract).then_inc(e["qst_made"], 1)

                def group(g, more):
                    gi = b * NG + g
                    m0 = pool.snap(gi * G)

                    def null_part(hh):
                        if hh == 0:
                            pool.wait_ge(e["pn_made"], gi + 1)
                        pool.wait_ge(e["num_made"], m0 + (hh + 2))
                        pool.tensor_tensor(nul, pn[:, :, hh:hh + 1].to_broadcast([P, NT, VW]),
                                           sb["vnull"][:].unsqueeze(1).to_broadcast([P, NT, VW]), ALU.mult)\
                            .then_inc(e["nul_made"], 1)

                    def scale(hh):
                        dst = AO[:, :, bass.ds((g * G + hh) * DH, DH)]
                        pool.wait_ge(e["rec_made"], m0 + (hh + 1))
                        pool.tensor_tensor(dst, num[hh % 2][:, :, 0:DH],
                                           rec[hh % 2].unsqueeze(2).to_broadcast([P, NT, DH]), ALU.mult)\
                            .then_inc(e["ao_made"], 1)

                    null_part(0)
                    if more:
                        queries(gi + 1)
                    null_part(1)
                    scale(0)
                    scale(1)

                queries(b * NG)
                with pool.Fori(0, NG // 2 - 1) as p2:
                    group(p2 * 2, True)
                    group(p2 * 2 + 1, True)
                group(NG - 2, True)
                group(NG - 1, False)

        @block.scalar
        def _(act):
            act.preload_act_table_set("natural_log_exp_and_others")
            with act.Fori(0, B) as b:
                n0 = act.snap(b * NT)
                chA = Chain(act, sa[0])
                chA.base = b * CH_A_A

                def y0s(t):
                    act.wait_ge(e["var_ready"], n0 + (t + 1))
                    chA.link(act.activation(lv[:, t:t + 1], ve[:, t:t + 1], ACT.Ln))
                    act.activation(y0[:, t:t + 1], lv[:, t:t + 1], ACT.Exp, scale=-0.5).then_inc(e["y0_ready"], 1)

                def xTc(t):
                    act.wait_ge(e["xT_made"], n0 + (t + 3))
                    act.activation(xnT[:, :, t * P:(t + 1) * P],
                                   psS[t % 2][:, 0, :].rearrange("p (k t) -> p k t", t=P), ACT.Copy)\
                        .then_inc(e["xT_copied"], 1)

                def sqk(t):
                    act.wait_ge(e["kv_made"], n0 + (t + 1))
                    act.activation(ksq[t % 2], psS[t % 2][:, 1, 0:DH], ACT.Square, accum_out=ssk[:, t:t + 1])\
                        .then_inc(e["ssk_made"], 1)

                def yks(t):
                    act.wait_ge(e["ssk_clamped"], n0 + (t + 1))
                    chA.link(act.activation(lk[:, t:t + 1], ssc[:, t:t + 1], ACT.Ln, scale=float(2 ** LIFT)))
                    act.activation(yk[:, t:t + 1], lk[:, t:t + 1], ACT.Exp, scale=-0.5).then_inc(e["yk_ready"], 1)

                def kTc(t):
                    act.wait_ge(e["kT_made"], n0 + (t + 3))
                    act.activation(KT[:, :, t * P:(t + 1) * P],
                                   psO[t % 2][:, 0, 0:256].rearrange("p (s t) -> p s t", t=P), ACT.Copy)\
                        .then_inc(e["kT_copied"], 1)

                skewed(dict(y0=y0s, xTc=xTc, sq=sqk, yk=yks, kTc=kTc), A_LAG, NT)
                assert chA.n == CH_A_A, chA.n

                def steps_of(gi, par):
                    m = act.snap(gi * 2)
                    m2 = act.snap(gi * 4)
                    ch = Chain(act, sa[1])
                    ch.base = gi * CH_G_A

                    def sqq(q):
                        act.wait_ge(e["q_made"], m + (q + 1))
                        act.wait_ge(e["qst_made"], m + (q + 2))
                        act.activation(qn.rearrange("p n d -> p (n d)"), psO[1][:, q, :], ACT.Square)\
                            .then_inc(e["sq_made"], 1)

                    def yqs(q):
                        w = slice(q * 8, q * 8 + 8)
                        act.wait_ge(e["ssq_made"], m + (q + 1))
                        ch.link(act.activation(lq[:, w], ssq[:, w], ACT.Ln, scale=float(2 ** LIFT)))
                        act.activation(yq[:, w], lq[:, w], ACT.Exp, scale=-0.5).then_inc(e["yq_made"], 1)

                    def hi(q):
                        act.wait_ge(e["qn_made"], m + (q + 1))
                        act.wait_ge(e["qT_made"], m2 + (2 * q + 2))
                        act.activation(qst[:, :, 0, :], qn, ACT.Copy).then_inc(e["qhi_made"], 1)

                    def cpq(q):
                        act.wait_ge(e["qT_made"], m2 + (2 * q + 3))
                        act.activation(QT[:, par, :, 4 * q * P:(4 * q + 2) * P],
                                       psO[1][:, q, :].rearrange("p (h t) -> p h t", h=G), ACT.Copy)\
                            .then_inc(e["qTa_copied"], 1)

                    return dict(sq=sqq, y=yqs, hi=hi, cp=cpq)

                def group(g, par, more):
                    gi = b * NG + g
                    f0 = act.snap(gi * (G * NF))
                    steps = steps_of(gi + 1, 1 - par) if more else None
                    act.wait_ge(e["nz_made"], gi + 1)
                    act.activation(pe_, pz, ACT.Exp, bias=sb["negc"][:]).then_inc(e["nexp_made"], 1)
                    for f in range(G * NF):
                        n = fill_width(f % NF)
                        act.wait_ge(e["s_made"], f0 + (f + 1))
                        act.wait_ge(e["pv_made"], f0 + max(f, 2))
                        act.activation(E[f % 3][:, 0:n], psS[f % 2][:].rearrange("p a n -> p (a n)")[:, 0:n], ACT.Exp,
                                       bias=sb["negc"][:]).then_inc(e["exp_made"], 1)
                        if more:
                            beside(ACT_Q, f, steps)

                first = steps_of(b * NG, 0)
                for n, q in (("sq", 0), ("y", 0), ("hi", 0), ("sq", 1), ("cp", 0), ("y", 1), ("hi", 1), ("cp", 1)):
                    first[n](q)
                with act.Fori(0, NG // 2 - 1) as p2:
                    group(p2 * 2, 0, True)
                    group(p2 * 2 + 1, 1, True)
                group(NG - 2, 0, True)
                group(NG - 1, 1, False)
                chD = Chain(act, sa[2])
                chD.base = b * CH_D_A

                def cpa(t):
                    act.wait_ge(e["aT_made"], n0 + (t + 3))
                    act.wait_ge(e["y_made"], n0 + (t + 1))
                    act.activation(AOT[t % 2][:, 0:4, :].rearrange("p k t -> p (k t)"), psS[t % 2][:, 0, :], ACT.Copy)\
                        .then_inc(e["aTa_copied"], 1)

                def y0d(t):
                    act.wait_ge(e["var2_ready"], n0 + (t + 1))
                    chD.link(act.activation(lv[:, t:t + 1], ve[:, t:t + 1], ACT.Ln))
                    act.activation(y0[:, t:t + 1], lv[:, t:t + 1], ACT.Exp, scale=-0.5).then_inc(e["y02_ready"], 1)

                def x1Tc(t):
                    act.wait_ge(e["x1T_made"], n0 + (t + 3))
                    act.wait_ge(e["lg_made"], n0 + (t + 1))
                    act.activation(x1T[t % 2].rearrange("p k t -> p (k t)"), psO[t % 2][:, 1, :], ACT.Copy)\
                        .then_inc(e["x1T_copied"], 1)

                skewed(dict(cp=cpa, y0=y0d, x1Tc=x1Tc), D_LAG, NT)
                assert chD.n == CH_D_A, chD.n

        @block.tensor
        def _(pe):
            W, Wo = sb["W"], sb["Wo"]
            with pe.Fori(0, B) as b:
                n0 = pe.snap(b * NT)
                xb = pe.snap(b * 16)

                def T(t):
                    pe.wait_ge(e["x_used"], xb + (t + 3))
                    pe.wait_ge(e["xT_copied"], n0 + (t + 1))
                    for k in range(KD):
                        ins = pe.transpose(psS[t % 2][:, 0, k * P:(k + 1) * P], xn[t % 2][:, k * P:(k + 1) * P], ident[:])
                    ins.then_inc(e["xT_made"], 1)

                def kv(t):
                    pe.wait_ge(e["xT_copied"], n0 + (t + 3))
                    pe.wait_ge(e["kv_used"], n0 + (t + 1))
                    for k in range(KD):
                        ins = pe.matmul(psS[t % 2][:, 1, 0:2 * DH + H], xnT[:, k, t * P:(t + 1) * P], W[:, k, KVC:],
                                        start=(k == 0), stop=(k == KD - 1))
                    ins.then_inc(e["kv_made"], 1)

                def kT(t):
                    pe.wait_ge(e["kst_made"], n0 + (t + 1))
                    pe.wait_ge(e["kT_copied"], n0 + (t + 1))
                    for s in range(2):
                        ins = pe.matmul(psO[t % 2][:, 0, s * P:(s + 1) * P],
                                        kst[t % 2][:, s].rearrange("p r d -> p (r d)"), identr[:], start=True, stop=True)
                    ins.then_inc(e["kT_made"], 1)

                skewed(dict(T=T, kv=kv, kT=kT), A_LAG, NT)
                pe.wait_ge(e["kv_used"], n0 + (NT + 2))
                pe.wait_ge(e["kT_copied"], n0 + (NT + 2))

                def steps_of(gi, g):
                    m = pe.snap(gi * 2)
                    cols = bass.ds(g * (G * DH), G * DH)

                    def Q(t):
                        q, i = t // 4, t % 4
                        if i == 0:
                            pe.wait_ge(e["qTa_copied"], m + (q + 1))
                            pe.wait_ge(e["qTv_copied"], m + (q + 1))
                        for k in range(KD):
                            ins = pe.matmul(psO[1][:, q, i * P:(i + 1) * P], xnT[:, k, t * P:(t + 1) * P],
                                            W[:, k, cols], start=(k == 0), stop=(k == KD - 1))
                        if i == 3:
                            ins.then_inc(e["q_made"], 1)

                    def TQ(n):
                        q, half = n // 2, n % 2
                        if half == 0:
                            pe.wait_ge(e["qst_made"], m + (q + 3))
                        else:
                            pe.wait_ge(e["qTa_copied"], m + (q + 3))
                        for i in range(2):
                            for h in range(G):
                                ins = pe.matmul(psO[1][:, q, (h * 2 + i) * P:(h * 2 + i + 1) * P],
                                                qst[:, (half * 2 + i) * G + h].rearrange("p s d -> p (s d)"),
                                                identr[:], start=True, stop=True)
                        ins.then_inc(e["qT_made"], 1)

                    return dict(Q=Q, T=TQ)

                def group(g, par, more):
                    gi = b * NG + g
                    m0 = pe.snap(gi * G)
                    f0 = pe.snap(gi * (G * NF))
                    steps = steps_of(gi + 1, g + 1) if more else None
                    pe.wait_ge(e["qTa_copied"], m0 + 4)
                    pe.wait_ge(e["qTv_copied"], m0 + 4)

                    def scores(f):
                        hh, k = f // NF, f % NF
                        pe.wait_ge(e["exp_made"], f0 + (f + 1))
                        for j, c0 in FILLS[k]:
                            w, at = width(j), 0
                            while at < w:
                                m = min(w - at, 512 - (c0 + at) % 512)
                                bank, off = (c0 + at) // 512, (c0 + at) % 512
                                for s in range(2):
                                    ins = pe.matmul(psS[f % 2][:, bank, off:off + m], KT[:, s, j * P:(j + 1) * P],
                                                    QT[:, par, hh, j * P + at:j * P + at + m],
                                                    start=(s == 0), stop=(s == 1))
                                at += m
                        ins.then_inc(e["s_made"], 1)

                    def values(f):
                        hh, k = f // NF, f % NF
                        pe.wait_ge(e["p_made"], f0 + (f + 1))
                        if k == 0:
                            pe.wait_ge(e["num_made"], m0 + (hh + 2))
                        for j, c0 in FILLS[k]:
                            for i in range(j, NT):
                                ins = pe.matmul(psO[0][:, i // 4, (i % 4) * VW:(i % 4 + 1) * VW],
                                                E[f % 3][:, c0 + (i - j) * P:c0 + (i - j + 1) * P], V[:, j, :],
                                                start=(j == 0 and i % 4 == 0), stop=(k == NF - 1),
                                                skip_group_check=True)
                        ins.then_inc(e["pv_made"], 1)

                    for f in range(G * NF + 2):
                        if f < G * NF:
                            scores(f)
                        if more:
                            beside(PE_Q, f, steps)
                        if f >= 2:
                            values(f - 2)

                first = steps_of(b * NG, 0)
                for t in range(NT):
                    first["Q"](t)
                for n in range(4):
                    first["T"](n)
                with pe.Fori(0, NG // 2 - 1) as p2:
                    group(p2 * 2, 0, True)
                    group(p2 * 2 + 1, 1, True)
                group(NG - 2, 0, True)
                group(NG - 1, 1, False)
                pe.wait_ge(e["ao_made"], b * H + (H + 2))

                def TA(t):
                    pe.wait_ge(e["aTa_copied"], n0 + (t + 1))
                    pe.wait_ge(e["aTv_copied"], n0 + (t + 1))
                    for k in range(8):
                        ins = pe.transpose(psS[t % 2][:, k // 4, (k % 4) * P:(k % 4 + 1) * P],
                                           AO[:, t, k * P:(k + 1) * P], ident[:])
                    ins.then_inc(e["aT_made"], 1)

                def Y(t):
                    pe.wait_ge(e["aTa_copied"], n0 + (t + 3))
                    pe.wait_ge(e["aTv_copied"], n0 + (t + 3))
                    if t >= 2:
                        pe.wait_ge(e["x_used"], xb + (8 + t + 1))
                    for k in range(8):
                        ins = pe.matmul(psO[t % 2][:, 0, :], AOT[t % 2][:, k, :], Wo[:, k, :],
                                        start=(k == 0), stop=(k == 7))
                    ins.then_inc(e["y_made"], 1)

                def T1(t):
                    pe.wait_ge(e["x_used"], xb + (8 + t + 3))
                    pe.wait_ge(e["lg_used"], n0 + (t + 1))
                    for k in range(KD):
                        ins = pe.transpose(psO[t % 2][:, 1, k * P:(k + 1) * P], y[t % 2][:, k * P:(k + 1) * P], ident[:])
                    ins.then_inc(e["x1T_made"], 1)

                def lg(t):
                    pe.wait_ge(e["x1T_copied"], n0 + (t + 3))
                    for k in range(KD):
                        ins = pe.matmul(psO[t % 2][:, 1, 0:NE], x1T[t % 2][:, k, :], sb["wtT"][:, k, :],
                                        start=(k == 0), stop=(k == KD - 1))
                    ins.then_inc(e["lg_made"], 1)

                skewed(dict(TA=TA, Y=Y, T1=T1, lg=lg), D_LAG, NT)

        @block.vector
        def _(dve):
            with dve.Fori(0, B) as b:
                n0 = dve.snap(b * NT)
                ch = Chain(dve, sv[0])
                ch.base = b * CH_A_V

                def stats(t):
                    u = t % 2
                    dve.wait_ge(e[f"x_in{u}"], b * 128 + 16 * (t // 2 + 1))
                    ch.link(dve.bn_stats(st[u], xt[:, u, :]))
                    dve.memset(idle, 0.0)
                    ch.link(dve.bn_aggr(mv[u], st[u]))
                    dve.tensor_scalar(ve[:, t:t + 1], mv[u][:, 1:2], LN_EPS, None, ALU.add).then_inc(e["var_ready"], 1)

                def xns(t):
                    u = t % 2
                    dve.wait_ge(e["var_ready"], n0 + (t + 1))
                    dve.wait_ge(e["y0_ready"], n0 + (t + 1))
                    ch.link(newton(dve, ch, rs[:, t:t + 1], y0[:, t:t + 1], ve[:, t:t + 1], nt[:, t:t + 1], 1.0))
                    dve.wait_ge(e["xT_made"], n0 + (t + 1))
                    dve.tensor_scalar(xn[u], xt[:, u, :], mv[u][:, 0:1], rs[:, t:t + 1], ALU.subtract, ALU.mult)\
                        .then_inc(e["x_used"], 1)

                def ck(t):
                    dve.wait_ge(e["ssk_made"], n0 + (t + 1))
                    dve.tensor_scalar(ssc[:, t:t + 1], ssk[:, t:t + 1], NORM_EPS ** 2, None, ALU.max)\
                        .then_inc(e["ssk_clamped"], 1)

                def kst_(t):
                    u = t % 2
                    pkv = psS[u][:, 1, :]
                    mask = sb["maskf"][:, bass.ds(n0 + t, 1)]
                    dve.wait_ge(e["ssk_clamped"], n0 + (t + 1))
                    dve.wait_ge(e["yk_ready"], n0 + (t + 1))
                    ch.link(newton(dve, ch, rk[:, t:t + 1], yk[:, t:t + 1], ssc[:, t:t + 1], nt[:, t:t + 1],
                                   float(2 ** (LIFT // 2))))
                    ch.link(dve.scalar_tensor_tensor(out=knr[u], in0=pkv[:, 0:DH], scalar=rk[:, t:t + 1],
                                                     in1=sb["kfac"][:], op0=ALU.mult, op1=ALU.mult))
                    kb = knr[u].unsqueeze(1).to_broadcast([P, 2, DH])
                    dve.wait_ge(e["kT_made"], n0 + (t + 1))
                    ch.link(dve.tensor_copy(kst[u][:, 0], kb))
                    dve.tensor_tensor(kst[u][:, 1], kb, kst[u][:, 0].bitcast(F32), ALU.subtract).then_inc(e["kst_made"], 1)
                    dve.tensor_scalar(V[:, t, 0:DH], pkv[:, DH:2 * DH], mask, None, ALU.mult)
                    dve.tensor_copy(V[:, t, DH:VW], mask)
                    dve.tensor_copy(snull[:, t, :], pkv[:, 2 * DH:2 * DH + H]).then_inc(e["kv_used"], 1)

                skewed(dict(stats=stats, xn=xns, ck=ck, k=kst_), A_LAG, NT)
                assert ch.n == CH_A_V, ch.n

                def steps_of(gi, par):
                    m = dve.snap(gi * 2)
                    m2 = dve.snap(gi * 4)
                    cg = Chain(dve, sv[1])
                    cg.base = gi * CH_G_V

                    def red(q):
                        w = slice(q * 8, q * 8 + 8)
                        dve.wait_ge(e["sq_made"], m + (q + 1))
                        cg.link(dve.tensor_reduce(ssq[:, w], qn, AX.X, ALU.add))
                        dve.tensor_scalar(ssq[:, w], ssq[:, w], NORM_EPS ** 2, None, ALU.max).then_inc(e["ssq_made"], 1)

                    def qns(q):
                        w = slice(q * 8, q * 8 + 8)
                        dve.wait_ge(e["ssq_made"], m + (q + 1))
                        dve.wait_ge(e["yq_made"], m + (q + 1))
                        cg.link(newton(dve, cg, rq[:, w], yq[:, w], ssq[:, w], nq, float(2 ** (LIFT // 2))))
                        dve.tensor_tensor(qn, psO[1][:, q, :].rearrange("p (n d) -> p n d", d=DH),
                                          rq[:, w].unsqueeze(2).to_broadcast([P, 8, DH]), ALU.mult)\
                            .then_inc(e["qn_made"], 1)

                    def cpq(q):
                        dve.wait_ge(e["qT_made"], m2 + (2 * q + 4))
                        dve.tensor_copy(QT[:, par, :, (4 * q + 2) * P:(4 * q + 4) * P],
                                        psO[1][:, q, :].rearrange("p (h t) -> p h t", h=G))\
                            .then_inc(e["qTv_copied"], 1)

                    return dict(red=red, qn=qns, cp=cpq)

                def group(g, par, more):
                    gi = b * NG + g
                    m0 = dve.snap(gi * G)
                    f0 = dve.snap(gi * (G * NF))
                    steps = steps_of(gi + 1, 1 - par) if more else None
                    dve.tensor_tensor(pz, snull[:, :, bass.ds(g * G, G)], rq.rearrange("p (t h) -> p t h", h=G),
                                      ALU.mult).then_inc(e["nz_made"], 1)

                    def weigh(f):
                        hh, k = f // NF, f % NF
                        dve.wait_ge(e["exp_made"], f0 + (f + 3))
                        for j, c0 in FILLS[k]:
                            w = width(j)
                            ins = dve.tensor_tensor(E[f % 3][:, c0:c0 + w], E[f % 3][:, c0:c0 + w],
                                                    sb["EB"][:, bass.ds(g * G + hh, 1), 0:w].rearrange("p a w -> p (a w)"),
                                                    ALU.mult)
                        ins.then_inc(e["p_made"], 1)

                    def total(hh):
                        u = hh % 2
                        dve.wait_ge(e["pv_made"], f0 + (hh * NF + NF + 2))
                        dve.wait_ge(e["nul_made"], m0 + (hh + 1))
                        dve.wait_ge(e["ao_made"], m0 + (hh + 1))
                        for i in range(2):
                            ins = dve.tensor_tensor(num[u][:, 4 * i:4 * i + 4, :],
                                                    psO[0][:, i, 0:4 * VW].rearrange("p (t d) -> p t d", d=VW),
                                                    nul[:, 4 * i:4 * i + 4, :], ALU.add)
                        ins.then_inc(e["num_made"], 1)
                        dve.wait_ge(e["num_made"], m0 + (hh + 3))
                        dve.reciprocal(rec[u].unsqueeze(2), num[u][:, :, DH:VW]).then_inc(e["rec_made"], 1)

                    for f in range(G * NF):
                        weigh(f)
                        if f == 0:
                            dve.wait_ge(e["nexp_made"], gi + 1)
                            dve.tensor_tensor(pn, pe_, sb["enull"][:, bass.ds(g * G, G)].unsqueeze(1)
                                              .to_broadcast([P, NT, G]), ALU.mult).then_inc(e["pn_made"], 1)
                        if f == NF:
                            total(0)
                        if more:
                            beside(DVE_Q, f, steps)
                    total(1)

                first = steps_of(b * NG, 0)
                for n, q in (("red", 0), ("qn", 0), ("red", 1), ("cp", 0), ("qn", 1), ("cp", 1)):
                    first[n](q)
                with dve.Fori(0, NG // 2 - 1) as p2:
                    group(p2 * 2, 0, True)
                    group(p2 * 2 + 1, 1, True)
                group(NG - 2, 0, True)
                group(NG - 1, 1, False)
                cd = Chain(dve, sv[2])
                cd.base = b * CH_D_V

                def cpa(t):
                    dve.wait_ge(e["aT_made"], n0 + (t + 3))
                    dve.wait_ge(e["y_made"], n0 + (t + 1))
                    dve.tensor_copy(AOT[t % 2][:, 4:8, :].rearrange("p k t -> p (k t)"), psS[t % 2][:, 1, :])\
                        .then_inc(e["aTv_copied"], 1)

                def std(t):
                    u = t % 2
                    dve.wait_ge(e["y_made"], n0 + (t + 3))
                    cd.link(dve.bn_stats(st[u], psO[u][:, 0, :]))
                    dve.memset(idle, 0.0)
                    cd.link(dve.bn_aggr(mv[u], st[u]))
                    dve.tensor_scalar(ve[:, t:t + 1], mv[u][:, 1:2], LN_EPS, None, ALU.add).then_inc(e["var2_ready"], 1)

                def nrm(t):
                    u = t % 2
                    dve.wait_ge(e["var2_ready"], n0 + (t + 1))
                    dve.wait_ge(e["y02_ready"], n0 + (t + 1))
                    cd.link(newton(dve, cd, rs[:, t:t + 1], y0[:, t:t + 1], ve[:, t:t + 1], nt[:, t:t + 1], 1.0))
                    dve.wait_ge(e[f"x1_stored{u}"], b * 64 + 16 * (t // 2 + 1))
                    dve.wait_ge(e["x1T_made"], n0 + (t + 1))
                    cd.link(dve.tensor_scalar(y[u], psO[u][:, 0, :], mv[u][:, 0:1], rs[:, t:t + 1], ALU.subtract, ALU.mult))
                    cd.link(dve.tensor_tensor(y[u], y[u], sb["gout"][:], ALU.mult))
                    dve.wait_ge(e[f"x_in{u}"], b * 128 + 16 * (4 + t // 2 + 1))
                    dve.tensor_tensor(y[u], y[u], xt[:, u, :], ALU.add).then_inc(e["x_used"], 1)

                def lgc(t):
                    dve.wait_ge(e["lg_made"], n0 + (t + 3))
                    dve.tensor_tensor(LG[:, bass.ds(n0 + t, 1), :].rearrange("p a n -> p (a n)"), psO[t % 2][:, 1, 0:NE],
                                      sb["glog"][:, bass.ds(b, 1), :].rearrange("p a n -> p (a n)"), ALU.add)\
                        .then_inc(e["lg_used"], 1)

                skewed(dict(cp=cpa, st=std, nrm=nrm, lgc=lgc), D_LAG, NT)
                assert cd.n == CH_D_V, cd.n


def pipelined(eng, steps, lags, count, unroll):
    order = sorted(steps, key=lambda n: -lags[n])
    deep = max(lags.values())
    head = -(-deep // unroll) * unroll

    def round_(i, r):
        for n in order:
            if isinstance(i, int) and not 0 <= i - lags[n] < count:
                continue
            steps[n](i - lags[n], (r - lags[n]) % unroll)

    for i in range(head):
        round_(i, i)
    with eng.Fori(head // unroll, count // unroll) as q:
        for r in range(unroll):
            round_(q * unroll + r, r)
    for i in range(count, count + deep):
        round_(i, i)


def value(eng, x):
    return x if isinstance(x, int) else eng.snap(x)


MOE_CREDITS = dict(xT_made=2, xT_copied=2, g_used=2, hT_made=2, h_copied=1, dn_made=2, yo_made=4, noted=1)


def experts(nc, a, sb, dr, sem, out):
    LG = sb["LG"]
    with ExitStack() as ctx:
        def tile(name, shape, dt=F32):
            return ctx.enter_context(nc.sbuf_tensor("m_" + name, shape, dt))

        def psum(name):
            return ctx.enter_context(nc.psum_tensor("m_" + name, [P, 512], F32))

        wgu = tile("wgu", [P, NE, KD, 2 * MD])
        wd = tile("wd", [P, NE, MD // P, D])
        sgu = tile("sgu", [P, KD, 2 * SMD])
        sd = tile("sd", [P, SMD // P, D])
        ident = tile("ident", [P, P])
        upper = tile("upper", [P, P])
        ones = tile("ones", [P, P])
        xr = tile("xr", [P, 4, D])
        xT = tile("xT", [P, 2, KD, P])
        tl = tile("tl", [P, 2, SMD])
        lh = tile("lh", [P, 2, SMD])
        hT = tile("hT", [P, 2, SMD // P, P])
        yo = tile("yo", [P, 2, D])
        xq = tile("xq", [P, 4, D])
        xe = tile("xe", [P, 2, D])
        y1, y2, z1, z2 = (tile(n, [P, 4, D]) for n in ("y1", "y2", "z1", "z2"))
        psA = [psum(f"A{i}") for i in range(2)]
        psG = [psum(f"G{i}") for i in range(2)]
        psU = [psum(f"U{i}") for i in range(2)]
        psH, psY = psum("H"), psum("Y")

        z = tile("z", [P, NTT, NE])
        t8 = tile("t8", [P, NTT, NE])
        ix = tile("ix", [P, NTT, NE], U32)
        ixf = tile("ixf", [P, NTT, 2])
        o1 = tile("o1", [P, NTT, NE])
        o2 = tile("o2", [P, NTT, NE])
        cnt = tile("cnt", [P, NTT, NE])
        tot = tile("tot", [P, NTT, NE])
        inc = tile("inc", [P, NTT, NE])
        col = tile("col", [P, NTT, 2])
        wts = tile("wts", [P, NTT, 2])
        i8 = tile("i8", [P, NE])
        pad = tile("pad", [P, NE])
        padi = tile("padi", [P, NE], I32)
        end = tile("end", [P, NE])
        first = tile("first", [P, NE])
        slot = tile("slot", [P, SLOTS])
        ge = tile("ge", [P, SLOTS, NE])
        sle = tile("sle", [P, SLOTS])
        slei = tile("slei", [P, SLOTS], I32)
        posu = tile("posu", [P, NTT, 2], U32)
        ib = tile("ib", [P, 4, 2, 2], U32)
        gb = tile("gb", [P, 4, 2, 2], U32)
        note = tile("note", [P, 1])

        c = {n: sem("m_" + n) for n in MOE_CREDITS}
        names = ("rv", "ez", "consts", "cnt_made", "pre_made", "pos_made", "w_shared",
                 "w_exp", "gu_made", "t_made", "l_made", "ib_made", "gb_made", "sum_made", "half_made",
                 "fin_half", "fin_made")
        e = {n: sem("m_" + n) for n in names}
        x_in, q_in, z_in = ([sem(f"m_{n}_in{i}") for i in range(4)] for n in "xqz")
        scat = [sem(f"m_scat{i}") for i in range(4)]
        y_st = [sem(f"m_y_st{i}") for i in range(2)]
        s_in = [sem(f"m_s_in{i}") for i in range(2)]
        y_out = [sem(f"m_y_out{i}") for i in range(2)]
        b_in = [sem(f"m_b_in{i}") for i in range(4)]
        g_in = [sem(f"m_g_in{i}") for i in range(4)]
        o_out = [sem(f"m_o_out{i}") for i in range(4)]
        block = ctx.enter_context(nc.Block())

        def rows(ap, i):
            return ap[bass.ds(i * P, P), :]

        x1, base, xs, ys, o = dr["x1"], dr["base"], dr["xs"], dr["ys"], out

        LAG = dict(load=0, scat=0, T=0, xTc=0, gu=1, tl=1, lh=1, T2=2, hTc=2, dn=3, yc=3, store=4, gind=0, tot=3)

        @block.sync
        def _(sp):
            sp.dma_start(sgu[:, :, 0:SMD], a["sw_gate"].rearrange("(k p) n -> p k n", p=P)).then_inc(e["w_shared"], 16)
            sp.dma_start(sgu[:, :, SMD:], a["sw_up"].rearrange("(k p) n -> p k n", p=P)).then_inc(e["w_shared"], 16)
            sp.dma_start(sd[:], a["sw_down"].rearrange("(k p) n -> p k n", p=P)).then_inc(e["w_shared"], 16)

            def load(i, r):
                src, src2 = rows(x1, i), rows(x1, i + NS)
                n, m = value(sp, (i - r) * 16), value(sp, i + 1)
                if not isinstance(n, int) or n > 0:
                    sp.wait_ge(scat[r], n)
                sp.dma_start(xq[:, r, :], src2).then_inc(q_in[r], 16)
                sp.wait_ge(c["yo_made"], m)
                sp.dma_start(xr[:, r, :], src).then_inc(x_in[r], 16)

            def store(i, r):
                dst = rows(base, i)
                n = value(sp, i + 5)
                sp.wait_ge(c["yo_made"], n)
                sp.dma_start(dst, yo[:, r % 2, :]).then_inc(y_st[r % 2], 16)

            pipelined(sp, dict(load=load, store=store), LAG, NS, 4)

            for r in range(4):
                sp.wait_ge(scat[r], 64 * (NS // 4))

            def loads(i, r):
                src = rows(xs, i)
                n = value(sp, i + (NS + 1))
                sp.wait_ge(c["xT_made"], n)
                sp.dma_start(xe[:, r % 2, :], src).then_inc(s_in[r % 2], 16)

            def stores(i, r):
                dst = rows(ys, i)
                n = value(sp, i + (NS + 5))
                sp.wait_ge(c["yo_made"], n)
                sp.dma_start(dst, yo[:, r % 2, :]).then_inc(y_out[r % 2], 16)

            pipelined(sp, dict(load=loads, store=stores), LAG, SLOTS, 2)
            for r in range(2):
                sp.wait_ge(y_st[r], 16 * (NS // 2 + 1))

            def last_loads(i, r):
                src, src2 = rows(x1, i + NS), rows(base, i)
                n, m = value(sp, i + (NS + SLOTS)), value(sp, (i - r) * 4 + 16)
                if not isinstance(i, int) or i >= 4:
                    sp.wait_ge(c["yo_made"], n)
                sp.dma_start(xr[:, r, :], src).then_inc(x_in[r], 16)
                sp.wait_ge(o_out[r], m)
                sp.dma_start(xq[:, r, :], src2).then_inc(b_in[r], 16)

            def last_stores(i, r):
                dst, dst2 = rows(o, i + NS), rows(o, i)
                n = value(sp, i + 1)
                sp.wait_ge(e["fin_made"], n)
                sp.dma_start(dst, yo[:, r % 2, :]).then_inc(y_st[r % 2], 16)
                sp.wait_ge(e["sum_made"], n)
                sp.dma_start(dst2, xq[:, r, :]).then_inc(o_out[r], 16)

            pipelined(sp, dict(load=last_loads, store=last_stores), LAG, NS, 4)
            for r in range(2):
                sp.wait_ge(y_st[r], 16 * (NS + 1))
            for r in range(4):
                sp.wait_ge(o_out[r], 16 * (NS // 4 + 1))

        @block.gpsimd
        def _(pool):
            col_ = 0
            for name, n in MOE_CREDITS.items():
                pool.memset(sb["credit"][:, col_:col_ + 1], 0.0).then_inc(c[name], n)
                col_ += 1
            for q in y_st + y_out + o_out:
                pool.memset(sb["credit"][:, col_:col_ + 1], 0.0).then_inc(q, 16)
                col_ += 1
            pool.memset(ident[:], 0.0).then_inc(e["consts"], 1)
            pool.memset(upper[:], 1.0).then_inc(e["consts"], 1)
            pool.memset(ones[:], 1.0).then_inc(e["consts"], 1)
            pool.wait_ge(e["consts"], 3)
            pool.affine_select(out=ident[:], in_=ident[:], compare_op=ALU.not_equal, fill=1.0, base=0,
                               pattern=[[-1, P]], channel_multiplier=1).then_inc(e["consts"], 1)
            pool.affine_select(out=upper[:], in_=upper[:], compare_op=ALU.is_gt, fill=0.0, base=0,
                               pattern=[[1, P]], channel_multiplier=-1).then_inc(e["consts"], 1)
            pool.iota(i8[:], [[1, NE]], base=0, channel_multiplier=0,
                      allow_small_or_imprecise_dtypes=True).then_inc(e["consts"], 1)
            pool.iota(slot[:], [[P, SLOTS]], base=0, channel_multiplier=0,
                      allow_small_or_imprecise_dtypes=True).then_inc(e["consts"], 1)
            for k in range(NE):
                pool.dma_start(wgu[:, k, :, 0:MD], a["w_gate"][k].rearrange("(k p) n -> p k n", p=P)).then_inc(e["w_exp"], 16)
                pool.dma_start(wgu[:, k, :, MD:], a["w_up"][k].rearrange("(k p) n -> p k n", p=P)).then_inc(e["w_exp"], 16)
                pool.dma_start(wd[:, k], a["w_down"][k].rearrange("(k p) n -> p k n", p=P)).then_inc(e["w_exp"], 16)

            def held(n):
                pool.wait_ge(c["noted"], n + 1)
                pool.tensor_tensor(note[:], ones[:, 0:1], ones[:, 0:1], ALU.add).then_inc(c["noted"], 1)

            def scatter(i, r):
                pool.wait_ge(x_in[r], (i - r) * 4 + 16)
                pool.wait_ge(q_in[r], (i - r) * 4 + 16)
                pool.wait_ge(e["ib_made"], i + 1)
                held(i)
                for h, x in enumerate((xr, xq)):
                    for w in range(2):
                        pool.indirect_dma_start(out=xs, in_=x[:, r, :], in_offset=None, out_offset=bass
                                                .IndirectOffsetOnAxis(ap=ib[:, r, h, w:w + 1], axis=0))\
                            .then_inc(scat[r], 16)

            pipelined(pool, dict(scat=scatter), dict(scat=0), NS, 4)
            for r in range(2):
                pool.wait_ge(y_out[r], 16 * (SLOTS // 2 + 1))

            def gather(i, r):
                pool.wait_ge(e["gb_made"], i + 1)
                held(i + NS)
                for h, ys_, q in ((0, (z1, z2), z_in), (1, (y1, y2), g_in)):
                    for w, y in enumerate(ys_):
                        pool.indirect_dma_start(out=y[:, r, :], out_offset=None, in_=ys, in_offset=bass
                                                .IndirectOffsetOnAxis(ap=gb[:, r, h, w:w + 1], axis=0))\
                            .then_inc(q[r], 16)

            pipelined(pool, dict(g=gather), dict(g=0), NS, 4)

        @block.scalar
        def _(act):
            act.wait_ge(e["rv"], 2)
            act.activation(z[:], z[:], ACT.Exp, scale=0.5).then_inc(e["ez"], 1)

            def stages(off, count, unroll, shared):
                n = SMD if shared else MD

                def xTc(i, r):
                    act.wait_ge(c["xT_made"], i + (off + 3))
                    act.wait_ge(c["g_used"], i + (off + 1))
                    act.activation(xT[:, r % 2].rearrange("p k t -> p (k t)"), psA[r % 2][:], ACT.Copy)\
                        .then_inc(c["xT_copied"], 1)

                def tls(i, r):
                    act.wait_ge(e["gu_made"], i + (off + 1))
                    act.wait_ge(c["g_used"], i + (off + 1))
                    act.activation(tl[:, r % 2, 0:n], psG[r % 2][:, 0:n], ACT.Copy, scale=0.01).then_inc(e["t_made"], 1)

                def yc(i, r):
                    act.wait_ge(c["dn_made"], i + (off + 3))
                    act.wait_ge(y_out[r % 2], (i - r) * 8 + 16 * (1 + r // 2))
                    act.activation(yo[:, r % 2, :], psY[:], ACT.Copy).then_inc(c["yo_made"], 1)

                steps = dict(xTc=xTc, tl=tls)
                if not shared:
                    steps["yc"] = yc
                pipelined(act, steps, LAG, count, unroll)

            stages(0, NS, 4, True)
            for r in range(2):
                act.wait_ge(y_st[r], 16 * (NS // 2 + 1))
            stages(NS, SLOTS, 2, False)
            stages(NS + SLOTS, NS, 4, True)

        @block.tensor
        def _(pe):
            pe.wait_ge(e["consts"], 7)
            pe.wait_ge(e["cnt_made"], 1)
            pe.matmul(psH[:, 0:NTT * NE], upper[:], cnt[:].rearrange("p t e -> p (t e)"), start=True, stop=True)\
              .then_inc(e["pre_made"], 1)
            pe.matmul(psY[:, 0:NTT * NE], ones[:], cnt[:].rearrange("p t e -> p (t e)"), start=True, stop=True)\
              .then_inc(e["pre_made"], 1)
            pe.wait_ge(e["pos_made"], 1)
            pe.wait_ge(e["w_shared"], 48)

            def stages(off, count, unroll, shared):
                kh = (SMD if shared else MD) // P

                def T(i, r):
                    x = xr[:, r, :] if shared else xe[:, r % 2, :]
                    if shared:
                        pe.wait_ge(x_in[r], (i - r) * 4 + (16 + (4 * NS if off else 0)))
                    else:
                        pe.wait_ge(s_in[r % 2], (i - r) * 8 + 16)
                    pe.wait_ge(c["xT_copied"], i + (off + 1))
                    for k in range(KD):
                        ins = pe.transpose(psA[r % 2][:, k * P:(k + 1) * P], x[:, k * P:(k + 1) * P], ident[:])
                    ins.then_inc(c["xT_made"], 1)

                def gu(i, r):
                    u = r % 2
                    pe.wait_ge(c["xT_copied"], i + (off + 3))
                    pe.wait_ge(c["g_used"], i + (off + 1))
                    if shared:
                        for half, ps in enumerate((psG[u], psU[u])):
                            for k in range(KD):
                                ins = pe.matmul(ps[:], xT[:, u, k, :], sgu[:, k, half * SMD:(half + 1) * SMD],
                                                start=(k == 0), stop=(k == KD - 1))
                    else:
                        x = pe.value_load(slei[0:1, bass.ds(i, 1)], min_val=0, max_val=NE - 1)
                        for k in range(KD):
                            ins = pe.matmul(psG[u][:], xT[:, u, k, :],
                                            wgu[:, bass.ds(x, 1), k, :].rearrange("p a n -> p (a n)"),
                                            start=(k == 0), stop=(k == KD - 1))
                    ins.then_inc(e["gu_made"], 1)

                def T2(i, r):
                    u = r % 2
                    pe.wait_ge(c["g_used"], i + (off + 3))
                    pe.wait_ge(c["h_copied"], i + (off + 1))
                    for k in range(kh):
                        ins = pe.transpose(psH[:, k * P:(k + 1) * P], lh[:, u, k * P:(k + 1) * P], ident[:])
                    ins.then_inc(c["hT_made"], 1)

                def dn(i, r):
                    u = r % 2
                    pe.wait_ge(c["h_copied"], i + (off + 2))
                    pe.wait_ge(c["yo_made"], i + (off + 4))
                    if not shared:
                        x = pe.value_load(slei[0:1, bass.ds(i, 1)], min_val=0, max_val=NE - 1)
                    for k in range(kh):
                        w = sd[:, k, :] if shared else wd[:, bass.ds(x, 1), k, :].rearrange("p a n -> p (a n)")
                        ins = pe.matmul(psY[:], hT[:, u, k, :], w, start=(k == 0), stop=(k == kh - 1))
                    ins.then_inc(c["dn_made"], 1)

                pipelined(pe, dict(T=T, gu=gu, T2=T2, dn=dn), LAG, count, unroll)

            stages(0, NS, 4, True)
            pe.wait_ge(e["w_exp"], 48 * NE)
            stages(NS, SLOTS, 2, False)
            stages(NS + SLOTS, NS, 4, True)

        @block.vector
        def _(dve):
            ch = Chain(dve, e["rv"])
            m, s = col[:, :, 0], col[:, :, 1]

            def per_tile(ap):
                return ap.unsqueeze(2).to_broadcast([P, NTT, NE])

            ch.link(dve.tensor_reduce(m, LG[:], AX.X, ALU.max))
            ch.link(dve.tensor_tensor(z[:], LG[:], per_tile(m), ALU.subtract))
            dve.wait_ge(e["ez"], 1)
            ch.link(dve.tensor_reduce(s, z[:], AX.X, ALU.add))
            ch.link(dve.reciprocal(m, s))
            ch.link(dve.tensor_tensor(z[:], z[:], per_tile(m), ALU.mult))
            for t in range(NTT):
                ins = dve.max(t8[:, t, :], z[:, t, :])
            ch.link(ins)
            for t in range(NTT):
                ins = dve.max_index(ix[:, t, :], t8[:, t, :], z[:, t, :])
            ch.link(ins)
            ch.link(dve.tensor_copy(ixf[:], ix[:, :, 0:2]))
            dve.wait_ge(e["consts"], 7)
            e8 = i8[:].unsqueeze(1).to_broadcast([P, NTT, NE])
            for w, oh in enumerate((o1, o2)):
                ins = dve.tensor_tensor(oh[:], per_tile(ixf[:, :, w]), e8, ALU.is_equal)
            ch.link(ins)
            dve.tensor_tensor(cnt[:], o1[:], o2[:], ALU.add).then_inc(e["cnt_made"], 1)
            ch.link(dve.tensor_tensor(s, t8[:, :, 0], t8[:, :, 1], ALU.add))
            ch.link(dve.tensor_scalar(s, s, 1e-20, None, ALU.add))
            ch.link(dve.reciprocal(m, s))
            ch.link(dve.tensor_tensor(wts[:], t8[:, :, 0:2], m.unsqueeze(2).to_broadcast([P, NTT, 2]), ALU.mult))
            dve.wait_ge(e["pre_made"], 2)
            ch.link(dve.tensor_copy(tot[:].rearrange("p t e -> p (t e)"), psY[:, 0:NTT * NE]))
            for x in range(NE):
                ins = dve.tensor_tensor_scan(inc[:, :, x], ones[:, 0:NTT], tot[:, :, x], 0.0, ALU.mult, ALU.add)
            ch.link(ins)
            ch.link(dve.tensor_scalar(pad[:], inc[:, NTT - 1, :], float(P - 1), None, ALU.add))
            ch.link(dve.tensor_copy(padi[:], pad[:]))
            sh = P.bit_length() - 1
            ch.link(dve.tensor_scalar(padi[:], padi[:], sh, sh, ALU.logical_shift_right, ALU.logical_shift_left))
            ch.link(dve.tensor_copy(pad[:], padi[:]))
            ch.link(dve.tensor_tensor_scan(end[:], ones[:, 0:NE], pad[:], 0.0, ALU.mult, ALU.add))
            ch.link(dve.tensor_tensor(first[:], end[:], pad[:], ALU.subtract))
            ch.link(dve.tensor_tensor(inc[:], inc[:], tot[:], ALU.subtract))
            ch.link(dve.tensor_tensor(inc[:], inc[:], first[:].unsqueeze(1).to_broadcast([P, NTT, NE]), ALU.add))
            ch.link(dve.tensor_tensor(inc[:].rearrange("p t e -> p (t e)"), psH[:, 0:NTT * NE],
                                      inc[:].rearrange("p t e -> p (t e)"), ALU.add))
            for w, oh in enumerate((o1, o2)):
                ch.link(dve.tensor_tensor(oh[:], oh[:], inc[:], ALU.mult))
                ch.link(dve.tensor_reduce(ixf[:, :, w], oh[:], AX.X, ALU.add))
            ch.link(dve.tensor_copy(posu[:], ixf[:]))
            ch.link(dve.tensor_tensor(ge[:], slot[:].unsqueeze(2).to_broadcast([P, SLOTS, NE]),
                                      end[:].unsqueeze(1).to_broadcast([P, SLOTS, NE]), ALU.is_ge))
            ch.link(dve.tensor_reduce(sle[:], ge[:], AX.X, ALU.add))
            ch.link(dve.tensor_scalar(sle[:], sle[:], float(NE - 1), None, ALU.min))
            dve.tensor_copy(slei[:], sle[:]).then_inc(e["pos_made"], 1)

            def stages(off, count, unroll, shared):
                n = SMD if shared else MD

                def index(i, r):
                    if not isinstance(i, int) or i >= 4:
                        dve.wait_ge(scat[r], (i - r) * 16)
                    for h in range(2):
                        ins = dve.tensor_copy(ib[:, r, h, :],
                                              posu[:, bass.ds(i + h * NS, 1), :].rearrange("p a w -> p (a w)"))
                    ins.then_inc(e["ib_made"], 1)

                def gindex(i, r):
                    if not isinstance(i, int) or i >= 4:
                        dve.wait_ge(z_in[r], (i - r) * 8)
                        dve.wait_ge(g_in[r], (i - r) * 8)
                    for h in range(2):
                        ins = dve.tensor_copy(gb[:, r, h, :],
                                              posu[:, bass.ds(i + h * NS, 1), :].rearrange("p a w -> p (a w)"))
                    ins.then_inc(e["gb_made"], 1)

                def lhs(i, r):
                    u = r % 2
                    up = psU[u][:, 0:n] if shared else psG[u][:, MD:2 * MD]
                    dve.wait_ge(e["t_made"], i + (off + 1))
                    dve.wait_ge(c["hT_made"], i + (off + 1))
                    dve.tensor_tensor(lh[:, u, 0:n], psG[u][:, 0:n], tl[:, u, 0:n], ALU.max).then_inc(e["l_made"], 1)
                    dve.wait_ge(e["l_made"], i + (off + 1))
                    dve.tensor_tensor(lh[:, u, 0:n], up, lh[:, u, 0:n], ALU.mult).then_inc(c["g_used"], 1)

                def hTc(i, r):
                    dve.wait_ge(c["hT_made"], i + (off + 3))
                    dve.wait_ge(c["dn_made"], i + (off + 1))
                    dve.tensor_copy(hT[:, r % 2].rearrange("p k t -> p (k t)")[:, 0:n], psH[:, 0:n])\
                       .then_inc(c["h_copied"], 1)

                def add(i, r):
                    done = 8 * NS if off else 0
                    dve.wait_ge(c["dn_made"], i + (off + 3))
                    dve.wait_ge(y_st[r % 2], (i - r) * 8 + (16 * (1 + r // 2) + done))
                    dve.tensor_tensor(yo[:, r % 2, :], psY[:], xr[:, r, :], ALU.add).then_inc(c["yo_made"], 1)

                def weighted(x, y, w, half, whole, i):
                    dve.scalar_tensor_tensor(out=x, in0=y[0], scalar=w[:, 0:1], in1=x, op0=ALU.mult, op1=ALU.add)\
                       .then_inc(e[half], 1)
                    dve.wait_ge(e[half], i + 1)
                    dve.scalar_tensor_tensor(out=x, in0=y[1], scalar=w[:, 1:2], in1=x, op0=ALU.mult, op1=ALU.add)\
                       .then_inc(e[whole], 1)

                def last_add(i, r):
                    add(i, r)
                    w = wts[:, bass.ds(i + NS, 1), :].rearrange("p a w -> p (a w)")
                    dve.wait_ge(c["yo_made"], i + (off + 5))
                    dve.wait_ge(g_in[r], (i - r) * 8 + 32)
                    weighted(yo[:, r % 2, :], (y1[:, r, :], y2[:, r, :]), w, "fin_half", "fin_made", i)

                def total(i, r):
                    w = wts[:, bass.ds(i, 1), :].rearrange("p a w -> p (a w)")
                    dve.wait_ge(b_in[r], (i - r) * 4 + 16)
                    dve.wait_ge(z_in[r], (i - r) * 8 + 32)
                    weighted(xq[:, r, :], (z1[:, r, :], z2[:, r, :]), w, "half_made", "sum_made", i)

                steps = dict(lh=lhs, hTc=hTc)
                if shared and off:
                    steps.update(gind=gindex, yc=last_add, tot=total)
                elif shared:
                    steps.update(scat=index, yc=add)
                pipelined(dve, steps, LAG, count, unroll)

            stages(0, NS, 4, True)
            stages(NS, SLOTS, 2, False)
            stages(NS + SLOTS, NS, 4, True)


INS = dict(x="x", cond_64="cond", mask_BxS_bf1="mask", L0_cond_g_norm="g_norm", L0_cond_Wq="Wq", L0_cond_Wkv="Wkv",
           L0_cond_q_scale="q_scale", L0_cond_k_scale="k_scale", L0_cond_null_attn_bias="null_bias",
           L0_cond_w0="w0", L0_cond_b0="b0", L0_cond_g0="g0", L0_cond_w1="w1", L0_cond_b1="b1", L0_cond_g1="g1",
           L0_cond_w2="w2", L0_cond_b2="b2", L0_cond_Wout="Wout", L0_cond_g_out="g_out",
           L1_cond_wt="wt", L1_cond_wg="wg", L1_cond_w_gate="w_gate", L1_cond_w_up="w_up", L1_cond_w_down="w_down",
           L1_cond_sw_gate="sw_gate", L1_cond_sw_up="sw_up", L1_cond_sw_down="sw_down")


def build(nc, a, out):
    with ExitStack() as ctx:
        def sem(name):
            return ctx.enter_context(nc.semaphore(name))

        sb = {n: sem(n) for n in CREDITS}
        dr = dict(bias=nc.dram_tensor("bias_rows", (H, P + S), F32, kind="Internal").ap(),
                  enull=nc.dram_tensor("enull_row", (H,), F32, kind="Internal").ap(),
                  x1=nc.dram_tensor("x1_rows", (T, D), F32, kind="Internal").ap(),
                  base=nc.dram_tensor("base_rows", (T, D), F32, kind="Internal").ap(),
                  xs=nc.dram_tensor("sorted_rows", (SLOTS * P, D), F32, kind="Internal").ap(),
                  ys=nc.dram_tensor("expert_rows", (SLOTS * P, D), F32, kind="Internal").ap())
        sb["LG"] = ctx.enter_context(nc.sbuf_tensor("LG", [P, NTT, NE], F32))
        sb["zero"] = ctx.enter_context(nc.sbuf_tensor("zero", [P, P], F32))
        sb["credit"] = ctx.enter_context(nc.sbuf_tensor("credit", [P, 48], F32))
        with ExitStack() as att:
            def tile(name, shape, dt=F32):
                sb[name] = att.enter_context(nc.sbuf_tensor(name, shape, dt))

            tile("ident", [P, P])
            tile("identr", [P, P], F32R)
            tile("EB", [P, H, S])
            tile("W", [P, KD, WQKV])
            tile("Wo", [P, 8, D])
            tile("wtT", [P, KD, NE])
            tile("gout", [P, D])
            tile("vnull", [P, VW])
            tile("negc", [P, 1])
            tile("enull", [P, H])
            tile("kfac", [P, DH])
            tile("maskf", [P, NTT])
            tile("glog", [P, B, NE])
            setup(nc, a, sb, dr, sem)
            tile("xnT", [P, KD, S])
            tile("QT", [P, 2, G, S], F32R)
            tile("KT", [P, 2, S], F32R)
            tile("V", [P, NT, VW])
            tile("AO", [P, NT, H * DH])
            tile("R1", [P, 3584])
            tile("parts", [P, 1024], F32R)

            tile("R2", [P, 3 * NT * VW])
            tile("xt", [P, 2, D])
            tile("small", [P, 450])
            psum = {n: [att.enter_context(nc.psum_tensor(f"ps{n}{i}", [P, 2, 512], F32)) for i in range(2)] for n in "SO"}
            attention(nc, a, sb, dr, sem, psum)
        experts(nc, a, sb, dr, sem, out.rearrange("b s d -> (b s) d"))


def kernel(**inputs):
    import numpy as np
    import concourse.bacc as bacc
    from concourse.bass_utils import run_bass_kernel_spmd

    nc = bacc.Bacc("TRN2", target_bir_lowering=False, num_devices=1)
    arrays, a = {}, {}
    for name, short in INS.items():
        v = np.ascontiguousarray(inputs[name])
        if v.dtype == np.bool_:
            v = v.view(np.uint8)
        arrays[f"in_{name}"] = v
        a[short] = nc.dram_tensor(f"in_{name}", v.shape, mybir.dt.from_np(v.dtype), kind="ExternalInput").ap()
    out = nc.dram_tensor("out_0", (B, S, D), F32, kind="ExternalOutput").ap()
    build(nc, a, out)
    r = run_bass_kernel_spmd(nc, [arrays], core_ids=[0])
    return r.results[0]["out_0"]
```

```python
from contextlib import ExitStack

import concourse.bass as bass
from concourse import mybir

P = 128
F32 = mybir.dt.float32
F32R = mybir.dt.float32r
I32 = mybir.dt.int32
U32 = mybir.dt.uint32
ALU = mybir.AluOpType
ACT = mybir.ActivationFunctionType
AX = mybir.AxisListType

B, S, D = 4, 1024, 512
H, DH = 16, 64
KD = D // P
NT = S // P
G = 2
NG = H // G
VW = DH + 1
WQKV = H * DH + 2 * DH + H
KVC = H * DH
NE, MD, SMD = 8, 256, 512
T = B * S
NTT = T // P
NS = 2 * NE
SLOTS = 2 * NTT + NE
LN_EPS = 1e-5
NORM_EPS = 1e-12
HEAD = 40.0
LIFT = 24

FILLS = [[(0, 0)], [(1, 0)], [(2, 0)], [(7, 0), (3, 128), (6, 768)], [(4, 0), (5, 512)]]
NF = len(FILLS)


def width(j):
    return S - P * j


def fill_width(k):
    j, c = FILLS[k][-1]
    return c + width(j)


class Chain:

    def __init__(self, eng, sem):
        self.eng, self.sem, self.base, self.n = eng, sem, 0, 0

    def link(self, ins):
        ins.then_inc(self.sem, 1)
        self.n += 1
        self.eng.wait_ge(self.sem, self.base + self.n)


def newton(dve, ch, y, y0, v, t, f):
    ch.link(dve.tensor_tensor(t, y0, y0, ALU.mult))
    ch.link(dve.tensor_tensor(t, t, v, ALU.mult))
    ch.link(dve.tensor_scalar(t, t, -0.5 * f * f * f, 1.5 * f, ALU.mult, ALU.add))
    return dve.tensor_tensor(y, y0, t, ALU.mult)


def x_scratch(sb):
    parts, at = {}, 0
    for name, n in (("st", 6 * NT), ("mv", 2 * NT), ("ve", NT), ("lv", NT), ("y0", NT), ("rs", NT)):
        parts[name] = sb["xstats"][:, at:at + n]
        at += n
    parts["var"] = parts["mv"].rearrange("p (t m) -> p t m", m=2)[:, :, 1]
    parts["in"] = sb["xnT"][:].rearrange("p k s -> p (k s)").rearrange("p (t n) -> p t n", n=D)
    return parts


def setup(nc, a, sb, dr, sem):
    xs = x_scratch(sb)
    with ExitStack() as ctx:
        def tmp(name, shape, dt=F32):
            return ctx.enter_context(nc.sbuf_tensor(name, shape, dt))

        def psum(name, shape):
            return ctx.enter_context(nc.psum_tensor(name, shape, F32))

        rows = {n: tmp("row_" + n, [P, D]) for n in ("w0", "b0", "g0", "b1", "g1")}
        gn = tmp("gn", [P, KD])
        w1 = tmp("w1", [P, KD, D])
        w2 = tmp("w2", [P, KD, H])
        h = tmp("h", [P, NT, D])
        hT = tmp("hT", [P, KD, S])
        pos = tmp("pos", [P, NT])
        st = tmp("st", [P, NT, 6])
        mv = tmp("mv", [P, NT, 2])
        ve = tmp("ve", [P, NT])
        y0 = tmp("y0", [P, NT])
        nt = tmp("nt", [P, NT])
        rs = tmp("rs", [P, NT])
        cond = tmp("cond", [P, B * DH])
        qs = tmp("qs", [P, DH])
        ks = tmp("ks", [P, DH])
        c2 = tmp("c2", [P, DH])
        ss = tmp("ss", [P, 4])
        kn = tmp("kn", [P, DH])
        wg = tmp("wg", [P, NE, DH])
        wgp = tmp("wgp", [P, NE, DH])
        mask8 = tmp("mask8", [P, NTT], mybir.dt.uint8)
        brow = tmp("brow", [H, P + S])
        braw = tmp("braw", [H, S])
        hcol = tmp("hcol", [H, 8])
        pA = [psum(f"pA{i}", [P, 512]) for i in range(4)]
        pB = psum("pB", [H, 2, 512])
        flip = tmp("flip", [P, P])
        turned = [x.rearrange("p a b -> p (a b)").rearrange("p (q h s) -> p q h s", h=2, s=S)[:, q]
                  for x in (h[:], hT[:]) for q in range(2)]
        wprod = tmp("wprod", [P, H, DH])
        wo = sb["EB"][:, 0:4, :].rearrange("p h s -> p (h s)").rearrange("p (k n) -> p k n", n=D)
        wol = tmp("wol", [P, 8, D], F32R)

        s_rows, s_w, s_cond, s_x = sem("s_rows"), sem("s_w"), sem("s_cond"), sem("s_x")
        s_id, s_dve, s_var, s_y0 = sem("s_id"), sem("s_dvec"), sem("s_svar"), sem("s_sy0")
        s_z, s_silu, s_tr, s_ev, s_mm, s_mv = (sem("s_" + n) for n in ("z", "silu", "tr", "ev", "mm", "mmev"))
        s_b, s_bex, s_bx, s_eb, s_kn = sem("s_b"), sem("s_bex"), sem("s_bx"), [sem(f"s_eb{i}") for i in range(4)], sem("s_kn")
        s_pw, s_dve2, s_hb = sem("s_pw"), sem("s_dve2"), sem("s_hb")
        s_kl, s_rs = sem("s_kl"), sem("s_rs")
        s_wo = sem("s_wo")
        block = ctx.enter_context(nc.Block())

        def bcast(ap, n):
            return bass.AP(ap.tensor, ap.offset, [[0, P], [1, n]])

        @block.sync
        def _(sp):
            for n in ("w0", "b0"):
                sp.dma_start(rows[n][:], bcast(a[n], D)).then_inc(s_rows, 16)
            for n in ("g0", "b1", "g1"):
                sp.dma_start(rows[n][:], bcast(a[n], D)).then_inc(s_cond, 16)
            sp.dma_start(cond[:], bcast(a["cond"], B * DH)).then_inc(s_cond, 16)
            sp.dma_start(qs[:], bcast(a["q_scale"], DH)).then_inc(s_cond, 16)
            sp.dma_start(ks[:], bcast(a["k_scale"], DH)).then_inc(s_cond, 16)
            sp.dma_start(wg[:], bass.AP(a["wg"].tensor, 0, [[0, P], [DH, NE], [1, DH]])).then_inc(s_cond, 16)
            sp.dma_start(gn[:], a["g_norm"].rearrange("(k p) -> p k", p=P),
                         allow_slow_non_contiguous=True).then_inc(s_w, 16)
            sp.dma_start(sb["W"][:, :, 0:KVC], a["Wq"].rearrange("(k p) n -> p k n", p=P)).then_inc(s_w, 16)
            sp.dma_start(sb["W"][:, :, KVC:KVC + 2 * DH], a["Wkv"].rearrange("(k p) n -> p k n", p=P)).then_inc(s_w, 16)
            sp.dma_start(mask8[:], a["mask"].rearrange("b (t p) -> p (b t)", p=P),
                         allow_slow_non_contiguous=True).then_inc(s_x, 16)
            for h_ in range(2):
                src = a["x"][0, 4 * h_ * P:(4 * h_ + 4) * P, :].rearrange("(t p) n -> p t n", p=P)
                sp.dma_start(xs["in"][:, 4 * h_:4 * h_ + 4, :], src).then_inc(s_x, 16)
            sp.wait_ge(s_bx, 2)
            sp.dma_start(dr["bias"], brow[:]).then_inc(s_bex, 16)
            sp.dma_start(dr["enull"].rearrange("(h a) -> h a", a=1), hcol[:, 5:6]).then_inc(s_bex, 16)
            sp.wait_ge(s_bex, 32)
            sp.dma_start(sb["enull"][:], bcast(dr["enull"], H)).then_inc(s_bex, 16)
            for q in range(8):
                if q >= 4:
                    sp.wait_ge(s_tr, 16 + 4 * (q - 3))
                src = bass.AP(dr["bias"].tensor, 2 * q * (P + S), [[1, P], [P + S, 2], [1, S]])
                sp.dma_start(turned[q % 4], src).then_inc(s_eb[q % 4], 16)
            sp.wait_ge(s_wo, 2)
            sp.dma_start(dr["wol"], wol[:].bitcast(F32).rearrange("p k n -> p (k n)")).then_inc(s_bex, 16)
            sp.wait_ge(s_bex, 64)

        @block.gpsimd
        def _(pool):
            pool.memset(sb["ident"][:], 0.0).then_inc(s_id, 1)
            pool.wait_ge(s_id, 1)
            pool.affine_select(out=sb["ident"][:], in_=sb["ident"][:], compare_op=ALU.not_equal, fill=1.0, base=0,
                               pattern=[[-1, P]], channel_multiplier=1).then_inc(s_id, 1)
            pool.memset(flip[:], 0.0).then_inc(s_id, 1)
            pool.memset(sb["zero"][:], 0.0).then_inc(s_id, 1)
            pool.wait_ge(s_id, 4)
            pool.affine_select(out=flip[:], in_=flip[:], compare_op=ALU.not_equal, fill=1.0, base=1 - P,
                               pattern=[[1, P]], channel_multiplier=1).then_inc(s_id, 1)
            pool.iota(pos[:], [[P, NT]], base=0, channel_multiplier=1,
                      allow_small_or_imprecise_dtypes=True).then_inc(s_id, 1)
            for i, name in enumerate(CREDITS):
                pool.memset(sb["credit"][:, i:i + 1], 0.0).then_inc(sb[name], CREDITS[name])
            pool.wait_ge(s_wo, 1)
            pool.tensor_tensor(wol[:], wo, sb["Wo"][:].bitcast(F32), ALU.subtract).then_inc(s_wo, 1)
            pool.wait_ge(s_kn, 1 + KD)
            for k in range(KD):
                if k:
                    pool.wait_ge(s_pw, 2 * k)
                pool.tensor_tensor(wprod[:], sb["W"][:, k, 0:KVC].rearrange("p (h d) -> p h d", h=H),
                                   kn[:].unsqueeze(1).to_broadcast([P, H, DH]), ALU.mult).then_inc(s_pw, 1)

        @block.scalar
        def _(act):
            act.dma_start(w1[:], a["w1"].rearrange("(k p) n -> p k n", p=P)).then_inc(s_mv, 16)
            act.dma_start(w2[:], a["w2"].rearrange("(k p) n -> p k n", p=P)).then_inc(s_mv, 16)
            act.dma_start(hcol[:, 0:1], a["b2"].rearrange("(h a) -> h a", a=1)).then_inc(s_mv, 16)
            act.dma_start(hcol[:, 1:2], a["null_bias"].rearrange("(h a) -> h a", a=1)).then_inc(s_mv, 16)
            act.dma_start(wo, a["Wout"].rearrange("(k p) n -> p k n", p=P)).then_inc(s_w, 16)
            act.dma_start(sb["gout"][:], bcast(a["g_out"], D)).then_inc(s_w, 16)
            for k in range(KD):
                act.dma_start(sb["wtT"][:, k, :], bass.AP(a["wt"].tensor, k * P, [[1, P], [D, NE]]),
                              allow_slow_non_contiguous=True).then_inc(s_w, 16)
            for layer in range(2):
                act.preload_act_table_set("natural_log_exp_and_others")
                if layer:
                    act.wait_ge(s_kn, 1)
                    act.activation(ss[:, 1:2], ss[:, 0:1], ACT.Ln, scale=float(2 ** LIFT)).then_inc(s_kl, 1)
                    act.wait_ge(s_kl, 1)
                    act.activation(ss[:, 2:3], ss[:, 1:2], ACT.Exp, scale=-0.5).then_inc(s_kl, 1)
                    act.wait_ge(s_w, 16 * (5 + KD))
                    act.activation(sb["Wo"][:], wo, ACT.Copy).then_inc(s_wo, 1)
                act.wait_ge(s_var, layer + 1)
                act.activation(nt[:], ve[:], ACT.Ln).then_inc(s_y0, 1)
                act.wait_ge(s_y0, 2 * layer + 1)
                act.activation(y0[:], nt[:], ACT.Exp, scale=-0.5).then_inc(s_y0, 1)
                for c in range(NT):
                    act.wait_ge(s_z, NT * layer + c + 1)
                    act.wait_ge(s_rs, layer + 1)
                    act.activation(h[:, c, :], h[:, c, :], ACT.Silu, scale=rs[:, c:c + 1]).then_inc(s_silu, 1)
                for i in range(1, 8, 2):
                    act.wait_ge(s_tr, 8 * layer + i + 1)
                    if layer:
                        act.wait_ge(s_mm, NT)
                    k, half = i % 4, i // 4
                    act.activation(hT[:, k, half * 512:(half + 1) * 512], pA[i % 4][:], ACT.Copy).then_inc(s_ev, 1)
            act.wait_ge(s_b, 1)
            act.activation(brow[:, P - 1:P - 1 + S], braw[:], ACT.Exp, bias=hcol[:, 4:5]).then_inc(s_bx, 1)
            act.activation(hcol[:, 5:6], hcol[:, 1:2], ACT.Exp, bias=hcol[:, 4:5]).then_inc(s_bx, 1)
            act.wait_ge(s_var, 3)
            act.activation(xs["lv"], xs["ve"], ACT.Ln).then_inc(s_y0, 1)
            act.wait_ge(s_y0, 5)
            act.activation(xs["y0"], xs["lv"], ACT.Exp, scale=-0.5).then_inc(s_y0, 1)
            for i in range(1, 2 * H, 2):
                act.wait_ge(s_tr, 16 + i + 1)
                if i == 1:
                    act.wait_ge(s_wo, 2)
                act.activation(sb["EB"][:, i // 2, 512:1024], pA[i % 4][:], ACT.Copy).then_inc(s_ev, 1)

        @block.tensor
        def _(pe):
            pe.wait_ge(s_id, 2)
            for layer in range(2):
                for i in range(8):
                    k, half = i % 4, i // 4
                    if k == 0:
                        pe.wait_ge(s_silu, NT * layer + 4 * half + 4)
                    if i >= 4:
                        pe.wait_ge(s_ev if i % 2 else s_dve2, 4 * layer + (i - 4) // 2 + 1)
                    for c in range(4):
                        ins = pe.transpose(pA[i % 4][:, c * P:(c + 1) * P],
                                           h[:, half * 4 + c, k * P:(k + 1) * P], sb["ident"][:])
                    ins.then_inc(s_tr, 1)
                pe.wait_ge(s_ev, 4 * layer + 4)
                pe.wait_ge(s_dve2, 4 * layer + 4)
                if layer == 0:
                    pe.wait_ge(s_mv, 64)
                    for c in range(NT):
                        if c >= 4:
                            pe.wait_ge(s_hb, c - 3)
                        for k in range(KD):
                            ins = pe.matmul(pA[c % 4][:], hT[:, k, c * P:(c + 1) * P], w1[:, k, :],
                                            start=(k == 0), stop=(k == KD - 1))
                        ins.then_inc(s_mm, 1)
                    pe.wait_ge(s_hb, NT)
                else:
                    for half in range(2):
                        for k in range(KD):
                            ins = pe.matmul(pB[:, half, :], w2[:, k, :], hT[:, k, half * 512:(half + 1) * 512],
                                            start=(k == 0), stop=(k == KD - 1))
                        ins.then_inc(s_mm, 1)
            pe.wait_ge(s_id, 5)
            for i in range(2 * H):
                if i % 4 == 0:
                    pe.wait_ge(s_eb[i // 4 % 4], 16 * (i // 16 + 1))
                if i >= 4:
                    pe.wait_ge(s_ev if i % 2 else s_dve2, 8 + (i - 4) // 2 + 1)
                pe.matmul(pA[i % 4][:], flip[:], turned[i // 4 % 4][:, i // 2 % 2, (i % 2) * 512:(i % 2 + 1) * 512],
                          start=True, stop=True).then_inc(s_tr, 1)

        @block.vector
        def _(dve):
            ch = Chain(dve, s_dve)
            dve.wait_ge(s_id, 2)
            ch.link(dve.tensor_copy(sb["identr"][:], sb["ident"][:]))
            def side(c):
                if c == 0:
                    dve.wait_ge(s_cond, 112)
                    ch.link(dve.tensor_tensor(c2[:], cond[:, 0:DH], cond[:, 0:DH], ALU.mult))
                    ch.link(dve.tensor_reduce(ss[:, 0:1], c2[:], AX.X, ALU.add))
                    dve.tensor_scalar(ss[:, 0:1], ss[:, 0:1], NORM_EPS ** 2, None, ALU.max).then_inc(s_kn, 1)
                    ch.link(dve.scalar_tensor_tensor(out=sb["kfac"][:], in0=qs[:], scalar=float(DH) ** 0.5, in1=ks[:],
                                                     op0=ALU.mult, op1=ALU.mult))
                    ch.link(dve.tensor_reduce(c2[:, 0:1], sb["kfac"][:], AX.X, ALU.max, apply_absolute_value=True))
                    ch.link(dve.tensor_scalar(sb["negc"][:], c2[:, 0:1], -1.0, HEAD, ALU.mult, ALU.add))
                if c == 2:
                    dve.wait_ge(s_kl, 2)
                    dve.wait_ge(s_kn, 1)
                    ch.link(newton(dve, ch, ss[:, 3:4], ss[:, 2:3], ss[:, 0:1], ss[:, 1:2], float(2 ** (LIFT // 2))))
                    ch.link(dve.scalar_tensor_tensor(out=kn[:], in0=cond[:, 0:DH], scalar=ss[:, 3:4], in1=sb["kfac"][:],
                                                     op0=ALU.mult, op1=ALU.mult))
                    ch.link(dve.memset(sb["vnull"][:], 1.0))
                    ch.link(dve.tensor_copy(sb["vnull"][:, 0:DH], cond[:, DH:2 * DH]))
                if 3 <= c <= 6:
                    k = c - 3
                    dve.wait_ge(s_w, 16 * (5 + KD))
                    dve.tensor_scalar(sb["W"][:, k, 0:KVC + 2 * DH], sb["W"][:, k, 0:KVC + 2 * DH], gn[:, k:k + 1],
                                      None, ALU.mult).then_inc(s_kn, 1)
                if c >= 4:
                    b = c - 4
                    ch.link(dve.tensor_tensor(wgp[:], wg[:], cond[:, b * DH:(b + 1) * DH].unsqueeze(1)
                                              .to_broadcast([P, NE, DH]), ALU.mult))
                    ch.link(dve.tensor_reduce(sb["glog"][:, b, :], wgp[:], AX.X, ALU.add))
                if c == 7:
                    dve.wait_ge(s_x, 48)
                    ch.link(dve.tensor_copy(sb["maskf"][:], mask8[:]))

            dve.wait_ge(s_rows, 32)
            dve.wait_ge(s_id, 6)
            for c in range(NT):
                ins = dve.scalar_tensor_tensor(out=h[:, c, :], in0=rows["w0"][:], scalar=pos[:, c:c + 1],
                                               in1=rows["b0"][:], op0=ALU.mult, op1=ALU.add)
            ch.link(ins)
            for layer in range(2):
                if layer:
                    for c in range(NT):
                        dve.wait_ge(s_mm, c + 1)
                        ins = dve.tensor_tensor(h[:, c, :], pA[c % 4][:], rows["b1"][:], ALU.add)
                        ins.then_inc(s_hb, 1)
                        side(c)
                        dve.wait_ge(s_hb, c + 1)
                        ins = dve.bn_stats(st[:, c, :], h[:, c, :])
                else:
                    for c in range(NT):
                        ins = dve.bn_stats(st[:, c, :], h[:, c, :])
                ch.link(ins)
                for c in range(NT):
                    ins = dve.bn_aggr(mv[:, c, :], st[:, c, :])
                ch.link(ins)
                dve.tensor_scalar(ve[:], mv[:, :, 1], LN_EPS, None, ALU.add).then_inc(s_var, 1)
                gain = rows["g1" if layer else "g0"]
                dve.wait_ge(s_cond, 112)
                for c in range(NT):
                    dve.scalar_tensor_tensor(out=h[:, c, :], in0=h[:, c, :], scalar=mv[:, c, 0:1], in1=gain[:],
                                             op0=ALU.subtract, op1=ALU.mult).then_inc(s_z, 1)
                    if c == 1:
                        dve.wait_ge(s_var, layer + 1)
                        dve.wait_ge(s_y0, 2 * layer + 2)
                        newton(dve, ch, rs[:], y0[:], ve[:], nt[:], 1.0).then_inc(s_rs, 1)
                for i in range(0, 8, 2):
                    dve.wait_ge(s_tr, 8 * layer + i + 1)
                    if layer:
                        dve.wait_ge(s_mm, NT)
                    k, half = i % 4, i // 4
                    dve.tensor_copy(hT[:, k, half * 512:(half + 1) * 512], pA[i % 4][:]).then_inc(s_dve2, 1)
            ch.link(dve.memset(brow[:], 0.0))
            dve.wait_ge(s_mm, NT + 2)
            dve.wait_ge(s_mv, 64)
            ch.link(dve.tensor_scalar(braw[:], pB[:].rearrange("h a n -> h (a n)"), hcol[:, 0:1], None, ALU.add))
            ch.link(dve.tensor_reduce(hcol[:, 2:3], braw[:], AX.X, ALU.max))
            ch.link(dve.tensor_tensor(hcol[:, 3:4], hcol[:, 2:3], hcol[:, 1:2], ALU.max))
            dve.tensor_scalar(hcol[:, 4:5], hcol[:, 3:4], -1.0, None, ALU.mult).then_inc(s_b, 1)
            dve.wait_ge(s_x, 48)
            for t in range(NT):
                ins = dve.bn_stats(xs["st"][:, 6 * t:6 * t + 6], xs["in"][:, t, :])
            ch.link(ins)
            for t in range(NT):
                ins = dve.bn_aggr(xs["mv"][:, 2 * t:2 * t + 2], xs["st"][:, 6 * t:6 * t + 6])
            ch.link(ins)
            dve.tensor_scalar(xs["ve"], xs["var"], LN_EPS, None, ALU.add).then_inc(s_var, 1)
            for k in range(KD):
                dve.wait_ge(s_pw, 1 + 2 * k)
                dve.tensor_reduce(sb["W"][:, k, KVC + 2 * DH:], wprod[:], AX.X, ALU.add).then_inc(s_pw, 1)
                if k == 0:
                    dve.wait_ge(s_var, 3)
                    dve.wait_ge(s_y0, 6)
                    ch.link(newton(dve, ch, xs["rs"], xs["y0"], xs["ve"], nt[:], 1.0))
            for i in range(0, 2 * H, 2):
                dve.wait_ge(s_tr, 16 + i + 1)
                if i == 0:
                    dve.wait_ge(s_wo, 2)
                dve.tensor_copy(sb["EB"][:, i // 2, 0:512], pA[i % 4][:]).then_inc(s_dve2, 1)


CREDITS = {n: 2 for n in (
    "x_used",
    "qst_made", "qT_made", "qTa_copied", "qTv_copied",
    "exp_made", "pv_made", "num_made", "ao_made",
    "aT_made", "y_made", "x1T_made", "x1T_copied", "lg_made", "lg_used")}
CREDITS.update(x1_stored0=16, x1_stored1=16)
EVENTS = ("var_ready", "y0_ready", "kv_made", "kv_copied", "ksq_made", "ssk_clamped", "yk_ready", "kst_made",
          "q_made", "sq_made", "qn_made", "p_made", "ssq_made", "yq_made", "qhi_made", "nz_made", "nexp_made", "pn_made",
          "s_made", "rec_made", "nul_made", "var2_ready", "y02_ready", "x_in0", "x_in1", "filled",
          "xa_in0", "xa_in1", "wol_in0", "wol_in1", "aTh_made", "aTl_made", "half_used", "xn_made", "xT_made", "xT_copied", "v_made", "kT_made", "kT_copied")

PE_Q = {0: [("Q", 0), ("Q", 1)], 1: [("Q", 2), ("Q", 3)], 2: [("Q", 4)], 3: [("Q", 5)], 4: [("Q", 6), ("Q", 7)],
        5: [("T", 0)], 7: [("T", 1)], 9: [("T", 2)], 11: [("T", 3)]}
ACT_Q = {1: [("sq", 0)], 2: [("y", 0)], 3: [("hi", 0)], 5: [("cp", 0), ("sq", 1)], 6: [("y", 1)], 7: [("hi", 1)],
         9: [("cp", 1)]}
DVE_Q = {1: [("red", 0)], 2: [("qn", 0)], 5: [("red", 1)], 6: [("qn", 1)], 7: [("cp", 0)], 9: [("cp", 1)]}
A_LAG = dict(T=0, kv=2)
D_LAG = dict(xs=0, xv=1, xe=1, xr=2, xn=5, TA=0, cp=1, Y=2, st=3, y0=3, nrm=3, T1=4, x1Tc=5, lg=5, lgc=6)
assert NS == NTT - NS
CH_S_V, CH_A_V, CH_G_V, CH_D_V = 6, 9, 10, 64
CH_S_A, CH_A_A, CH_G_A, CH_D_A = 1, 1, 2, 8


def skewed(steps, lags, count):
    order = sorted(steps, key=lambda n: -lags[n])
    for i in range(count + max(lags.values())):
        for n in order:
            if 0 <= i - lags[n] < count:
                steps[n](i - lags[n])


def beside(table, fill, steps):
    for name, n in table.get(fill, ()):
        steps[name](n)


def attention(nc, a, sb, dr, sem, psum):
    e = {n: sem(n) for n in EVENTS}
    e.update({n: sb[n] for n in CREDITS})
    psS, psO = psum["S"], psum["O"]
    R1, R2, xt = sb["R1"], sb["R2"], sb["xt"]
    xnT, QT, KT, V, AO, LG = (sb[n] for n in ("xnT", "QT", "KT", "V", "AO", "LG"))
    ident = sb["ident"]

    def r1(n, size, base=0):
        return R1[:, base + n * size:base + (n + 1) * size]

    x = x_scratch(sb)
    xin = x["in"]
    xn = [r1(u, D) for u in range(6)] + [xt[:, u, :] for u in range(2)]
    knr = R2[:, 0:NT * DH].rearrange("p (t d) -> p t d", d=DH)
    ksq = R2[:, NT * DH:2 * NT * DH].rearrange("p (t d) -> p t d", d=DH)
    KVW = 2 * DH + H
    kvs = R1[:, 0:NT * KVW].rearrange("p (t n) -> p t n", n=KVW)
    kst = sb["parts"][:].rearrange("p (t s r d) -> p t s r d", s=2, r=2, d=DH)
    qst = sb["parts"][:].rearrange("p (n s d) -> p n s d", s=2, d=DH)
    identr = sb["identr"]
    qn = R1[:, 3072:3584].rearrange("p (n d) -> p n d", d=DH)
    qn_first = [qn, R1[:, 2048:2560].rearrange("p (n d) -> p n d", d=DH)]
    E = [r1(u, 1024) for u in range(3)]
    nul, *num = [R2[:, u * NT * VW:(u + 1) * NT * VW].rearrange("p (t d) -> p t d", d=VW) for u in range(3)]
    turns = [KT[:, 0], KT[:, 1], sb["parts"][:]]
    AOT = [x.rearrange("p (s k t) -> p s k t", s=2, t=P) for x in turns]
    wol = QT[:].rearrange("p a h s -> p (a h s)").rearrange("p (k n) -> p k n", n=D)
    y = [r1(u, 512, 2048) for u in range(2)]
    x1T = [R2[:, u * 512:(u + 1) * 512].rearrange("p (k t) -> p k t", t=P) for u in range(2)]

    sm = sb["small"]
    c = [0]

    def small(n):
        c[0] += n
        return sm[:, c[0] - n:c[0]]

    st = [small(6) for _ in range(2)]
    mv = [small(2) for _ in range(2)]
    ve, lv, y0, rs, nt = (small(NT) for _ in range(5))
    xst, xmv, xve, xlv, xy0, xrs, xvar = (x[n] for n in ("st", "mv", "ve", "lv", "y0", "rs", "var"))
    ssk, ssc, lk, yk, rk = (small(NT) for _ in range(5))
    ssq, lq, yq, rq = (small(NT * G) for _ in range(4))
    nq, idle = small(8), small(1)
    rec = [small(8) for _ in range(2)]
    pz, pe_, pn = (small(NT * G).rearrange("p (t h) -> p t h", h=G) for _ in range(3))
    snull = small(NT * H).rearrange("p (t h) -> p t h", h=H)

    sv, sa = [sem("dve_" + n) for n in "agds"], [sem("act_" + n) for n in "agds"]

    kv_banks = (psO[0][:, 0], psO[0][:, 1], psS[1][:, 1])

    def xtp(t):
        return (psS[0][:, 0], psS[0][:, 1], psS[1][:, 0])[t % 3]

    def ktp(pair):
        return psS[pair // 2][:, pair % 2]

    block_ctx = nc.Block()
    with block_ctx as block:
        @block.sync
        def _(sp):
            def load_batch(b, after):
                for h in range(2):
                    src = a["x"][bass.ds(b, 1), 4 * h * P:(4 * h + 4) * P, :].rearrange("a (t p) n -> p (a t) n", p=P)
                    if h == 0:
                        sp.wait_ge(e["q_made"], after)
                    sp.dma_start(xin[:, 4 * h:4 * h + 4, :], src).then_inc(e[f"xa_in{h}"], 16)

            def batch(b, more):
                def load(t):
                    n = value(sp, b * NT + (t + 1 if t >= 2 else NT))
                    src = a["x"][bass.ds(b, 1), t * P:(t + 1) * P, :].rearrange("a p n -> (a p) n")
                    sp.wait_ge(e["x_used" if t >= 2 else "xT_made"], n)
                    sp.dma_start(xt[:, t % 2, :], src).then_inc(e[f"x_in{t % 2}"], 16)

                def store(t):
                    n = value(sp, b * NT + (t + 3))
                    dst = dr["x1"][bass.ds(b * S + t * P, P), :]
                    sp.wait_ge(e["x_used"], n)
                    sp.dma_start(dst, y[t % 2]).then_inc(e[f"x1_stored{t % 2}"], 16)

                load(0)
                load(1)
                n = SLOTS // B * P
                sp.dma_start(dr["xs"][bass.ds(b * n, n), :].rearrange("r d -> (r d)").rearrange("(n p f) -> p n f", p=P, f=P),
                             sb["zero"][:].unsqueeze(1).to_broadcast([P, n * D // (P * P), P])).then_inc(e["filled"], 16)
                if more:
                    load_batch(b + 1, value(sp, (b + 1) * (NG * 2)))
                for h in range(2):
                    n = value(sp, (b * NG + (NG - 1 + h)) * (G * NF))
                    dst = wol[:, 4 * h:4 * h + 4].rearrange("p k n -> p (k n)").bitcast(F32)
                    sp.wait_ge(e["s_made"], n)
                    sp.dma_start(dst, dr["wol"][:, 4 * h * D:(4 * h + 4) * D]).then_inc(e[f"wol_in{h}"], 16)
                for t in range(NT):
                    store(t)
                    if t + 2 < NT:
                        load(t + 2)

            with sp.Fori(0, B - 1) as b:
                batch(b, True)
            batch(B - 1, False)
            for u in range(2):
                sp.wait_ge(e[f"x1_stored{u}"], 16 + 16 * B * NT // 2)
            sp.wait_ge(e["filled"], 16 * B)

        @block.gpsimd
        def _(pool):
            with pool.Fori(0, B) as b:
                def queries(gi, bufs=(qn, qn)):
                    for q in range(2):
                        pool.wait_ge(e["qhi_made"], gi * 2 + (q + 1))
                        pool.tensor_tensor(qst[:, :, 1, :], bufs[q], qst[:, :, 0, :].bitcast(F32), ALU.subtract).then_inc(e["qst_made"], 1)

                def group(g, more):
                    gi = b * NG + g
                    m0 = pool.snap(gi * G)

                    def null_part(hh):
                        if hh == 0:
                            pool.wait_ge(e["pn_made"], gi + 1)
                        pool.wait_ge(e["num_made"], m0 + (hh + 2))
                        pool.tensor_tensor(nul, pn[:, :, hh:hh + 1].to_broadcast([P, NT, VW]),
                                           sb["vnull"][:].unsqueeze(1).to_broadcast([P, NT, VW]), ALU.mult)\
                            .then_inc(e["nul_made"], 1)

                    def scale(hh):
                        dst = AO[:, :, bass.ds((g * G + hh) * DH, DH)]
                        pool.wait_ge(e["rec_made"], m0 + (hh + 1))
                        pool.tensor_tensor(dst, num[hh % 2][:, :, 0:DH],
                                           rec[hh % 2].unsqueeze(2).to_broadcast([P, NT, DH]), ALU.mult)\
                            .then_inc(e["ao_made"], 1)

                    null_part(0)
                    if more:
                        queries(gi + 1)
                    null_part(1)
                    scale(0)
                    scale(1)

                queries(b * NG, qn_first)
                with pool.Fori(0, NG // 2 - 1) as p2:
                    group(p2 * 2, True)
                    group(p2 * 2 + 1, True)
                group(NG - 2, True)
                group(NG - 1, False)

        @block.scalar
        def _(act):
            act.preload_act_table_set("natural_log_exp_and_others")
            def deviations(b):
                ch = Chain(act, sa[3])
                ch.base = (b - 1) * CH_S_A
                act.wait_ge(e["var_ready"], b)
                ch.link(act.activation(xlv, xve, ACT.Ln))
                act.activation(xy0, xlv, ACT.Exp, scale=-0.5).then_inc(e["y0_ready"], 1)
                assert ch.n == CH_S_A, ch.n

            def batch(b, more):
                n0 = value(act, b * NT)
                chA = Chain(act, sa[0])
                chA.base = b * CH_A_A

                def xTc(t):
                    act.wait_ge(e["xT_made"], n0 + (t + 1))
                    if t == 0:
                        act.wait_ge(e["xn_made"], n0 + NT)
                    act.activation(xnT[:, :, t * P:(t + 1) * P], xtp(t).rearrange("p (k t) -> p k t", t=P), ACT.Copy)\
                        .then_inc(e["xT_copied"], 1)

                def kTc(pair):
                    act.wait_ge(e["kT_made"], b * 4 + (pair + 1))
                    act.activation(KT[:, :, 2 * pair * P:(2 * pair + 2) * P],
                                   ktp(pair).rearrange("p (s t) -> p s t", s=2), ACT.Copy).then_inc(e["kT_copied"], 1)

                for t in range(NT):
                    xTc(t)
                act.wait_ge(e["kv_copied"], b + 1)
                act.activation(ksq, kvs[:, :, 0:DH], ACT.Square).then_inc(e["ksq_made"], 1)
                act.wait_ge(e["ssk_clamped"], b + 1)
                chA.link(act.activation(lk, ssc, ACT.Ln, scale=float(2 ** LIFT)))
                act.activation(yk, lk, ACT.Exp, scale=-0.5).then_inc(e["yk_ready"], 1)
                assert chA.n == CH_A_A, chA.n

                def steps_of(gi, par, bufs=(qn, qn)):
                    m = act.snap(gi * 2)
                    m2 = act.snap(gi * 4)
                    ch = Chain(act, sa[1])
                    ch.base = gi * CH_G_A

                    def sqq(q):
                        act.wait_ge(e["q_made"], m + (q + 1))
                        act.wait_ge(e["qst_made"], m + (q + 2 if bufs[0] is bufs[1] else 2))
                        act.activation(bufs[q].rearrange("p n d -> p (n d)"), psO[1][:, q, :], ACT.Square)\
                            .then_inc(e["sq_made"], 1)

                    def yqs(q):
                        w = slice(q * 8, q * 8 + 8)
                        act.wait_ge(e["ssq_made"], m + (q + 1))
                        ch.link(act.activation(lq[:, w], ssq[:, w], ACT.Ln, scale=float(2 ** LIFT)))
                        act.activation(yq[:, w], lq[:, w], ACT.Exp, scale=-0.5).then_inc(e["yq_made"], 1)

                    def hi(q):
                        act.wait_ge(e["qn_made"], m + (q + 1))
                        act.wait_ge(e["qT_made"], m2 + (2 * q + 2))
                        act.activation(qst[:, :, 0, :], bufs[q], ACT.Copy).then_inc(e["qhi_made"], 1)

                    def cpq(q):
                        act.wait_ge(e["qT_made"], m2 + (2 * q + 3))
                        act.activation(QT[:, par, :, 4 * q * P:(4 * q + 2) * P],
                                       psO[1][:, q, :].rearrange("p (h t) -> p h t", h=G), ACT.Copy)\
                            .then_inc(e["qTa_copied"], 1)

                    return dict(sq=sqq, y=yqs, hi=hi, cp=cpq)

                def group(g, par, more):
                    gi = b * NG + g
                    f0 = act.snap(gi * (G * NF))
                    steps = steps_of(gi + 1, 1 - par) if more else None
                    act.wait_ge(e["nz_made"], gi + 1)
                    act.activation(pe_, pz, ACT.Exp, bias=sb["negc"][:]).then_inc(e["nexp_made"], 1)
                    for f in range(G * NF):
                        n = fill_width(f % NF)
                        act.wait_ge(e["s_made"], f0 + (f + 1))
                        act.wait_ge(e["pv_made"], f0 + max(f, 2))
                        act.activation(E[f % 3][:, 0:n], psS[f % 2][:].rearrange("p a n -> p (a n)")[:, 0:n], ACT.Exp,
                                       bias=sb["negc"][:]).then_inc(e["exp_made"], 1)
                        if more:
                            beside(ACT_Q, f, steps)

                first = steps_of(b * NG, 0, qn_first)
                for n, q in (("sq", 0), ("y", 0), ("sq", 1), ("y", 1)):
                    first[n](q)
                kTc(0)
                kTc(1)
                act.wait_ge(e["kT_made"], b * 4 + 4)
                first["hi"](0)
                kTc(2)
                kTc(3)
                for n, q in (("cp", 0), ("hi", 1), ("cp", 1)):
                    first[n](q)
                with act.Fori(0, NG // 2 - 1) as p2:
                    group(p2 * 2, 0, True)
                    group(p2 * 2 + 1, 1, True)
                group(NG - 2, 0, True)
                group(NG - 1, 1, False)
                chD = Chain(act, sa[2])
                chD.base = b * CH_D_A

                def cpa(t):
                    act.wait_ge(e["aT_made"], n0 + (t + 3))
                    for h in range(2):
                        g = 2 * t + h
                        if g >= 3 and h:
                            act.wait_ge(e["half_used"], n0 + t)
                        elif g >= 3:
                            act.wait_ge(e["y_made"], n0 + (t + 1))
                        act.activation(AOT[g % 3][:, 0].rearrange("p k t -> p (k t)"), psS[t % 2][:, h, :], ACT.Copy)\
                            .then_inc(e["aTh_made"], 1)

                def y0d(t):
                    act.wait_ge(e["var2_ready"], n0 + (t + 1))
                    chD.link(act.activation(lv[:, t:t + 1], ve[:, t:t + 1], ACT.Ln))
                    act.activation(y0[:, t:t + 1], lv[:, t:t + 1], ACT.Exp, scale=-0.5).then_inc(e["y02_ready"], 1)

                def x1Tc(t):
                    act.wait_ge(e["x1T_made"], n0 + (t + 3))
                    act.wait_ge(e["lg_made"], n0 + (t + 1))
                    act.activation(x1T[t % 2].rearrange("p k t -> p (k t)"), psO[t % 2][:, 1, :], ACT.Copy)\
                        .then_inc(e["x1T_copied"], 1)

                def xe(t):
                    if t == NT - 1:
                        deviations(b + 1)

                steps = dict(cp=cpa, y0=y0d, x1Tc=x1Tc)
                if more:
                    steps["xe"] = xe
                skewed(steps, D_LAG, NT)
                assert chD.n == CH_D_A, chD.n

            with act.Fori(0, B - 1) as b:
                batch(b, True)
            batch(B - 1, False)

        @block.tensor
        def _(pe):
            W, Wo = sb["W"], sb["Wo"]
            with pe.Fori(0, B) as b:
                n0 = pe.snap(b * NT)

                def T(t):
                    pe.wait_ge(e["xn_made"], n0 + (t + 1))
                    if t >= 3:
                        pe.wait_ge(e["xT_copied"], n0 + (t - 2))
                    for k in range(KD):
                        ins = pe.transpose(xtp(t)[:, k * P:(k + 1) * P], xn[t][:, k * P:(k + 1) * P], ident[:])
                    ins.then_inc(e["xT_made"], 1)

                def kv(t):
                    pe.wait_ge(e["xT_copied"], n0 + (t + 1))
                    for k in range(KD):
                        ins = pe.matmul(kv_banks[t // 3][:, t % 3 * KVW:(t % 3 + 1) * KVW], xnT[:, k, t * P:(t + 1) * P], W[:, k, KVC:],
                                        start=(k == 0), stop=(k == KD - 1))
                    ins.then_inc(e["kv_made"], 1)

                def kT(pair):
                    if pair % 2 == 0:
                        pe.wait_ge(e["kst_made"], b * 2 + (pair // 2 + 1))
                    for t in range(2 * pair, 2 * pair + 2):
                        for s in range(2):
                            ins = pe.matmul(ktp(pair)[:, (2 * s + t % 2) * P:(2 * s + t % 2 + 1) * P],
                                            kst[:, t % 4, s].rearrange("p r d -> p (r d)"), identr[:], start=True, stop=True)
                    ins.then_inc(e["kT_made"], 1)

                skewed(dict(T=T, kv=kv), A_LAG, NT)

                def steps_of(gi, g, other=1):
                    m = pe.snap(gi * 2)
                    cols = bass.ds(g * (G * DH), G * DH)

                    def Q(t):
                        q, i = t // 4, t % 4
                        if i == 0:
                            pe.wait_ge(e["qTa_copied"], m + (q + 1))
                            pe.wait_ge(e["qTv_copied"], m + (q + 1))
                        for k in range(KD):
                            ins = pe.matmul(psO[1][:, q, i * P:(i + 1) * P], xnT[:, k, t * P:(t + 1) * P],
                                            W[:, k, cols], start=(k == 0), stop=(k == KD - 1))
                        if i == 3:
                            ins.then_inc(e["q_made"], 1)

                    def TQ(n):
                        q, half = n // 2, n % 2
                        if half == 0:
                            pe.wait_ge(e["qst_made"], m + (q + 3))
                        elif other == 1:
                            pe.wait_ge(e["qTa_copied"], m + (q + 3))
                        bank = psO[other if half else 1][:, q]
                        for i in range(2):
                            for h in range(G):
                                ins = pe.matmul(bank[:, (h * 2 + i) * P:(h * 2 + i + 1) * P],
                                                qst[:, (half * 2 + i) * G + h].rearrange("p s d -> p (s d)"),
                                                identr[:], start=True, stop=True)
                        ins.then_inc(e["qT_made"], 1)

                    return dict(Q=Q, T=TQ)

                def group(g, par, more):
                    gi = b * NG + g
                    m0 = pe.snap(gi * G)
                    f0 = pe.snap(gi * (G * NF))
                    steps = steps_of(gi + 1, g + 1) if more else None
                    pe.wait_ge(e["qTa_copied"], m0 + 4)
                    pe.wait_ge(e["qTv_copied"], m0 + 4)

                    def scores(f):
                        hh, k = f // NF, f % NF
                        pe.wait_ge(e["exp_made"], f0 + (f + 1))
                        for j, c0 in FILLS[k]:
                            w, at = width(j), 0
                            while at < w:
                                m = min(w - at, 512 - (c0 + at) % 512)
                                bank, off = (c0 + at) // 512, (c0 + at) % 512
                                for s in range(2):
                                    ins = pe.matmul(psS[f % 2][:, bank, off:off + m], KT[:, s, j * P:(j + 1) * P],
                                                    QT[:, par, hh, j * P + at:j * P + at + m],
                                                    start=(s == 0), stop=(s == 1))
                                at += m
                        ins.then_inc(e["s_made"], 1)

                    def values(f):
                        hh, k = f // NF, f % NF
                        pe.wait_ge(e["p_made"], f0 + (f + 1))
                        if k == 0:
                            pe.wait_ge(e["num_made"], m0 + (hh + 2))
                        for j, c0 in FILLS[k]:
                            for i in range(j, NT):
                                ins = pe.matmul(psO[0][:, i // 4, (i % 4) * VW:(i % 4 + 1) * VW],
                                                E[f % 3][:, c0 + (i - j) * P:c0 + (i - j + 1) * P], V[:, j, :],
                                                start=(j == 0 and i % 4 == 0), stop=(k == NF - 1),
                                                skip_group_check=True)
                        ins.then_inc(e["pv_made"], 1)

                    for f in range(G * NF + 2):
                        if f < G * NF:
                            scores(f)
                        if more:
                            beside(PE_Q, f, steps)
                        if f >= 2:
                            values(f - 2)

                first = steps_of(b * NG, 0, 0)
                for t in range(NT):
                    first["Q"](t)
                for pair in range(4):
                    kT(pair)
                pe.wait_ge(e["kT_copied"], b * 4 + 4)
                for n in range(4):
                    if n == 2:
                        pe.wait_ge(e["v_made"], b + 1)
                    first["T"](n)
                with pe.Fori(0, NG // 2 - 1) as p2:
                    group(p2 * 2, 0, True)
                    group(p2 * 2 + 1, 1, True)
                group(NG - 2, 0, True)
                group(NG - 1, 1, False)
                pe.wait_ge(e["ao_made"], b * H + H)
                def TA(t):
                    if t >= 2:
                        pe.wait_ge(e["aTl_made"], b * 2 * NT + 2 * (t - 1))
                    for k in range(8):
                        if t == 0 and k == 7:
                            pe.wait_ge(e["ao_made"], b * H + (H + 2))
                        ins = pe.transpose(psS[t % 2][:, k // 4, (k % 4) * P:(k % 4 + 1) * P],
                                           AO[:, t, k * P:(k + 1) * P], ident[:])
                    ins.then_inc(e["aT_made"], 1)

                def Y(t):
                    if t >= 2:
                        pe.wait_ge(e["x_used"], n0 + (t + 1))
                    for h in range(2):
                        pe.wait_ge(e["aTl_made"], b * 2 * NT + (2 * t + h + 1))
                        if t == 0:
                            pe.wait_ge(e[f"wol_in{h}"], 16 * b + 16)
                        for k in range(4):
                            x, kk = AOT[(2 * t + h) % 3], 4 * h + k
                            for j, (s, w) in enumerate(((0, Wo), (0, wol), (1, Wo))):
                                ins = pe.matmul(psO[t % 2][:, 0, :], x[:, s, k, :], w[:, kk, :],
                                                start=(kk + j == 0), stop=(kk == 7 and j == 2))
                        if h == 0:
                            ins.then_inc(e["half_used"], 1)
                    ins.then_inc(e["y_made"], 1)

                def T1(t):
                    pe.wait_ge(e["x_used"], n0 + (t + 3))
                    pe.wait_ge(e["lg_used"], n0 + (t + 1))
                    for k in range(KD):
                        ins = pe.transpose(psO[t % 2][:, 1, k * P:(k + 1) * P], y[t % 2][:, k * P:(k + 1) * P], ident[:])
                    ins.then_inc(e["x1T_made"], 1)

                def lg(t):
                    pe.wait_ge(e["x1T_copied"], n0 + (t + 3))
                    for k in range(KD):
                        ins = pe.matmul(psO[t % 2][:, 1, 0:NE], x1T[t % 2][:, k, :], sb["wtT"][:, k, :],
                                        start=(k == 0), stop=(k == KD - 1))
                    ins.then_inc(e["lg_made"], 1)

                skewed(dict(TA=TA, Y=Y, T1=T1, lg=lg), D_LAG, NT)

        @block.vector
        def _(dve):
            def x_stats(b, t):
                if t % 4 == 0:
                    dve.wait_ge(e[f"xa_in{t // 4}"], b * 16)
                return dve.bn_stats(xst[:, 6 * t:6 * t + 6], xin[:, t, :])

            def x_variance(b, ch, last):
                ch.link(last)
                dve.memset(idle, 0.0)
                for t in range(NT):
                    ins = dve.bn_aggr(xmv[:, 2 * t:2 * t + 2], xst[:, 6 * t:6 * t + 6])
                ch.link(ins)
                dve.tensor_scalar(xve, xvar, LN_EPS, None, ALU.add)\
                    .then_inc(e["var_ready"], 1)

            def x_scale(b, ch):
                dve.wait_ge(e["var_ready"], b)
                dve.wait_ge(e["y0_ready"], b)
                ch.link(newton(dve, ch, xrs, xy0, xve, nt, 1.0))
                assert ch.n == CH_S_V, ch.n

            def normed(tiles):
                for t in tiles:
                    dve.tensor_scalar(xn[t], xin[:, t, :], xmv[:, 2 * t:2 * t + 1], xrs[:, t:t + 1], ALU.subtract, ALU.mult)\
                        .then_inc(e["xn_made"], 1)

            def batch(b, more):
                n0 = value(dve, b * NT)
                ch = Chain(dve, sv[0])
                ch.base = b * CH_A_V
                for u in range(2):
                    dve.wait_ge(e[f"x1_stored{u}"], b * 64 + 16)
                normed(range(4, NT))
                def steps_of(gi, par, bufs=(qn, qn), other=1):
                    m = dve.snap(gi * 2)
                    m2 = dve.snap(gi * 4)
                    cg = Chain(dve, sv[1])
                    cg.base = gi * CH_G_V

                    def red(q):
                        w = slice(q * 8, q * 8 + 8)
                        dve.wait_ge(e["sq_made"], m + (q + 1))
                        cg.link(dve.tensor_reduce(ssq[:, w], bufs[q], AX.X, ALU.add))
                        dve.tensor_scalar(ssq[:, w], ssq[:, w], NORM_EPS ** 2, None, ALU.max).then_inc(e["ssq_made"], 1)

                    def qns(q):
                        w = slice(q * 8, q * 8 + 8)
                        dve.wait_ge(e["ssq_made"], m + (q + 1))
                        dve.wait_ge(e["yq_made"], m + (q + 1))
                        cg.link(newton(dve, cg, rq[:, w], yq[:, w], ssq[:, w], nq, float(2 ** (LIFT // 2))))
                        dve.tensor_tensor(bufs[q], psO[1][:, q, :].rearrange("p (n d) -> p n d", d=DH),
                                          rq[:, w].unsqueeze(2).to_broadcast([P, 8, DH]), ALU.mult)\
                            .then_inc(e["qn_made"], 1)

                    def cpq(q):
                        dve.wait_ge(e["qT_made"], m2 + (2 * q + 4))
                        dve.tensor_copy(QT[:, par, :, (4 * q + 2) * P:(4 * q + 4) * P],
                                        psO[other][:, q, :].rearrange("p (h t) -> p h t", h=G))\
                            .then_inc(e["qTv_copied"], 1)

                    return dict(red=red, qn=qns, cp=cpq)

                def group(g, par, more):
                    gi = b * NG + g
                    m0 = dve.snap(gi * G)
                    f0 = dve.snap(gi * (G * NF))
                    steps = steps_of(gi + 1, 1 - par) if more else None
                    dve.tensor_tensor(pz, snull[:, :, bass.ds(g * G, G)], rq.rearrange("p (t h) -> p t h", h=G),
                                      ALU.mult).then_inc(e["nz_made"], 1)

                    def weigh(f):
                        hh, k = f // NF, f % NF
                        dve.wait_ge(e["exp_made"], f0 + (f + 3))
                        for j, c0 in FILLS[k]:
                            w = width(j)
                            ins = dve.tensor_tensor(E[f % 3][:, c0:c0 + w], E[f % 3][:, c0:c0 + w],
                                                    sb["EB"][:, bass.ds(g * G + hh, 1), 0:w].rearrange("p a w -> p (a w)"),
                                                    ALU.mult)
                        ins.then_inc(e["p_made"], 1)

                    def total(hh):
                        u = hh % 2
                        dve.wait_ge(e["pv_made"], f0 + (hh * NF + NF + 2))
                        dve.wait_ge(e["nul_made"], m0 + (hh + 1))
                        dve.wait_ge(e["ao_made"], m0 + (hh + 1))
                        for i in range(2):
                            ins = dve.tensor_tensor(num[u][:, 4 * i:4 * i + 4, :],
                                                    psO[0][:, i, 0:4 * VW].rearrange("p (t d) -> p t d", d=VW),
                                                    nul[:, 4 * i:4 * i + 4, :], ALU.add)
                        ins.then_inc(e["num_made"], 1)
                        dve.wait_ge(e["num_made"], m0 + (hh + 3))
                        dve.reciprocal(rec[u].unsqueeze(2), num[u][:, :, DH:VW]).then_inc(e["rec_made"], 1)

                    for f in range(G * NF):
                        weigh(f)
                        if f == 0:
                            dve.wait_ge(e["nexp_made"], gi + 1)
                            dve.tensor_tensor(pn, pe_, sb["enull"][:, bass.ds(g * G, G)].unsqueeze(1)
                                              .to_broadcast([P, NT, G]), ALU.mult).then_inc(e["pn_made"], 1)
                        if f == NF:
                            total(0)
                        if more:
                            beside(DVE_Q, f, steps)
                    total(1)

                for i, bank in enumerate(kv_banks):
                    t0, t1 = 3 * i, min(3 * i + 3, NT)
                    dve.wait_ge(e["kv_made"], n0 + t1)
                    ins = dve.tensor_copy(kvs[:, t0:t1, :], bank[:, 0:(t1 - t0) * KVW].rearrange("p (t n) -> p t n", n=KVW))
                ins.then_inc(e["kv_copied"], 1)
                dve.wait_ge(e["ksq_made"], b + 1)
                ch.link(dve.tensor_reduce(ssk, ksq, AX.X, ALU.add))
                dve.tensor_scalar(ssc, ssk, NORM_EPS ** 2, None, ALU.max).then_inc(e["ssk_clamped"], 1)
                dve.wait_ge(e["ssk_clamped"], b + 1)
                dve.wait_ge(e["yk_ready"], b + 1)
                ch.link(newton(dve, ch, rk, yk, ssc, nt, float(2 ** (LIFT // 2))))
                first = steps_of(b * NG, 0, qn_first, 0)
                first["red"](0)
                ch.link(dve.tensor_tensor(knr, kvs[:, :, 0:DH], rk.unsqueeze(2).to_broadcast([P, NT, DH]), ALU.mult))
                ch.link(dve.tensor_tensor(knr, knr, sb["kfac"][:].unsqueeze(1).to_broadcast([P, NT, DH]), ALU.mult))

                def keys(half):
                    if half:
                        dve.wait_ge(e["kT_made"], b * 4 + 2)
                    kh = knr[:, 4 * half:4 * half + 4, :]
                    for r in range(2):
                        ins = dve.tensor_copy(kst[:, :, 0, r], kh)
                    ch.link(ins)
                    for r in range(2):
                        ins = dve.tensor_tensor(kst[:, :, 1, r], kh, kst[:, :, 0, r].bitcast(F32), ALU.subtract)
                    ins.then_inc(e["kst_made"], 1)

                keys(0)
                first["qn"](0)
                keys(1)
                assert ch.n == CH_A_V, ch.n
                first["red"](1)
                first["qn"](1)
                mask = sb["maskf"][:, bass.ds(n0, NT)].unsqueeze(2)
                dve.tensor_tensor(V[:, :, 0:DH], kvs[:, :, DH:2 * DH], mask.to_broadcast([P, NT, DH]), ALU.mult)
                dve.tensor_copy(V[:, :, DH:VW], mask)
                dve.tensor_copy(snull, kvs[:, :, 2 * DH:]).then_inc(e["v_made"], 1)
                first["cp"](0)
                first["cp"](1)
                with dve.Fori(0, NG // 2 - 1) as p2:
                    group(p2 * 2, 0, True)
                    group(p2 * 2 + 1, 1, True)
                group(NG - 2, 0, True)
                group(NG - 1, 1, False)
                cd = Chain(dve, sv[2])
                cd.base = b * CH_D_V

                def cpa(t):
                    for h in range(2):
                        g = 2 * t + h
                        dve.wait_ge(e["aTh_made"], b * 2 * NT + (g + 1))
                        dve.tensor_tensor(AOT[g % 3][:, 1].rearrange("p k t -> p (k t)"), psS[t % 2][:, h, :],
                                          AOT[g % 3][:, 0].rearrange("p k t -> p (k t)").bitcast(F32), ALU.subtract)\
                            .then_inc(e["aTl_made"], 1)

                def std(t):
                    u = t % 2
                    dve.wait_ge(e["y_made"], n0 + (t + 3))
                    cd.link(dve.bn_stats(st[u], psO[u][:, 0, :]))
                    dve.memset(idle, 0.0)
                    cd.link(dve.bn_aggr(mv[u], st[u]))
                    dve.tensor_scalar(ve[:, t:t + 1], mv[u][:, 1:2], LN_EPS, None, ALU.add).then_inc(e["var2_ready"], 1)

                def nrm(t):
                    u = t % 2
                    dve.wait_ge(e["var2_ready"], n0 + (t + 1))
                    dve.wait_ge(e["y02_ready"], n0 + (t + 1))
                    cd.link(newton(dve, cd, rs[:, t:t + 1], y0[:, t:t + 1], ve[:, t:t + 1], nt[:, t:t + 1], 1.0))
                    dve.wait_ge(e[f"x1_stored{u}"], b * 64 + 16 * (t // 2 + 1))
                    dve.wait_ge(e["x1T_made"], n0 + (t + 1))
                    cd.link(dve.tensor_scalar(y[u], psO[u][:, 0, :], mv[u][:, 0:1], rs[:, t:t + 1], ALU.subtract, ALU.mult))
                    cd.link(dve.tensor_tensor(y[u], y[u], sb["gout"][:], ALU.mult))
                    dve.wait_ge(e[f"x_in{u}"], b * 64 + 16 * (t // 2 + 1))
                    dve.tensor_tensor(y[u], y[u], xt[:, u, :], ALU.add).then_inc(e["x_used"], 1)

                def lgc(t):
                    dve.wait_ge(e["lg_made"], n0 + (t + 3))
                    dve.tensor_tensor(LG[:, bass.ds(n0 + t, 1), :].rearrange("p a n -> p (a n)"), psO[t % 2][:, 1, 0:NE],
                                      sb["glog"][:, bass.ds(b, 1), :].rearrange("p a n -> p (a n)"), ALU.add)\
                        .then_inc(e["lg_used"], 1)

                steps = dict(cp=cpa, st=std, nrm=nrm, lgc=lgc)
                if more:
                    chS = Chain(dve, sv[3])
                    chS.base = b * CH_S_V
                    last = []

                    def xs(t):
                        last[:] = [x_stats(b + 1, t)]

                    def xv(t):
                        if t == NT - 1:
                            x_variance(b + 1, chS, last[0])

                    def xr(t):
                        if t == NT - 1:
                            x_scale(b + 1, chS)

                    def xn_(t):
                        if t == NT - 1:
                            dve.wait_ge(e["y_made"], n0 + (NT + 2))
                            normed(range(4))

                    steps.update(xs=xs, xv=xv, xr=xr, xn=xn_)
                skewed(steps, D_LAG, NT)
                assert cd.n == CH_D_V, cd.n

            normed(range(4))
            with dve.Fori(0, B - 1) as b:
                batch(b, True)
            batch(B - 1, False)


def pipelined(eng, phases, lags):
    deep = max(lags[n] for steps, _, _ in phases for n in steps)
    before = None

    def round_(phase, before, i, r):
        for lag in range(deep, -1, -1):
            whose, t = phase, i - lag
            if isinstance(i, int) and t < 0:
                if before is None:
                    continue
                whose, t = before, before[1] + t
            if whose is None or isinstance(t, int) and t >= whose[1]:
                continue
            for n in whose[0]:
                if lags[n] == lag:
                    whose[0][n](t, (t if isinstance(t, int) else r - lag) % whose[2])

    for phase in phases:
        steps, count, unroll = phase
        head = -(-deep // unroll) * unroll
        for i in range(head):
            round_(phase, before, i, i)
        with eng.Fori(head // unroll, count // unroll) as q:
            for r in range(unroll):
                round_(phase, before, q * unroll + r, r)
        before = phase
    for i in range(deep):
        round_(None, before, i, i)


def value(eng, x):
    return x if isinstance(x, int) else eng.snap(x)


MOE_CREDITS = dict(xl_made=2, xT_made=2, xT_copied=2, g_used=2, hT_made=2, h_copied=1, dn_made=2, yo_made=4, noted=1)


def experts(nc, a, sb, dr, sem, out):
    LG = sb["LG"]
    with ExitStack() as ctx:
        def tile(name, shape, dt=F32):
            return ctx.enter_context(nc.sbuf_tensor("m_" + name, shape, dt))

        def psum(name):
            return ctx.enter_context(nc.psum_tensor("m_" + name, [P, 512], F32))

        wgu = tile("wgu", [P, NE, KD, 2 * MD])
        wd = tile("wd", [P, NE, MD // P, D])
        sguh, sgul = (tile(n, [P, KD, 2 * SMD], F32R) for n in ("sguh", "sgul"))
        sdh, sdl = (tile(n, [P, SMD // P, D], F32R) for n in ("sdh", "sdl"))
        stage = wgu[:, 0:3].rearrange("p e k n -> p (e k n)")
        sgu = stage[:, 0:KD * 2 * SMD].rearrange("p (k n) -> p k n", k=KD)
        sd = stage[:, KD * 2 * SMD:KD * 2 * SMD + SMD // P * D].rearrange("p (k n) -> p k n", n=D)
        ident = tile("ident", [P, P])
        upper = tile("upper", [P, P])
        ones = tile("ones", [P, P])
        xr = tile("xr", [P, 4, D])
        xTh, xTl = (tile(n, [P, 2, KD, P], F32R) for n in ("xTh", "xTl"))
        lh = tile("lh", [P, 2, SMD])
        hTh, hTl = (tile(n, [P, 2, SMD // P, P], F32R) for n in ("hTh", "hTl"))
        yo = tile("yo", [P, 2, D])
        xq = tile("xq", [P, 4, D])
        xe = xq[:, 0:2, :]
        late = tile("late", [P, 8, D])
        y1, y2, z1, z2 = (late[:, 2 * i:2 * i + 2, :] for i in range(4))
        flat = late[:].rearrange("p a n -> p (a n)")
        xT = flat[:, 4 * D:6 * D].rearrange("p (u k t) -> p u k t", u=2, t=P)
        hT = flat[:, 6 * D:7 * D].rearrange("p (u k t) -> p u k t", u=2, t=P)
        te = NTT * NE

        def scratch(i):
            return flat[:, i * te:(i + 1) * te].rearrange("p (t e) -> p t e", e=NE)
        psA = [psum(f"A{i}") for i in range(2)]
        psG = [psum(f"G{i}") for i in range(2)]
        psU = [psum(f"U{i}") for i in range(2)]
        psH, psY = psum("H"), psum("Y")

        z = scratch(0)
        t8 = scratch(1)
        ix = scratch(7).bitcast(U32)
        ixf = tile("ixf", [P, NTT, 2])
        o1 = scratch(2)
        o2 = scratch(3)
        cnt = scratch(4)
        tot = scratch(5)
        inc = scratch(6)
        col = tile("col", [P, NTT, 2])
        wts = tile("wts", [P, NTT, 2])
        i8 = tile("i8", [P, NE])
        pad = tile("pad", [P, NE])
        padi = tile("padi", [P, NE], I32)
        end = tile("end", [P, NE])
        first = tile("first", [P, NE])
        slot = tile("slot", [P, SLOTS])
        ge = tile("ge", [P, SLOTS, NE])
        sle = tile("sle", [P, SLOTS])
        slei = tile("slei", [P, SLOTS], I32)
        posu = tile("posu", [P, NTT, 2], U32)
        ib = tile("ib", [P, 4, 2, 2], U32)
        gb = tile("gb", [P, 4, 2, 2], U32)
        note = tile("note", [P, 1])

        c = {n: sem("m_" + n) for n in MOE_CREDITS}
        names = ("rv", "ez", "consts", "cnt_made", "pre_made", "pos_made", "w_shared", "w_hi", "w_lo", "hh_made",
                 "w_exp", "gu_made", "t_made", "l_made", "ib_made", "gb_made", "sum_made", "half_made",
                 "fin_half", "fin_made")
        e = {n: sem("m_" + n) for n in names}
        x_in, q_in, z_in = ([sem(f"m_{n}_in{i}") for i in range(4)] for n in "xqz")
        scat = [sem(f"m_scat{i}") for i in range(4)]
        y_st = [sem(f"m_y_st{i}") for i in range(2)]
        s_in = [sem(f"m_s_in{i}") for i in range(2)]
        y_out = [sem(f"m_y_out{i}") for i in range(2)]
        b_in = [sem(f"m_b_in{i}") for i in range(4)]
        g_in = [sem(f"m_g_in{i}") for i in range(4)]
        o_out = [sem(f"m_o_out{i}") for i in range(4)]
        block = ctx.enter_context(nc.Block())

        def rows(ap, i):
            return ap[bass.ds(i * P, P), :]

        x1, base, xs, ys, o = dr["x1"], dr["base"], dr["xs"], dr["ys"], out

        LAG = dict(load=0, scat=0, T=0, xTc=0, gu=1, tl=1, lh=1, T2=2, hTc=2, dn=3, yc=3, store=4, gind=1, tot=3, xl=0)

        @block.sync
        def _(sp):
            sp.dma_start(sgu[:, :, 0:SMD], a["sw_gate"].rearrange("(k p) n -> p k n", p=P)).then_inc(e["w_shared"], 16)
            sp.dma_start(sgu[:, :, SMD:], a["sw_up"].rearrange("(k p) n -> p k n", p=P)).then_inc(e["w_shared"], 16)
            sp.dma_start(sd[:], a["sw_down"].rearrange("(k p) n -> p k n", p=P)).then_inc(e["w_shared"], 16)

            def load(i, r):
                src, src2 = rows(x1, i), rows(x1, i + NS)
                n, m = value(sp, (i - r) * 16), value(sp, i + 1)
                if not isinstance(n, int) or n > 0:
                    sp.wait_ge(scat[r], n)
                sp.dma_start(xq[:, r, :], src2).then_inc(q_in[r], 16)
                sp.wait_ge(c["yo_made"], m)
                sp.dma_start(xr[:, r, :], src).then_inc(x_in[r], 16)

            def store(i, r):
                dst = rows(base, i)
                n = value(sp, i + 5)
                sp.wait_ge(c["yo_made"], n)
                sp.dma_start(dst, yo[:, r % 2, :]).then_inc(y_st[r % 2], 16)

            def weights(i, r):
                if isinstance(i, int):
                    if i < 3:
                        return
                    units = range(4)
                else:
                    units = (i,)
                for u in units:
                    moves = []
                    for w, at in (("w_gate", 0), ("w_up", MD)):
                        src = a[w].rearrange("e (h k p) n -> (e h) p k n", h=2, p=P)[bass.ds(u, 1)]
                        dst = wgu[:].rearrange("p e (h k) n -> p (e h) k n", h=2)[:, bass.ds(u, 1), :, at:at + MD]
                        moves.append((dst.rearrange("p a k n -> p (a k) n"), src.rearrange("a p k n -> p (a k) n")))
                    src = a["w_down"].rearrange("e (k p) n -> (e k) p n", p=P)[bass.ds(u, 1)]
                    dst = wd[:].rearrange("p e k n -> p (e k) n")[:, bass.ds(u, 1)]
                    moves.append((dst, src.rearrange("a p n -> p a n")))
                    for n, (dst, src) in enumerate(moves):
                        if n == 0 and isinstance(u, int) and u == 0:
                            sp.wait_ge(e["w_lo"], KD + 1)
                        sp.dma_start(dst, src).then_inc(e["w_exp"], 16)

            def loads(i, r):
                src = rows(xs, i)
                n = value(sp, i + (NS + 1))
                if isinstance(i, int) and i == 0:
                    for q in range(4):
                        sp.wait_ge(scat[q], 64 * (NS // 4))
                sp.wait_ge(c["xT_made"], n)
                sp.dma_start(xe[:, r % 2, :], src).then_inc(s_in[r % 2], 16)

            def stores(i, r):
                dst = rows(ys, i)
                n = value(sp, i + (NS + 5))
                sp.wait_ge(c["yo_made"], n)
                sp.dma_start(dst, yo[:, r % 2, :]).then_inc(y_out[r % 2], 16)

            def last_loads(i, r):
                src, src2 = rows(x1, i + NS), rows(base, i)
                n, m = value(sp, i + (NS + SLOTS)), value(sp, (i - r) * 4 + 16)
                if not isinstance(i, int) or i >= 4:
                    sp.wait_ge(c["yo_made"], n)
                else:
                    sp.wait_ge(c["yo_made"], NS + 4)
                sp.dma_start(xr[:, r, :], src).then_inc(x_in[r], 16)
                if isinstance(i, int) and i < 4:
                    sp.wait_ge(c["xT_made"], NS + SLOTS + 2)
                    sp.wait_ge(y_st[i % 2], 16 * (NS // 2 + 1))
                sp.wait_ge(o_out[r], m)
                sp.dma_start(xq[:, r, :], src2).then_inc(b_in[r], 16)

            def last_stores(i, r):
                dst, dst2 = rows(o, i + NS), rows(o, i)
                n = value(sp, i + 1)
                sp.wait_ge(e["fin_made"], n)
                sp.dma_start(dst, yo[:, r % 2, :]).then_inc(y_st[r % 2], 16)
                sp.wait_ge(e["sum_made"], n)
                sp.dma_start(dst2, xq[:, r, :]).then_inc(o_out[r], 16)

            pipelined(sp, [(dict(load=load, scat=weights, store=store), NS, 4),
                           (dict(load=loads, store=stores), SLOTS, 2),
                           (dict(load=last_loads, store=last_stores), NS, 4)], LAG)
            for r in range(2):
                sp.wait_ge(y_st[r], 16 * (NS + 1))
            for r in range(4):
                sp.wait_ge(o_out[r], 16 * (NS // 4 + 1))

        @block.gpsimd
        def _(pool):
            col_ = 0
            for name, n in MOE_CREDITS.items():
                pool.memset(sb["credit"][:, col_:col_ + 1], 0.0).then_inc(c[name], n)
                col_ += 1
            for q in y_st + y_out + o_out:
                pool.memset(sb["credit"][:, col_:col_ + 1], 0.0).then_inc(q, 16)
                col_ += 1
            pool.memset(ident[:], 0.0).then_inc(e["consts"], 1)
            pool.memset(upper[:], 1.0).then_inc(e["consts"], 1)
            pool.memset(ones[:], 1.0).then_inc(e["consts"], 1)
            pool.wait_ge(e["consts"], 3)
            pool.affine_select(out=ident[:], in_=ident[:], compare_op=ALU.not_equal, fill=1.0, base=0,
                               pattern=[[-1, P]], channel_multiplier=1).then_inc(e["consts"], 1)
            pool.affine_select(out=upper[:], in_=upper[:], compare_op=ALU.is_gt, fill=0.0, base=0,
                               pattern=[[1, P]], channel_multiplier=-1).then_inc(e["consts"], 1)
            pool.iota(i8[:], [[1, NE]], base=0, channel_multiplier=0,
                      allow_small_or_imprecise_dtypes=True).then_inc(e["consts"], 1)
            pool.iota(slot[:], [[P, SLOTS]], base=0, channel_multiplier=0,
                      allow_small_or_imprecise_dtypes=True).then_inc(e["consts"], 1)
            for k in range(KD):
                pool.wait_ge(e["w_hi"], k + 1)
                pool.tensor_tensor(sgul[:, k, :], sgu[:, k, :], sguh[:, k, :].bitcast(F32), ALU.subtract).then_inc(e["w_lo"], 1)
            pool.wait_ge(e["w_hi"], KD + 1)
            pool.tensor_tensor(sdl[:], sd, sdh[:].bitcast(F32), ALU.subtract).then_inc(e["w_lo"], 1)

            def held(n):
                pool.wait_ge(c["noted"], n + 1)
                pool.tensor_tensor(note[:], ones[:, 0:1], ones[:, 0:1], ALU.add).then_inc(c["noted"], 1)

            def scatter(i, r):
                pool.wait_ge(x_in[r], (i - r) * 4 + 16)
                pool.wait_ge(q_in[r], (i - r) * 4 + 16)
                pool.wait_ge(e["ib_made"], i + 1)
                held(i)
                for h, x in enumerate((xr, xq)):
                    for w in range(2):
                        pool.indirect_dma_start(out=xs, in_=x[:, r, :], in_offset=None, out_offset=bass
                                                .IndirectOffsetOnAxis(ap=ib[:, r, h, w:w + 1], axis=0))\
                            .then_inc(scat[r], 16)

            pipelined(pool, [(dict(scat=scatter), NS, 4)], LAG)
            for r in range(2):
                pool.wait_ge(y_out[r], 16 * (SLOTS // 2 + 1))

            def gather(i, r):
                pool.wait_ge(e["gb_made"], i + 1)
                held(i + NS)
                for h, ys_, q in ((0, (z1, z2), z_in), (1, (y1, y2), g_in)):
                    for w, y in enumerate(ys_):
                        pool.indirect_dma_start(out=y[:, r % 2, :], out_offset=None, in_=ys, in_offset=bass
                                                .IndirectOffsetOnAxis(ap=gb[:, r, h, w:w + 1], axis=0))\
                            .then_inc(q[r], 16)

            pipelined(pool, [(dict(scat=gather), NS, 4)], LAG)

        @block.scalar
        def _(act):
            act.wait_ge(e["rv"], 2)
            act.activation(z, z, ACT.Exp, scale=0.5).then_inc(e["ez"], 1)

            act.wait_ge(e["w_shared"], 48)
            for k in range(KD):
                act.activation(sguh[:, k, :], sgu[:, k, :], ACT.Copy).then_inc(e["w_hi"], 1)
            act.activation(sdh[:], sd, ACT.Copy).then_inc(e["w_hi"], 1)

            def stages(off, count, unroll, shared):
                n = SMD if shared else MD

                def xTc(i, r):
                    act.wait_ge(c["xT_made"], i + (off + 3))
                    act.wait_ge(c["g_used"], i + (off + 1))
                    act.activation((xTh if shared else xT)[:, r % 2].rearrange("p k t -> p (k t)"), psA[r % 2][:], ACT.Copy)\
                        .then_inc(c["xT_copied"], 1)

                def tls(i, r):
                    act.wait_ge(e["gu_made"], i + (off + 1))
                    act.wait_ge(c["hT_made"], i + (off + 1))
                    act.activation(lh[:, r % 2, 0:n], psG[r % 2][:, 0:n], ACT.Copy, scale=0.01).then_inc(e["t_made"], 1)

                def yc(i, r):
                    act.wait_ge(c["dn_made"], i + (off + 3))
                    if isinstance(i, int) and i < 2:
                        act.wait_ge(y_st[i], 16 * (NS // 2 + 1))
                    act.wait_ge(y_out[r % 2], (i - r) * 8 + 16 * (1 + r // 2))
                    act.activation(yo[:, r % 2, :], psY[:], ACT.Copy).then_inc(c["yo_made"], 1)

                def hh(i, r):
                    act.wait_ge(c["hT_made"], i + (off + 3))
                    act.wait_ge(c["dn_made"], i + (off + 1))
                    act.activation(hTh[:, r % 2].rearrange("p k t -> p (k t)"), psH[:], ACT.Copy).then_inc(e["hh_made"], 1)

                steps = dict(xTc=xTc, tl=tls)
                if shared:
                    steps["hTc"] = hh
                else:
                    steps["yc"] = yc
                return steps, count, unroll

            pipelined(act, [stages(0, NS, 4, True), stages(NS, SLOTS, 2, False), stages(NS + SLOTS, NS, 4, True)], LAG)

        @block.tensor
        def _(pe):
            pe.wait_ge(e["consts"], 7)
            pe.wait_ge(e["cnt_made"], 1)
            pe.matmul(psH[:, 0:NTT * NE], upper[:], cnt.rearrange("p t e -> p (t e)"), start=True, stop=True)\
              .then_inc(e["pre_made"], 1)
            pe.matmul(psY[:, 0:NTT * NE], ones[:], cnt.rearrange("p t e -> p (t e)"), start=True, stop=True)\
              .then_inc(e["pre_made"], 1)

            def product(out, x, w):
                kn = len(x[0])
                for k in range(kn):
                    for j, (a_, b_) in enumerate(((0, 0), (0, 1), (1, 0))):
                        ins = pe.matmul(out, x[a_][k], w[b_][k], start=(k + j == 0), stop=(k == kn - 1 and j == 2))
                return ins

            def stages(off, count, unroll, shared):
                soff = NS if off else 0
                kh = (SMD if shared else MD) // P
                picked = []

                def expert(i):
                    return pe.value_load(slei[0:1, bass.ds(i, 1)], min_val=0, max_val=NE - 1)

                def T(i, r):
                    x = xr[:, r, :] if shared else xe[:, r % 2, :]
                    if shared:
                        pe.wait_ge(x_in[r], (i - r) * 4 + (16 + (4 * NS if off else 0)))
                    else:
                        pe.wait_ge(s_in[r % 2], (i - r) * 8 + 16)
                    pe.wait_ge(c["xT_copied"], i + (off + 1))
                    if shared:
                        pe.wait_ge(c["xl_made"], i + (soff + 1))
                    for k in range(KD):
                        ins = pe.transpose(psA[r % 2][:, k * P:(k + 1) * P], x[:, k * P:(k + 1) * P], ident[:])
                    ins.then_inc(c["xT_made"], 1)

                def gu(i, r):
                    u = r % 2
                    if shared:
                        if off == 0 and isinstance(i, int) and i == 0:
                            pe.wait_ge(e["w_lo"], KD)
                        pe.wait_ge(c["xl_made"], i + (soff + 3))
                    else:
                        if isinstance(i, int) and i == 0:
                            pe.wait_ge(e["w_exp"], 48 * NE)
                        pe.wait_ge(c["xT_copied"], i + (off + 3))
                    pe.wait_ge(c["g_used"], i + (off + 1))
                    if shared:
                        for half, ps in enumerate((psG[u], psU[u])):
                            n = slice(half * SMD, (half + 1) * SMD)
                            ins = product(ps[:], [[x[:, u, k, :] for k in range(KD)] for x in (xTh, xTl)],
                                          [[w[:, k, n] for k in range(KD)] for w in (sguh, sgul)])
                    else:
                        x = picked.pop() if picked else expert(i)
                        for k in range(KD):
                            ins = pe.matmul(psG[u][:], xT[:, u, k, :],
                                            wgu[:, bass.ds(x, 1), k, :].rearrange("p a n -> p (a n)"),
                                            start=(k == 0), stop=(k == KD - 1))
                    ins.then_inc(e["gu_made"], 1)

                def T2(i, r):
                    u = r % 2
                    if off == 0 and isinstance(i, int) and i == 0:
                        pe.wait_ge(e["pos_made"], 1)
                        pe.wait_ge(e["w_lo"], KD + 1)
                    pe.wait_ge(c["g_used"], i + (off + 3))
                    pe.wait_ge(c["h_copied"], i + (off + 1))
                    for k in range(kh):
                        ins = pe.transpose(psH[:, k * P:(k + 1) * P], lh[:, u, k * P:(k + 1) * P], ident[:])
                    ins.then_inc(c["hT_made"], 1)

                def dn(i, r):
                    u = r % 2
                    pe.wait_ge(c["h_copied"], i + (off + 2))
                    pe.wait_ge(c["yo_made"], i + (off + 4))
                    if not shared:
                        x = expert(i)
                        if not isinstance(i, int) or i + 2 < count:
                            picked.append(expert(i + 2))
                    if shared:
                        ins = product(psY[:], [[y[:, u, k, :] for k in range(kh)] for y in (hTh, hTl)],
                                      [[w[:, k, :] for k in range(kh)] for w in (sdh, sdl)])
                    else:
                        for k in range(kh):
                            ins = pe.matmul(psY[:], hT[:, u, k, :], wd[:, bass.ds(x, 1), k, :].rearrange("p a n -> p (a n)"),
                                            start=(k == 0), stop=(k == kh - 1))
                    ins.then_inc(c["dn_made"], 1)

                return dict(T=T, gu=gu, T2=T2, dn=dn), count, unroll

            pipelined(pe, [stages(0, NS, 4, True), stages(NS, SLOTS, 2, False), stages(NS + SLOTS, NS, 4, True)], LAG)

        @block.vector
        def _(dve):
            ch = Chain(dve, e["rv"])
            m, s = col[:, :, 0], col[:, :, 1]

            def per_tile(ap):
                return ap.unsqueeze(2).to_broadcast([P, NTT, NE])

            ch.link(dve.tensor_reduce(m, LG[:], AX.X, ALU.max))
            ch.link(dve.tensor_tensor(z, LG[:], per_tile(m), ALU.subtract))
            dve.wait_ge(e["ez"], 1)
            ch.link(dve.tensor_reduce(s, z, AX.X, ALU.add))
            ch.link(dve.reciprocal(m, s))
            ch.link(dve.tensor_tensor(z, z, per_tile(m), ALU.mult))
            for t in range(NTT):
                ins = dve.max(t8[:, t, :], z[:, t, :])
            ch.link(ins)
            for t in range(NTT):
                ins = dve.max_index(ix[:, t, :], t8[:, t, :], z[:, t, :])
            ch.link(ins)
            ch.link(dve.tensor_copy(ixf[:], ix[:, :, 0:2]))
            dve.wait_ge(e["consts"], 7)
            e8 = i8[:].unsqueeze(1).to_broadcast([P, NTT, NE])
            for w, oh in enumerate((o1, o2)):
                ins = dve.tensor_tensor(oh, per_tile(ixf[:, :, w]), e8, ALU.is_equal)
            ch.link(ins)
            dve.tensor_tensor(cnt, o1[:], o2[:], ALU.add).then_inc(e["cnt_made"], 1)
            ch.link(dve.tensor_tensor(s, t8[:, :, 0], t8[:, :, 1], ALU.add))
            ch.link(dve.tensor_scalar(s, s, 1e-20, None, ALU.add))
            ch.link(dve.reciprocal(m, s))
            ch.link(dve.tensor_tensor(wts[:], t8[:, :, 0:2], m.unsqueeze(2).to_broadcast([P, NTT, 2]), ALU.mult))
            dve.wait_ge(e["pre_made"], 2)
            ch.link(dve.tensor_copy(tot.rearrange("p t e -> p (t e)"), psY[:, 0:NTT * NE]))
            for x in range(NE):
                ins = dve.tensor_tensor_scan(inc[:, :, x], ones[:, 0:NTT], tot[:, :, x], 0.0, ALU.mult, ALU.add)
            ch.link(ins)
            ch.link(dve.tensor_scalar(pad[:], inc[:, NTT - 1, :], float(P - 1), None, ALU.add))
            ch.link(dve.tensor_copy(padi[:], pad[:]))
            sh = P.bit_length() - 1
            ch.link(dve.tensor_scalar(padi[:], padi[:], sh, sh, ALU.logical_shift_right, ALU.logical_shift_left))
            ch.link(dve.tensor_copy(pad[:], padi[:]))
            ch.link(dve.tensor_tensor_scan(end[:], ones[:, 0:NE], pad[:], 0.0, ALU.mult, ALU.add))
            ch.link(dve.tensor_tensor(first[:], end[:], pad[:], ALU.subtract))
            ch.link(dve.tensor_tensor(inc, inc, tot, ALU.subtract))
            ch.link(dve.tensor_tensor(inc, inc, first[:].unsqueeze(1).to_broadcast([P, NTT, NE]), ALU.add))
            ch.link(dve.tensor_tensor(inc.rearrange("p t e -> p (t e)"), psH[:, 0:NTT * NE],
                                      inc.rearrange("p t e -> p (t e)"), ALU.add))
            for w, oh in enumerate((o1, o2)):
                ch.link(dve.tensor_tensor(oh, oh, inc, ALU.mult))
                ch.link(dve.tensor_reduce(ixf[:, :, w], oh, AX.X, ALU.add))
            ch.link(dve.tensor_copy(posu[:], ixf[:]))
            ch.link(dve.tensor_tensor(ge[:], slot[:].unsqueeze(2).to_broadcast([P, SLOTS, NE]),
                                      end[:].unsqueeze(1).to_broadcast([P, SLOTS, NE]), ALU.is_ge))
            ch.link(dve.tensor_reduce(sle[:], ge[:], AX.X, ALU.add))
            ch.link(dve.tensor_scalar(sle[:], sle[:], float(NE - 1), None, ALU.min))
            dve.tensor_copy(slei[:], sle[:]).then_inc(e["pos_made"], 1)

            def stages(off, count, unroll, shared):
                n = SMD if shared else MD
                soff = NS if off else 0

                def index(i, r):
                    if not isinstance(i, int) or i >= 4:
                        dve.wait_ge(scat[r], (i - r) * 16)
                    for h in range(2):
                        ins = dve.tensor_copy(ib[:, r, h, :],
                                              posu[:, bass.ds(i + h * NS, 1), :].rearrange("p a w -> p (a w)"))
                    ins.then_inc(e["ib_made"], 1)

                def gindex(i, r):
                    if not isinstance(i, int) or i >= 4:
                        dve.wait_ge(z_in[r], (i - r) * 8)
                        dve.wait_ge(g_in[r], (i - r) * 8)
                    if not isinstance(i, int) or i >= 2:
                        dve.wait_ge(e["sum_made"], i - 1)
                    for h in range(2):
                        ins = dve.tensor_copy(gb[:, r, h, :],
                                              posu[:, bass.ds(i + h * NS, 1), :].rearrange("p a w -> p (a w)"))
                    ins.then_inc(e["gb_made"], 1)

                def lhs(i, r):
                    u = r % 2
                    up = psU[u][:, 0:n] if shared else psG[u][:, MD:2 * MD]
                    dve.wait_ge(e["t_made"], i + (off + 1))
                    dve.tensor_tensor(lh[:, u, 0:n], psG[u][:, 0:n], lh[:, u, 0:n], ALU.max).then_inc(e["l_made"], 1)
                    dve.wait_ge(e["l_made"], i + (off + 1))
                    dve.tensor_tensor(lh[:, u, 0:n], up, lh[:, u, 0:n], ALU.mult).then_inc(c["g_used"], 1)

                def xl(i, r):
                    u = r % 2
                    dve.wait_ge(c["xT_copied"], i + (off + 3))
                    dve.tensor_tensor(xTl[:, u].rearrange("p k t -> p (k t)"), psA[u][:],
                                      xTh[:, u].rearrange("p k t -> p (k t)").bitcast(F32), ALU.subtract)\
                        .then_inc(c["xl_made"], 1)

                def hl(i, r):
                    u = r % 2
                    dve.wait_ge(e["hh_made"], i + (soff + 1))
                    dve.tensor_tensor(hTl[:, u].rearrange("p k t -> p (k t)"), psH[:],
                                      hTh[:, u].rearrange("p k t -> p (k t)").bitcast(F32), ALU.subtract)\
                        .then_inc(c["h_copied"], 1)

                def hTc(i, r):
                    dve.wait_ge(c["hT_made"], i + (off + 3))
                    dve.wait_ge(c["dn_made"], i + (off + 1))
                    dve.tensor_copy(hT[:, r % 2].rearrange("p k t -> p (k t)")[:, 0:n], psH[:, 0:n])\
                       .then_inc(c["h_copied"], 1)

                def add(i, r):
                    done = 8 * NS if off else 0
                    dve.wait_ge(c["dn_made"], i + (off + 3))
                    if off and isinstance(i, int) and i < 2:
                        dve.wait_ge(y_out[i], 16 * (SLOTS // 2 + 1))
                    dve.wait_ge(y_st[r % 2], (i - r) * 8 + (16 * (1 + r // 2) + done))
                    dve.tensor_tensor(yo[:, r % 2, :], psY[:], xr[:, r, :], ALU.add).then_inc(c["yo_made"], 1)

                def weighted(x, y, w, half, whole, i):
                    dve.scalar_tensor_tensor(out=x, in0=y[0], scalar=w[:, 0:1], in1=x, op0=ALU.mult, op1=ALU.add)\
                       .then_inc(e[half], 1)
                    dve.wait_ge(e[half], i + 1)
                    dve.scalar_tensor_tensor(out=x, in0=y[1], scalar=w[:, 1:2], in1=x, op0=ALU.mult, op1=ALU.add)\
                       .then_inc(e[whole], 1)

                def last_add(i, r):
                    add(i, r)
                    w = wts[:, bass.ds(i + NS, 1), :].rearrange("p a w -> p (a w)")
                    dve.wait_ge(c["yo_made"], i + (off + 5))
                    dve.wait_ge(g_in[r], (i - r) * 8 + 32)
                    weighted(yo[:, r % 2, :], (y1[:, r % 2, :], y2[:, r % 2, :]), w, "fin_half", "fin_made", i)

                def total(i, r):
                    w = wts[:, bass.ds(i, 1), :].rearrange("p a w -> p (a w)")
                    dve.wait_ge(b_in[r], (i - r) * 4 + 16)
                    dve.wait_ge(z_in[r], (i - r) * 8 + 32)
                    weighted(xq[:, r, :], (z1[:, r % 2, :], z2[:, r % 2, :]), w, "half_made", "sum_made", i)

                steps = dict(lh=lhs, hTc=hl if shared else hTc)
                if shared:
                    steps["xl"] = xl
                if shared and off:
                    steps.update(gind=gindex, yc=last_add, tot=total)
                elif shared:
                    steps.update(scat=index, yc=add)
                return steps, count, unroll

            pipelined(dve, [stages(0, NS, 4, True), stages(NS, SLOTS, 2, False), stages(NS + SLOTS, NS, 4, True)], LAG)


INS = dict(x="x", cond_64="cond", mask_BxS_bf1="mask", L0_cond_g_norm="g_norm", L0_cond_Wq="Wq", L0_cond_Wkv="Wkv",
           L0_cond_q_scale="q_scale", L0_cond_k_scale="k_scale", L0_cond_null_attn_bias="null_bias",
           L0_cond_w0="w0", L0_cond_b0="b0", L0_cond_g0="g0", L0_cond_w1="w1", L0_cond_b1="b1", L0_cond_g1="g1",
           L0_cond_w2="w2", L0_cond_b2="b2", L0_cond_Wout="Wout", L0_cond_g_out="g_out",
           L1_cond_wt="wt", L1_cond_wg="wg", L1_cond_w_gate="w_gate", L1_cond_w_up="w_up", L1_cond_w_down="w_down",
           L1_cond_sw_gate="sw_gate", L1_cond_sw_up="sw_up", L1_cond_sw_down="sw_down")


def build(nc, a, out):
    with ExitStack() as ctx:
        def sem(name):
            return ctx.enter_context(nc.semaphore(name))

        sb = {n: sem(n) for n in CREDITS}
        dr = dict(wol=nc.dram_tensor("wout_low_parts", (P, 8 * D), F32, kind="Internal").ap(),
                  bias=nc.dram_tensor("bias_rows", (H, P + S), F32, kind="Internal").ap(),
                  enull=nc.dram_tensor("enull_row", (H,), F32, kind="Internal").ap(),
                  x1=nc.dram_tensor("x1_rows", (T, D), F32, kind="Internal").ap(),
                  base=nc.dram_tensor("base_rows", (T, D), F32, kind="Internal").ap(),
                  xs=nc.dram_tensor("sorted_rows", (SLOTS * P, D), F32, kind="Internal").ap(),
                  ys=nc.dram_tensor("expert_rows", (SLOTS * P, D), F32, kind="Internal").ap())
        sb["LG"] = ctx.enter_context(nc.sbuf_tensor("LG", [P, NTT, NE], F32))
        sb["zero"] = ctx.enter_context(nc.sbuf_tensor("zero", [P, P], F32))
        sb["credit"] = ctx.enter_context(nc.sbuf_tensor("credit", [P, 32], F32))
        with ExitStack() as att:
            def tile(name, shape, dt=F32):
                sb[name] = att.enter_context(nc.sbuf_tensor(name, shape, dt))

            tile("ident", [P, P])
            tile("identr", [P, P], F32R)
            tile("EB", [P, H, S])
            tile("W", [P, KD, WQKV])
            tile("Wo", [P, 8, D], F32R)
            tile("wtT", [P, KD, NE])
            tile("gout", [P, D])
            tile("vnull", [P, VW])
            tile("negc", [P, 1])
            tile("enull", [P, H])
            tile("kfac", [P, DH])
            tile("maskf", [P, NTT])
            tile("glog", [P, B, NE])
            tile("xnT", [P, KD, S])
            tile("xstats", [P, 12 * NT])
            setup(nc, a, sb, dr, sem)
            tile("QT", [P, 2, G, S], F32R)
            tile("KT", [P, 2, S], F32R)
            tile("V", [P, NT, VW])
            tile("AO", [P, NT, H * DH])
            tile("R1", [P, 3584])
            tile("parts", [P, 1024], F32R)

            tile("R2", [P, 3 * NT * VW])
            tile("xt", [P, 2, D])
            tile("small", [P, 361])
            psum = {n: [att.enter_context(nc.psum_tensor(f"ps{n}{i}", [P, 2, 512], F32)) for i in range(2)] for n in "SO"}
            attention(nc, a, sb, dr, sem, psum)
        experts(nc, a, sb, dr, sem, out.rearrange("b s d -> (b s) d"))


def kernel(**inputs):
    import numpy as np
    import concourse.bacc as bacc
    from concourse.bass_utils import run_bass_kernel_spmd

    nc = bacc.Bacc("TRN2", target_bir_lowering=False, num_devices=1)
    arrays, a = {}, {}
    for name, short in INS.items():
        v = np.ascontiguousarray(inputs[name])
        if v.dtype == np.bool_:
            v = v.view(np.uint8)
        arrays[f"in_{name}"] = v
        a[short] = nc.dram_tensor(f"in_{name}", v.shape, mybir.dt.from_np(v.dtype), kind="ExternalInput").ap()
    out = nc.dram_tensor("out_0", (B, S, D), F32, kind="ExternalOutput").ap()
    build(nc, a, out)
    r = run_bass_kernel_spmd(nc, [arrays], core_ids=[0])
    return r.results[0]["out_0"]
```
